# Optimizing a Trainium2 kernel written in Bass

```python
import numpy as np
import jax
import jax.numpy as jnp

def _softmax(x, axis=-1):
    return jax.nn.softmax(x, axis=axis)

def _gelu(x):
    return jax.nn.gelu(x, approximate=True)

def _silu(x):
    return jax.nn.silu(x)

def _sigmoid(x):
    return jax.nn.sigmoid(x)

def _layernorm(x, axis=-1, eps=1e-05):
    m = jnp.mean(x, axis=axis, keepdims=True)
    v = jnp.var(x, axis=axis, keepdims=True)
    return (x - m) / jnp.sqrt(v + eps)

def _scatter_add(tgt, idx, src, axis=0):
    return tgt.at[idx].add(src)

def _segment_sum(src, seg, n):
    return jax.ops.segment_sum(src, seg, n)
kernel_name = 'mk_audio_tower_d4_tok_audfeat512_r4_7ce488'

def setup_inputs(seed: int=0):
    np.random.seed(seed)
    _w = jnp.asarray

    def _rec_inputs():
        import jax
        import jax.numpy as jnp
        _rk = jax.random.key(seed)
        x = -0.0003702 + 0.999946 * jax.random.normal(jax.random.fold_in(_rk, 1), (4, 750, 128), jnp.float32)
        return x
    x = _rec_inputs()

    def _L0_tok_setup():
        import jax, jax.numpy as jnp
        import numpy as np
        CONTEXT_LEN = 3
        SUBSAMPLING = 1
        key = jax.random.key(seed)
        k1, k2, k3 = jax.random.split(key, 3)
        mb, N, D = (32, 250, 128)
        out_features = 128
        inp = jax.random.normal(k1, (mb, N, D), dtype=jnp.float32)
        fan_in = D * CONTEXT_LEN
        weight = jax.random.normal(k2, (out_features, fan_in), dtype=jnp.float32) / np.sqrt(fan_in)
        bias = jax.random.normal(k3, (out_features,), dtype=jnp.float32) * 0.01
        return {'input': inp, 'weight': weight, 'bias': bias}
    _L0_tok_all = _L0_tok_setup()
    _L0_tok_in = {k: v for k, v in _L0_tok_all.items() if k in ('weight', 'bias')}
    del _L0_tok_all

    def _L0_attn_setup():
        import jax, jax.numpy as jnp
        import numpy as np
        DIM = 128
        QK_DIM = DIM // 8
        EXPAND_DIM = DIM * 2
        LN_EPS = 1e-05

        def _layer_norm(x):
            mu = jnp.mean(x, axis=-1, keepdims=True)
            var = jnp.mean(jnp.square(x - mu), axis=-1, keepdims=True)
            return (x - mu) * jax.lax.rsqrt(var + LN_EPS)
        key = jax.random.key(seed)
        k1, k2, k3 = jax.random.split(key, 3)
        B, N = (8, 512)
        x = jax.random.normal(k1, (B, N, DIM), dtype=jnp.float32)
        out_e = 2 * QK_DIM + 2 * EXPAND_DIM
        be = float(np.sqrt(6.0 / (DIM + out_e)))
        expand = jax.random.uniform(k2, (DIM, out_e), minval=-be, maxval=be, dtype=jnp.float32)
        bp = float(np.sqrt(6.0 / (EXPAND_DIM + DIM)))
        project = jax.random.uniform(k3, (EXPAND_DIM, DIM), minval=-bp, maxval=bp, dtype=jnp.float32)
        position_bias_mult = jnp.array(4.0, dtype=jnp.float32)
        return {'x': x, 'expand': expand, 'project': project, 'position_bias_mult': position_bias_mult}
    _L0_attn_all = _L0_attn_setup()
    _L0_attn_in = {k: v for k, v in _L0_attn_all.items() if k in ('expand', 'project', 'position_bias_mult')}
    del _L0_attn_all

    def _L0_ffn_setup():
        import jax, jax.numpy as jnp
        import numpy as np
        B, S, D, F, E = (8, 1024, 128, 512, 8)
        INIT_LAMBDA = 0.2
        LN_EPS = 1e-05
        LN_MERGE = 0.03
        key = jax.random.key(seed)
        ks = jax.random.split(key, 12)
        n = lambda k, shp, s=1.0: jax.random.normal(k, shp, dtype=jnp.float32) * s
        return {'hidden_states': n(ks[0], (B, S, D)), 'gfc1_w': n(ks[1], (D, D), 0.01), 'gfc1_b': jnp.zeros((D,), jnp.float32), 'gfc2_w': n(ks[2], (E, D), 0.01), 'gfc2_b': jnp.full((E,), INIT_LAMBDA, dtype=jnp.float32), 'W1': n(ks[3], (F, D), 0.02), 'b1': jnp.zeros((F,), jnp.float32), 'W2': n(ks[4], (D, F), 0.02), 'b2': jnp.zeros((D,), jnp.float32), 'ln_g': jnp.ones((D,), jnp.float32), 'ln_b': jnp.zeros((D,), jnp.float32), 'tv_W1': n(ks[5], (E, F, D), 0.02), 'tv_b1': n(ks[6], (E, F), 0.02), 'tv_W2': n(ks[7], (E, D, F), 0.02), 'tv_b2': n(ks[8], (E, D), 0.02), 'tv_ln_g': n(ks[9], (E, D), 0.02), 'tv_ln_b': n(ks[10], (E, D), 0.02)}
    _L0_ffn_all = _L0_ffn_setup()
    _L0_ffn_in = {k: v for k, v in _L0_ffn_all.items() if k in ('gfc1_w', 'gfc1_b', 'gfc2_w', 'gfc2_b', 'W1', 'b1', 'W2', 'b2', 'ln_g', 'ln_b', 'tv_W1', 'tv_b1', 'tv_W2', 'tv_b2', 'tv_ln_g', 'tv_ln_b')}
    del _L0_ffn_all

    def _L1_attn_setup():
        import jax, jax.numpy as jnp
        import numpy as np

        def _rope(v):
            B, S, H = v.shape
            inv_freq = 1.0 / 10000.0 ** (jnp.arange(0, H, 2, dtype=jnp.float32) / H)
            t = jnp.arange(S, dtype=jnp.float32)
            freqs = t[:, None] * inv_freq[None, :]
            emb = jnp.concatenate([jnp.sin(freqs), jnp.cos(freqs)], -1)
            x1, x2 = (v[..., ::2], v[..., 1::2])
            emb_sin, emb_cos = (emb[..., ::2], emb[..., 1::2])
            return jnp.concatenate([x1 * emb_cos - x2 * emb_sin, x1 * emb_sin + x2 * emb_cos], -1)
        WINDOW_SIZE = 128
        key = jax.random.key(seed)
        ks = jax.random.split(key, 9)
        B, S, H = (2, 512, 128)
        sc = 0.02
        return {'x': jax.random.normal(ks[0], (B, S, H), dtype=jnp.float32), 'Wq': jax.random.normal(ks[1], (H, H), dtype=jnp.float32) * sc, 'bq': jax.random.normal(ks[2], (H,), dtype=jnp.float32) * sc, 'Wk': jax.random.normal(ks[3], (H, H), dtype=jnp.float32) * sc, 'bk': jax.random.normal(ks[4], (H,), dtype=jnp.float32) * sc, 'Wv': jax.random.normal(ks[5], (H, H), dtype=jnp.float32) * sc, 'bv': jax.random.normal(ks[6], (H,), dtype=jnp.float32) * sc, 'Wo': jax.random.normal(ks[7], (H, H), dtype=jnp.float32) * sc, 'bo': jax.random.normal(ks[8], (H,), dtype=jnp.float32) * sc}
    _L1_attn_all = _L1_attn_setup()
    _L1_attn_in = {k: v for k, v in _L1_attn_all.items() if k in ('Wq', 'bq', 'Wk', 'bk', 'Wv', 'bv', 'Wo', 'bo')}
    del _L1_attn_all

    def _L1_ffn_setup():
        import jax, jax.numpy as jnp
        import numpy as np
        B, S, D, F, E, K, H = (4, 256, 128, 512, 8, 2, 8)
        HEAD_DIM = D // H

        def _layernorm(x, g, b):
            m = x.mean(-1, keepdims=True)
            v = ((x - m) ** 2).mean(-1, keepdims=True)
            return (x - m) * jax.lax.rsqrt(v + 1e-05) * g + b

        def _expert(x, Wqkv, bqkv, Wo, bo, g1, be1, W1, bf1, W2, bf2, g2, be2):
            b, s, d = x.shape
            qkv = x @ Wqkv.T + bqkv
            q, k, v = jnp.split(qkv, 3, axis=-1)
            to_heads = lambda t: t.reshape(b, s, H, HEAD_DIM).transpose(0, 2, 1, 3)
            q, k, v = (to_heads(q), to_heads(k), to_heads(v))
            scale = 1.0 / np.sqrt(HEAD_DIM).astype(np.float32)
            attn = jax.nn.softmax(jnp.einsum('bhqd,bhkd->bhqk', q * scale, k), axis=-1)
            ctx = jnp.einsum('bhqk,bhkd->bhqd', attn, v).transpose(0, 2, 1, 3).reshape(b, s, d)
            ctx = ctx @ Wo.T + bo
            x = _layernorm(x + ctx, g1, be1)
            h = jax.nn.gelu(x @ W1.T + bf1, approximate=False)
            h = jax.nn.gelu(h @ W2.T + bf2, approximate=False)
            return _layernorm(x + h, g2, be2)
        key = jax.random.key(seed)
        ks = jax.random.split(key, 8)
        s = 0.02
        return {'x': jax.random.normal(ks[0], (B, S, D), jnp.float32), 'gate_Wk': jax.random.normal(ks[1], (D, D), jnp.float32) * s, 'gate_bk': jnp.zeros((D,), jnp.float32), 'expert_queries': jax.random.normal(ks[2], (E, D), jnp.float32), 'Wqkv': jax.random.normal(ks[3], (E, 3 * D, D), jnp.float32) * s, 'bqkv': jnp.zeros((E, 3 * D), jnp.float32), 'Wo': jax.random.normal(ks[4], (E, D, D), jnp.float32) * s, 'bo': jnp.zeros((E, D), jnp.float32), 'g1': jnp.ones((E, D), jnp.float32), 'be1': jnp.zeros((E, D), jnp.float32), 'W1': jax.random.normal(ks[5], (E, F, D), jnp.float32) * s, 'bf1': jnp.zeros((E, F), jnp.float32), 'W2': jax.random.normal(ks[6], (E, D, F), jnp.float32) * s, 'bf2': jnp.zeros((E, D), jnp.float32), 'g2': jnp.ones((E, D), jnp.float32), 'be2': jnp.zeros((E, D), jnp.float32)}
    _L1_ffn_all = _L1_ffn_setup()
    _L1_ffn_in = {k: v for k, v in _L1_ffn_all.items() if k in ('gate_Wk', 'gate_bk', 'expert_queries', 'Wqkv', 'bqkv', 'Wo', 'bo', 'g1', 'be1', 'W1', 'bf1', 'W2', 'bf2', 'g2', 'be2')}
    del _L1_ffn_all

    def _L2_attn_setup():
        import jax, jax.numpy as jnp
        import numpy as np
        B, S, E, H = (4, 256, 128, 16)
        key = jax.random.key(seed)
        ks = jax.random.split(key, 6)
        return {'x': jax.random.normal(ks[0], (B, S, E), dtype=jnp.float32), 'Wq': jax.random.normal(ks[1], (E, E), dtype=jnp.float32) * E ** (-0.5), 'Wk': jax.random.normal(ks[2], (E, E), dtype=jnp.float32) * E ** (-0.5), 'Wv': jax.random.normal(ks[3], (E, E), dtype=jnp.float32) * E ** (-0.5), 'W1': jax.random.normal(ks[4], (H, 2 * E), dtype=jnp.float32) * (2 * E) ** (-0.5), 'b1': jnp.zeros((H,), dtype=jnp.float32), 'W2': jax.random.normal(ks[5], (1, H), dtype=jnp.float32) * H ** (-0.5), 'b2': jnp.zeros((1,), dtype=jnp.float32)}
    _L2_attn_all = _L2_attn_setup()
    _L2_attn_in = {k: v for k, v in _L2_attn_all.items() if k in ('Wq', 'Wk', 'Wv', 'W1', 'b1', 'W2', 'b2')}
    del _L2_attn_all

    def _L2_ffn_setup():
        import jax, jax.numpy as jnp
        import numpy as np
        B, S, D = (32, 128, 128)
        E, H, O, K = (8, 512, 128, 2)
        key = jax.random.key(seed)
        ks = jax.random.split(key, 5)
        sc = lambda k, shape, scale: jax.random.normal(k, shape, jnp.float32) * scale
        return {'x': sc(ks[0], (B, S, D), 1.0), 'attn_w': sc(ks[1], (D, 1), 0.05), 'attn_b': jnp.zeros((1,), jnp.float32), 'gate_w': sc(ks[2], (D, E), 0.05), 'gate_b': jnp.zeros((E,), jnp.float32), 'w1': sc(ks[3], (E, D, H), 0.02), 'b1': jnp.zeros((E, H), jnp.float32), 'w2': sc(ks[4], (E, H, O), 0.02), 'b2': jnp.zeros((E, O), jnp.float32)}
    _L2_ffn_all = _L2_ffn_setup()
    _L2_ffn_in = {k: v for k, v in _L2_ffn_all.items() if k in ('attn_w', 'attn_b', 'gate_w', 'gate_b', 'w1', 'b1', 'w2', 'b2')}
    del _L2_ffn_all

    def _L3_attn_setup():
        import jax, jax.numpy as jnp
        import numpy as np
        B, T, K, H = (8, 256, 128, 8)
        key = jax.random.key(seed)
        kx, kq, kk, kv, ko = jax.random.split(key, 5)
        s = 0.02
        return {'x': jax.random.normal(kx, (B, T, K), dtype=jnp.float32), 'Wq': jax.random.normal(kq, (K * H, K), dtype=jnp.float32) * s, 'Wk': jax.random.normal(kk, (K * H, K), dtype=jnp.float32) * s, 'Wv': jax.random.normal(kv, (K * H, K), dtype=jnp.float32) * s, 'Wo': jax.random.normal(ko, (K, K * H), dtype=jnp.float32) * s}
    _L3_attn_all = _L3_attn_setup()
    _L3_attn_in = {k: v for k, v in _L3_attn_all.items() if k in ('Wq', 'Wk', 'Wv', 'Wo')}
    del _L3_attn_all

    def _L3_ffn_setup():
        import jax, jax.numpy as jnp
        import numpy as np
        B, S, H, E, K = (8, 1024, 128, 8, 2)
        key = jax.random.key(seed)
        ks = jax.random.split(key, 7)
        s_h = 1.0 / np.sqrt(H)
        s_2h = 1.0 / np.sqrt(2 * H)
        return {'x': jax.random.normal(ks[0], (B, S, H), dtype=jnp.float32), 'gate_w': jax.random.uniform(ks[1], (H, E), minval=-s_h, maxval=s_h, dtype=jnp.float32), 'gate_b': jax.random.uniform(ks[2], (E,), minval=-s_h, maxval=s_h, dtype=jnp.float32), 'w1': jax.random.uniform(ks[3], (E, H, 2 * H), minval=-s_h, maxval=s_h, dtype=jnp.float32), 'b1': jax.random.uniform(ks[4], (E, 2 * H), minval=-s_h, maxval=s_h, dtype=jnp.float32), 'w2': jax.random.uniform(ks[5], (E, 2 * H, H), minval=-s_2h, maxval=s_2h, dtype=jnp.float32), 'b2': jax.random.uniform(ks[6], (E, H), minval=-s_2h, maxval=s_2h, dtype=jnp.float32)}
    _L3_ffn_all = _L3_ffn_setup()
    _L3_ffn_in = {k: v for k, v in _L3_ffn_all.items() if k in ('gate_w', 'gate_b', 'w1', 'b1', 'w2', 'b2')}
    del _L3_ffn_all
    return {'x': x, 'L0_tok_weight': _L0_tok_in['weight'], 'L0_tok_bias': _L0_tok_in['bias'], 'L0_attn_expand': _L0_attn_in['expand'], 'L0_attn_project': _L0_attn_in['project'], 'L0_attn_position_bias_mult': _L0_attn_in['position_bias_mult'], 'L0_ffn_gfc1_w': _L0_ffn_in['gfc1_w'], 'L0_ffn_gfc1_b': _L0_ffn_in['gfc1_b'], 'L0_ffn_gfc2_w': _L0_ffn_in['gfc2_w'], 'L0_ffn_gfc2_b': _L0_ffn_in['gfc2_b'], 'L0_ffn_W1': _L0_ffn_in['W1'], 'L0_ffn_b1': _L0_ffn_in['b1'], 'L0_ffn_W2': _L0_ffn_in['W2'], 'L0_ffn_b2': _L0_ffn_in['b2'], 'L0_ffn_ln_g': _L0_ffn_in['ln_g'], 'L0_ffn_ln_b': _L0_ffn_in['ln_b'], 'L0_ffn_tv_W1': _L0_ffn_in['tv_W1'], 'L0_ffn_tv_b1': _L0_ffn_in['tv_b1'], 'L0_ffn_tv_W2': _L0_ffn_in['tv_W2'], 'L0_ffn_tv_b2': _L0_ffn_in['tv_b2'], 'L0_ffn_tv_ln_g': _L0_ffn_in['tv_ln_g'], 'L0_ffn_tv_ln_b': _L0_ffn_in['tv_ln_b'], 'L1_attn_Wq': _L1_attn_in['Wq'], 'L1_attn_bq': _L1_attn_in['bq'], 'L1_attn_Wk': _L1_attn_in['Wk'], 'L1_attn_bk': _L1_attn_in['bk'], 'L1_attn_Wv': _L1_attn_in['Wv'], 'L1_attn_bv': _L1_attn_in['bv'], 'L1_attn_Wo': _L1_attn_in['Wo'], 'L1_attn_bo': _L1_attn_in['bo'], 'L1_ffn_gate_Wk': _L1_ffn_in['gate_Wk'], 'L1_ffn_gate_bk': _L1_ffn_in['gate_bk'], 'L1_ffn_expert_queries': _L1_ffn_in['expert_queries'], 'L1_ffn_Wqkv': _L1_ffn_in['Wqkv'], 'L1_ffn_bqkv': _L1_ffn_in['bqkv'], 'L1_ffn_Wo': _L1_ffn_in['Wo'], 'L1_ffn_bo': _L1_ffn_in['bo'], 'L1_ffn_g1': _L1_ffn_in['g1'], 'L1_ffn_be1': _L1_ffn_in['be1'], 'L1_ffn_W1': _L1_ffn_in['W1'], 'L1_ffn_bf1': _L1_ffn_in['bf1'], 'L1_ffn_W2': _L1_ffn_in['W2'], 'L1_ffn_bf2': _L1_ffn_in['bf2'], 'L1_ffn_g2': _L1_ffn_in['g2'], 'L1_ffn_be2': _L1_ffn_in['be2'], 'L2_attn_Wq': _L2_attn_in['Wq'], 'L2_attn_Wk': _L2_attn_in['Wk'], 'L2_attn_Wv': _L2_attn_in['Wv'], 'L2_attn_W1': _L2_attn_in['W1'], 'L2_attn_b1': _L2_attn_in['b1'], 'L2_attn_W2': _L2_attn_in['W2'], 'L2_attn_b2': _L2_attn_in['b2'], 'L2_ffn_attn_w': _L2_ffn_in['attn_w'], 'L2_ffn_attn_b': _L2_ffn_in['attn_b'], 'L2_ffn_gate_w': _L2_ffn_in['gate_w'], 'L2_ffn_gate_b': _L2_ffn_in['gate_b'], 'L2_ffn_w1': _L2_ffn_in['w1'], 'L2_ffn_b1': _L2_ffn_in['b1'], 'L2_ffn_w2': _L2_ffn_in['w2'], 'L2_ffn_b2': _L2_ffn_in['b2'], 'L3_attn_Wq': _L3_attn_in['Wq'], 'L3_attn_Wk': _L3_attn_in['Wk'], 'L3_attn_Wv': _L3_attn_in['Wv'], 'L3_attn_Wo': _L3_attn_in['Wo'], 'L3_ffn_gate_w': _L3_ffn_in['gate_w'], 'L3_ffn_gate_b': _L3_ffn_in['gate_b'], 'L3_ffn_w1': _L3_ffn_in['w1'], 'L3_ffn_b1': _L3_ffn_in['b1'], 'L3_ffn_w2': _L3_ffn_in['w2'], 'L3_ffn_b2': _L3_ffn_in['b2']}

def reference(x, L0_tok_weight, L0_tok_bias, L0_attn_expand, L0_attn_project, L0_attn_position_bias_mult, L0_ffn_gfc1_w, L0_ffn_gfc1_b, L0_ffn_gfc2_w, L0_ffn_gfc2_b, L0_ffn_W1, L0_ffn_b1, L0_ffn_W2, L0_ffn_b2, L0_ffn_ln_g, L0_ffn_ln_b, L0_ffn_tv_W1, L0_ffn_tv_b1, L0_ffn_tv_W2, L0_ffn_tv_b2, L0_ffn_tv_ln_g, L0_ffn_tv_ln_b, L1_attn_Wq, L1_attn_bq, L1_attn_Wk, L1_attn_bk, L1_attn_Wv, L1_attn_bv, L1_attn_Wo, L1_attn_bo, L1_ffn_gate_Wk, L1_ffn_gate_bk, L1_ffn_expert_queries, L1_ffn_Wqkv, L1_ffn_bqkv, L1_ffn_Wo, L1_ffn_bo, L1_ffn_g1, L1_ffn_be1, L1_ffn_W1, L1_ffn_bf1, L1_ffn_W2, L1_ffn_bf2, L1_ffn_g2, L1_ffn_be2, L2_attn_Wq, L2_attn_Wk, L2_attn_Wv, L2_attn_W1, L2_attn_b1, L2_attn_W2, L2_attn_b2, L2_ffn_attn_w, L2_ffn_attn_b, L2_ffn_gate_w, L2_ffn_gate_b, L2_ffn_w1, L2_ffn_b1, L2_ffn_w2, L2_ffn_b2, L3_attn_Wq, L3_attn_Wk, L3_attn_Wv, L3_attn_Wo, L3_ffn_gate_w, L3_ffn_gate_b, L3_ffn_w1, L3_ffn_b1, L3_ffn_w2, L3_ffn_b2):
    import jax
    import jax.numpy as jnp

    def _L0_tok_ref(input, weight, bias):
        import jax, jax.numpy as jnp
        import numpy as np
        CONTEXT_LEN = 3
        SUBSAMPLING = 1
        mb, N, D = input.shape
        l = CONTEXT_LEN
        expected_N = N - l + 1
        padded = jnp.concatenate([jax.lax.dynamic_slice_in_dim(input, i, expected_N, axis=1) for i in range(l)], axis=-1)
        if SUBSAMPLING > 1:
            padded = padded[:, ::SUBSAMPLING, :]
        x = jnp.einsum('btf,of->bto', padded, weight) + bias
        return jax.nn.relu(x)

    def _L0_attn_ref(x, expand, project, position_bias_mult):
        import jax, jax.numpy as jnp
        import numpy as np
        DIM = 128
        QK_DIM = DIM // 8
        EXPAND_DIM = DIM * 2
        LN_EPS = 1e-05

        def _layer_norm(x):
            mu = jnp.mean(x, axis=-1, keepdims=True)
            var = jnp.mean(jnp.square(x - mu), axis=-1, keepdims=True)
            return (x - mu) * jax.lax.rsqrt(var + LN_EPS)
        B, N, _ = x.shape
        nx = _layer_norm(x)
        h = nx @ expand
        q = h[..., :QK_DIM]
        k = h[..., QK_DIM:2 * QK_DIM]
        linear = h[..., 2 * QK_DIM:2 * QK_DIM + EXPAND_DIM]
        pre_gelu = h[..., 2 * QK_DIM + EXPAND_DIM:]
        gated = linear * jax.nn.gelu(pre_gelu, approximate=False)
        local = gated[..., :EXPAND_DIM - DIM]
        v = gated[..., EXPAND_DIM - DIM:]
        pos = jnp.arange(N)
        rel = (pos[None, :] - pos[:, None]).astype(x.dtype)
        causal = pos[None, :] <= pos[:, None]
        mask = jnp.where(causal, jax.nn.sigmoid(rel + position_bias_mult), -jnp.inf)
        logits = jnp.einsum('bqd,bkd->bqk', q, k) / jnp.sqrt(jnp.array(QK_DIM, dtype=x.dtype)) + mask
        scores = jax.nn.softmax(logits, axis=-1)
        attn = jnp.einsum('bqk,bkd->bqd', scores, v)
        return x + jnp.concatenate([local, attn], axis=-1) @ project

    def _L0_ffn_ref(hidden_states, gfc1_w, gfc1_b, gfc2_w, gfc2_b, W1, b1, W2, b2, ln_g, ln_b, tv_W1, tv_b1, tv_W2, tv_b2, tv_ln_g, tv_ln_b):
        import jax, jax.numpy as jnp
        import numpy as np
        B, S, D, F, E = (8, 1024, 128, 512, 8)
        INIT_LAMBDA = 0.2
        LN_EPS = 1e-05
        LN_MERGE = 0.03
        x = hidden_states
        gh = jax.nn.relu(jnp.einsum('bsd,hd->bsh', x, gfc1_w) + gfc1_b)
        g = (jnp.einsum('bsh,eh->bse', gh, gfc2_w) + gfc2_b).mean(axis=1)
        W1m = W1 + jnp.einsum('be,efd->bfd', g, tv_W1)
        b1m = b1 + g @ tv_b1
        W2m = W2 + jnp.einsum('be,edf->bdf', g, tv_W2)
        b2m = b2 + g @ tv_b2
        lng = ln_g + LN_MERGE * (tv_ln_g - ln_g).sum(axis=0)
        lnb = ln_b + LN_MERGE * (tv_ln_b - ln_b).sum(axis=0)
        h = jax.nn.relu(jnp.einsum('bsd,bfd->bsf', x, W1m) + b1m[:, None, :])
        out = jnp.einsum('bsf,bdf->bsd', h, W2m) + b2m[:, None, :]
        res = x + out
        mu = res.mean(axis=-1, keepdims=True)
        var = res.var(axis=-1, keepdims=True)
        return (res - mu) * jax.lax.rsqrt(var + LN_EPS) * lng + lnb

    def _L1_attn_ref(x, Wq, bq, Wk, bk, Wv, bv, Wo, bo):
        import jax, jax.numpy as jnp
        import numpy as np

        def _rope(v):
            B, S, H = v.shape
            inv_freq = 1.0 / 10000.0 ** (jnp.arange(0, H, 2, dtype=jnp.float32) / H)
            t = jnp.arange(S, dtype=jnp.float32)
            freqs = t[:, None] * inv_freq[None, :]
            emb = jnp.concatenate([jnp.sin(freqs), jnp.cos(freqs)], -1)
            x1, x2 = (v[..., ::2], v[..., 1::2])
            emb_sin, emb_cos = (emb[..., ::2], emb[..., 1::2])
            return jnp.concatenate([x1 * emb_cos - x2 * emb_sin, x1 * emb_sin + x2 * emb_cos], -1)
        WINDOW_SIZE = 128
        B, S, H = x.shape
        W = WINDOW_SIZE
        pad = W // 2
        Q = x @ Wq.T + bq
        K = x @ Wk.T + bk
        V = x @ Wv.T + bv
        rQ = _rope(Q)
        rK = _rope(K)
        pK = jnp.pad(rK, ((0, 0), (pad, pad), (0, 0)))
        pV = jnp.pad(V, ((0, 0), (pad, pad), (0, 0)))
        idx = jnp.arange(S)[:, None] + jnp.arange(W)[None, :]
        Kw = pK[:, idx, :]
        Vw = pV[:, idx, :]
        scores = jnp.einsum('bth,btwh->btw', rQ, Kw) / jnp.sqrt(jnp.float32(H))
        weights = jax.nn.softmax(scores, axis=-1)
        out = jnp.einsum('btw,btwh->bth', weights, Vw)
        return out @ Wo.T + bo

    def _L1_ffn_ref(x, gate_Wk, gate_bk, expert_queries, Wqkv, bqkv, Wo, bo, g1, be1, W1, bf1, W2, bf2, g2, be2):
        import jax, jax.numpy as jnp
        import numpy as np
        B, S, D, F, E, K, H = (4, 256, 128, 512, 8, 2, 8)
        HEAD_DIM = D // H

        def _layernorm(x, g, b):
            m = x.mean(-1, keepdims=True)
            v = ((x - m) ** 2).mean(-1, keepdims=True)
            return (x - m) * jax.lax.rsqrt(v + 1e-05) * g + b

        def _expert(x, Wqkv, bqkv, Wo, bo, g1, be1, W1, bf1, W2, bf2, g2, be2):
            b, s, d = x.shape
            qkv = x @ Wqkv.T + bqkv
            q, k, v = jnp.split(qkv, 3, axis=-1)
            to_heads = lambda t: t.reshape(b, s, H, HEAD_DIM).transpose(0, 2, 1, 3)
            q, k, v = (to_heads(q), to_heads(k), to_heads(v))
            scale = 1.0 / np.sqrt(HEAD_DIM).astype(np.float32)
            attn = jax.nn.softmax(jnp.einsum('bhqd,bhkd->bhqk', q * scale, k), axis=-1)
            ctx = jnp.einsum('bhqk,bhkd->bhqd', attn, v).transpose(0, 2, 1, 3).reshape(b, s, d)
            ctx = ctx @ Wo.T + bo
            x = _layernorm(x + ctx, g1, be1)
            h = jax.nn.gelu(x @ W1.T + bf1, approximate=False)
            h = jax.nn.gelu(h @ W2.T + bf2, approximate=False)
            return _layernorm(x + h, g2, be2)
        keys = x @ gate_Wk.T + gate_bk
        scores = jnp.einsum('bsd,ed->bse', keys, expert_queries) * D ** (-0.5)
        probs = jax.nn.softmax(scores, axis=-1)
        _, idx = jax.lax.top_k(probs, K)
        mask = jax.nn.one_hot(idx, E, dtype=probs.dtype).sum(-2)
        gated = probs * mask
        gated = gated / (gated.sum(-1, keepdims=True) + 1e-09)
        eo = jax.vmap(_expert, in_axes=(None,) + (0,) * 12)(x, Wqkv, bqkv, Wo, bo, g1, be1, W1, bf1, W2, bf2, g2, be2)
        return jnp.einsum('ebsd,bse->bsd', eo, gated)

    def _L2_attn_ref(x, Wq, Wk, Wv, W1, b1, W2, b2):
        import jax, jax.numpy as jnp
        import numpy as np
        B, S, E, H = (4, 256, 128, 16)
        embed_dim = x.shape[-1]
        Q = jnp.einsum('bse,oe->bso', x, Wq)
        K = jnp.einsum('bse,oe->bso', x, Wk)
        V = jnp.einsum('bse,oe->bso', x, Wv)
        scores = jnp.einsum('bqe,bke->bqk', Q, K) / jnp.sqrt(jnp.float32(embed_dim))
        W1q, W1k = (W1[:, :embed_dim], W1[:, embed_dim:])
        hq = jnp.einsum('bqe,he->bqh', Q, W1q)
        hk = jnp.einsum('bke,he->bkh', K, W1k)
        hid = jnp.tanh(hq[:, :, None, :] + hk[:, None, :, :] + b1)
        est = jnp.einsum('bqkh,h->bqk', hid, W2[0]) + b2[0]
        attn = jax.nn.softmax(scores + est, axis=-1)
        return jnp.einsum('bqk,bke->bqe', attn, V)

    def _L2_ffn_ref(x, attn_w, attn_b, gate_w, gate_b, w1, b1, w2, b2):
        import jax, jax.numpy as jnp
        import numpy as np
        B, S, D = (32, 128, 128)
        E, H, O, K = (8, 512, 128, 2)
        scores = x @ attn_w + attn_b
        aw = jax.nn.softmax(scores, axis=1)
        pooled = jnp.sum(x * aw, axis=1)
        gates = jax.nn.softmax(pooled @ gate_w + gate_b, axis=-1)
        _, idx = jax.lax.top_k(gates, K)
        mask = jnp.sum(jax.nn.one_hot(idx, E, dtype=gates.dtype), axis=-2)
        g = gates * mask
        g = g / (jnp.sum(g, axis=-1, keepdims=True) + 1e-09)
        h = jax.nn.gelu(jnp.einsum('bsd,edh->ebsh', x, w1) + b1[:, None, None, :], approximate=False)
        eo = jax.nn.gelu(jnp.einsum('ebsh,eho->ebso', h, w2) + b2[:, None, None, :], approximate=False)
        return jnp.einsum('ebso,be->bso', eo, g)

    def _L3_attn_ref(x, Wq, Wk, Wv, Wo):
        import jax, jax.numpy as jnp
        import numpy as np
        B, T, K, H = (8, 256, 128, 8)
        b, t, k = x.shape
        h = H
        scale = k ** 0.25

        def proj(W):
            return (x @ W.T).reshape(b, t, h, k).transpose(0, 2, 1, 3)
        q = proj(Wq) / scale
        kk_ = proj(Wk) / scale
        v = proj(Wv)
        dot = jnp.einsum('bhtd,bhsd->bhts', q, kk_)
        causal = jnp.tril(jnp.ones((t, t), dtype=bool))
        dot = jnp.where(causal[None, None], dot, -jnp.inf)
        attn = jax.nn.softmax(dot, axis=-1)
        out = jnp.einsum('bhts,bhsd->bhtd', attn, v)
        out = out.transpose(0, 2, 1, 3).reshape(b, t, h * k)
        return out @ Wo.T

    def _L3_ffn_ref(x, gate_w, gate_b, w1, b1, w2, b2):
        import jax, jax.numpy as jnp
        import numpy as np
        B, S, H, E, K = (8, 1024, 128, 8, 2)
        logits = jnp.einsum('bsh,he->bse', x, gate_w) + gate_b
        topk_vals, topk_idx = jax.lax.top_k(logits, K)
        topk_weights = jax.nn.softmax(topk_vals, axis=-1)
        mask = jax.nn.one_hot(topk_idx, E, dtype=topk_weights.dtype)
        weights = jnp.einsum('bske,bsk->bse', mask, topk_weights)
        h = jax.nn.relu(jnp.einsum('bsh,ehf->bsef', x, w1) + b1)
        expert_out = jnp.einsum('bsef,efh->bseh', h, w2) + b2
        return jnp.einsum('bseh,bse->bsh', expert_out, weights)
    h = _L0_tok_ref(x, L0_tok_weight, L0_tok_bias)
    h = h + _L0_attn_ref(_layernorm(h, axis=-1), L0_attn_expand, L0_attn_project, L0_attn_position_bias_mult)
    h = h + _L0_ffn_ref(_layernorm(h, axis=-1), L0_ffn_gfc1_w, L0_ffn_gfc1_b, L0_ffn_gfc2_w, L0_ffn_gfc2_b, L0_ffn_W1, L0_ffn_b1, L0_ffn_W2, L0_ffn_b2, L0_ffn_ln_g, L0_ffn_ln_b, L0_ffn_tv_W1, L0_ffn_tv_b1, L0_ffn_tv_W2, L0_ffn_tv_b2, L0_ffn_tv_ln_g, L0_ffn_tv_ln_b)
    h = h + _L1_attn_ref(_layernorm(h, axis=-1), L1_attn_Wq, L1_attn_bq, L1_attn_Wk, L1_attn_bk, L1_attn_Wv, L1_attn_bv, L1_attn_Wo, L1_attn_bo)
    h = h + _L1_ffn_ref(_layernorm(h, axis=-1), L1_ffn_gate_Wk, L1_ffn_gate_bk, L1_ffn_expert_queries, L1_ffn_Wqkv, L1_ffn_bqkv, L1_ffn_Wo, L1_ffn_bo, L1_ffn_g1, L1_ffn_be1, L1_ffn_W1, L1_ffn_bf1, L1_ffn_W2, L1_ffn_bf2, L1_ffn_g2, L1_ffn_be2)
    h = h + _L2_attn_ref(_layernorm(h, axis=-1), L2_attn_Wq, L2_attn_Wk, L2_attn_Wv, L2_attn_W1, L2_attn_b1, L2_attn_W2, L2_attn_b2)
    h = h + _L2_ffn_ref(_layernorm(h, axis=-1), L2_ffn_attn_w, L2_ffn_attn_b, L2_ffn_gate_w, L2_ffn_gate_b, L2_ffn_w1, L2_ffn_b1, L2_ffn_w2, L2_ffn_b2)
    h = h + _L3_attn_ref(_layernorm(h, axis=-1), L3_attn_Wq, L3_attn_Wk, L3_attn_Wv, L3_attn_Wo)
    h = h + _L3_ffn_ref(_layernorm(h, axis=-1), L3_ffn_gate_w, L3_ffn_gate_b, L3_ffn_w1, L3_ffn_b1, L3_ffn_w2, L3_ffn_b2)
    return h

_drawn_inputs = setup_inputs


def setup_inputs(seed=0):
    import zlib

    import numpy as np

    out = dict(_drawn_inputs(seed))
    spreads = {'L0_ffn_gfc1_b': (0.0, 0.8),
     'L0_ffn_gfc2_b': (0.20000000298023224, 0.6),
     'L0_ffn_b1': (0.0, 0.513),
     'L0_ffn_b2': (0.0, 0.1),
     'L0_ffn_ln_g': (1.0, 0.2),
     'L0_ffn_ln_b': (0.0, 0.1),
     'L1_ffn_gate_bk': (0.0, 0.1),
     'L1_ffn_bqkv': (0.0, 0.8),
     'L1_ffn_bo': (0.0, 0.363),
     'L1_ffn_g1': (1.0, 0.2),
     'L1_ffn_be1': (0.0, 0.353),
     'L1_ffn_bf1': (0.0, 0.8),
     'L1_ffn_bf2': (0.0, 0.712),
     'L1_ffn_g2': (1.0, 0.2),
     'L1_ffn_be2': (0.0, 0.365),
     'L2_attn_b1': (0.0, 0.8),
     'L2_ffn_gate_b': (0.0, 0.568),
     'L2_ffn_b1': (0.0, 0.8),
     'L2_ffn_b2': (0.0, 0.613)}
    factors = {'L0_tok_bias': 4.094,
     'L0_ffn_gfc1_w': 8.0,
     'L0_ffn_gfc2_w': 8.0,
     'L0_ffn_tv_W1': 3.796,
     'L0_ffn_tv_b1': 8.0,
     'L0_ffn_tv_W2': 3.38,
     'L0_ffn_tv_b2': 8.0,
     'L0_ffn_tv_ln_g': 8.0,
     'L0_ffn_tv_ln_b': 8.0,
     'L1_attn_Wq': 8.0,
     'L1_attn_bq': 8.0,
     'L1_attn_Wk': 8.0,
     'L1_attn_bk': 8.0,
     'L1_attn_Wv': 8.0,
     'L1_attn_bv': 8.0,
     'L1_attn_Wo': 8.0,
     'L1_attn_bo': 5.795,
     'L1_ffn_Wqkv': 8.0,
     'L1_ffn_Wo': 8.0,
     'L1_ffn_W1': 8.0,
     'L1_ffn_W2': 8.0,
     'L2_attn_W1': 3.618,
     'L2_attn_W2': 3.959,
     'L2_ffn_attn_w': 6.885,
     'L2_ffn_gate_w': 6.875,
     'L2_ffn_w1': 8.0,
     'L2_ffn_w2': 8.0,
     'L3_attn_Wq': 8.0,
     'L3_attn_Wk': 8.0,
     'L3_attn_Wv': 8.0,
     'L3_attn_Wo': 8.0,
     'L3_ffn_gate_b': 20.328,
     'L3_ffn_b1': 31.373,
     'L3_ffn_b2': 7.342,
     'L3_ffn_w1': 2.82}
    for name, (base, spread) in spreads.items():
        noise = np.random.default_rng([zlib.crc32(name.encode()), seed]).standard_normal(out[name].shape)
        drawn = base * np.exp(spread * noise) if base else spread * noise
        out[name] = jnp.asarray(drawn.astype(out[name].dtype))
    for name, factor in factors.items():
        out[name] = (out[name] * factor).astype(out[name].dtype)
    return out
```

```python
from contextlib import ExitStack, contextmanager

import concourse.bass as bass
from concourse import mybir

F32 = mybir.dt.float32
I32 = mybir.dt.int32
ALU = mybir.AluOpType
ACT = mybir.ActivationFunctionType
X = mybir.AxisListType.X
XY = mybir.AxisListType.XY

B, T_IN, D = 4, 750, 128
CONTEXT = 3
T = T_IN - CONTEXT + 1
P = 128
NT = (T + P - 1) // P
TP = NT * P
H0 = 3 * P
HALVES = ((0, H0), (H0, T))
E = 8
QK0 = 16
HD = D // E
F = 512
FT = F // P
F3 = 256
WINDOW = 128
PAD = WINDOW // 2
TPAD = TP + 2 * PAD
EPS = 1e-5
MERGE = 0.03
FAR = -1.0e30

W1_Q, W1_K, W1_V, W1_O, W1_UP, W1_DOWN = 0, 256, 512, 640, 768, 1280
W1_BIAS = 1792
W1_END = W1_BIAS + 8
R_BV, R_BO, R_BF2, R_G1, R_BE1, R_G2, R_BE2 = range(7)
W2_UP, W2_DOWN, W2_BIAS, W2_END = 0, 512, 1024, 1028
W3_Q, W3_K, W3_V, W3_O, W3_END = 0, 128, 256, 384, 512
W4_UP, W4_DOWN, W4_BIAS, W4_END = 0, 256, 512, 514

CONST = [
    ("ident", P), ("ones", P), ("onehot8", 8), ("rank8", 8),
    ("tok_w", 3 * P), ("expand_q", QK0), ("expand_k", QK0), ("expand_lin", P), ("expand_pre", P),
    ("expand_v", 2 * P), ("project", 2 * P), ("rel", TP), ("causal", TP), ("valid", TPAD),
    ("gfc1", P), ("gfc1_b", 1), ("gfc2", 8), ("w1w2", 2 * F), ("b1", FT), ("tv_b1", E * FT),
    ("rope_qa", P), ("rope_qb", P), ("rope_ka", P), ("rope_kb", P), ("rope_bias", 4),
    ("rope_cos", T), ("rope_sin", T), ("v1", P), ("o1", P), ("band", 2 * P),
    ("gate_k", P), ("gate_kb", 1), ("queries", 8),
    ("q2", P), ("k2", P), ("v2", P), ("hq2", P), ("hk2", P), ("b1_2", 1), ("w2_2", 1),
    ("pool_w", 1), ("gate_w2", 8), ("gate_w3", 8),
]
ROWS = [
    ("tok_b", P), ("mult", 1), ("gfc2_b", 8), ("b2", P), ("tv_b2", E * P), ("ln_g", P), ("tv_ln_g", E * P),
    ("ln_b", P), ("tv_ln_b", E * P), ("bv1", P), ("bo1", P), ("b2_2", 1), ("pool_b", 1), ("gate_b2", 8), ("gate_b3", 8),
]


def offsets(parts):
    at, out = 0, {}
    for name, width in parts:
        out[name] = (at, width)
        at += width
    return out, at


CONST_AT, CONST_END = offsets(CONST)
ROWS_AT, ROWS_END = offsets(ROWS)

SEMAPHORES = [
    "loop_entered", "consts_loaded", "decay_ready", "setup_done", "x_loaded", "x_free", "h_free", "h_stored", "wts_free", "wts_loaded0", "wts_loaded1",
    "operand_ready",
    "feat_ready", "feat_done",
    "tok_ready", "tok_done_v", "tok_done_a",
    "turned0", "turned1", "copied0", "copied1",
    "var_ready", "rstd_ready",
    "scores_ready", "max_ready", "probs_ready", "heads_ready",
    "hidden_ready", "hidden_used",
    "query_part_ready",
    "logits_ready", "exps_ready",
]


class Tally:

    def __init__(self, engine, per_turn):
        self.engine, self.per_turn, self.n, self.loops = engine, per_turn, {}, []

    def now(self, name):
        value = self.n.get(name, 0)
        for register, loop in self.loops:
            per = self.per_turn.get((self.engine, loop, name), 0)
            if per:
                value = register * per + value
        return value

    def take(self, name, count=1):
        self.n[name] = self.n.get(name, 0) + count
        return self.now(name)

    @contextmanager
    def loop(self, eng, name, turns, entered):
        before = dict(self.n)
        eng.sem_inc(entered, 1)
        with eng.Fori(0, turns) as i:
            self.loops.append((i, name))
            yield i
            self.loops.pop()
        for key, n in list(self.n.items()):
            per = n - before.get(key, 0)
            self.per_turn[(self.engine, name, key)] = per
            self.n[key] = before.get(key, 0) + turns * per


def key_tiles(n):
    return list(range((n + P - 1) // P))


class Attention:

    def __init__(self, units, keys, scale, mask=None, additive=False):
        self.units, self.keys, self.scale, self.mask, self.additive = units, keys, scale, mask, additive


def causal_keys(tile):
    return min((tile + 1) * P, T)


LAYER0 = Attention(NT, lambda u: causal_keys(u % NT), 0.25, "rel")
LAYER1 = Attention(NT, lambda u: 2 * P, float(D) ** -0.5, "band")
EXPERT = Attention(E * NT, lambda u: T, float(HD) ** -0.5)
LAYER2 = Attention(NT, lambda u: T, 1.0, additive=True)
LAYER3 = Attention(NT, lambda u: causal_keys(u % NT), float(D) ** -0.5, "causal")


def cut(ap, n):
    return ap if n <= 512 else ap.rearrange("p (a n) -> p a n", a=2)


def audio_tower(nc, A, per_turn):
    with ExitStack() as ctx:
        def sb(name, shape, dt=F32):
            return ctx.enter_context(nc.sbuf_tensor(name, shape, dt))

        S = {name: ctx.enter_context(nc.semaphore(name)) for name in SEMAPHORES}
        ps = ctx.enter_context(nc.psum_tensor("ps", [P, 8, 512], F32))

        const = sb("const", [P, CONST_END])
        rows = sb("rows", [P, ROWS_END])
        tv = sb("tv", [P, E, 2 * F])
        wts = sb("wts", [P, 2, W1_END])
        wrow = sb("wrow", [P, 2, 7 * P])
        xT = sb("xT", [P, TP + CONTEXT - 1])
        h = sb("h", [P, NT, D])
        xn = sb("xn", [P, NT, D])
        x1 = sb("x1", [P, NT, D])
        y = sb("y", [P, NT, D])
        att = sb("att", [P, NT, D])
        xnT = sb("xnT", [P, TPAD])
        attT = sb("attT", [P, TP])
        QT = sb("QT", [P, 2, TP])
        KT = sb("KT", [P, 2, TP])
        keyT = sb("keyT", [P, TPAD])
        V = sb("V", [P, NT + 1, D])
        hid = sb("hid", [P, FT, TP])
        masked = sb("masked", [P, 2, TP])
        probs = sb("probs", [P, 2, TP])
        probsT = sb("probsT", [P, 6, P])
        merged = sb("merged", [P, 2 * F])
        merged_b1 = sb("merged_b1", [P, FT])
        merged_b2 = sb("merged_b2", [P, P])
        stats = sb("stats", [P, NT, 6])
        mv = sb("mv", [P, NT, 2])
        var = sb("var", [P, NT])
        rstd = sb("rstd", [P, NT])
        minus_half = sb("minus_half", [P, NT])
        top = sb("top", [P, 2])
        neg_top = sb("neg_top", [P, 2])
        total = sb("total", [P, 4])
        rtotal = sb("rtotal", [P, 2])
        half_sum = sb("half_sum", [P, 2])
        pooled = sb("pooled", [P, 4])
        spread = sb("spread", [P, P])
        g8 = sb("g8", [P, 8])
        add_w = sb("add_w", [P, 2 * P])
        hqb = sb("hqb", [P, TP // 8])
        lng = sb("lng", [P, P])
        lnb = sb("lnb", [P, P])
        pool_w = sb("pool_w", [P, P])
        lg = sb("lg", [P, NT, 8])
        lg2 = sb("lg2", [P, NT, 8])
        ex = sb("ex", [P, NT, 8])
        pick = sb("pick", [P, NT, 8])
        cand = sb("cand", [P, NT, 8])
        m1 = sb("m1", [P, NT])
        gates = sb("gates", [P, 8, NT])
        gcol = sb("gcol", [P, NT])

        def C(name):
            at, width = CONST_AT[name]
            return const[:, at:at + width]

        def R(name):
            at, width = ROWS_AT[name]
            return rows[:, at:at + width]

        ident, ones = C("ident"), C("ones")
        xT_ = xnT[:, PAD:PAD + TP]
        onerow = const[0:1, CONST_AT["ones"][0]:CONST_AT["ones"][0] + P]

        def row(ap):
            return ap[0:1]

        def tile_of(ap, t):
            return ap[:, t * P:(t + 1) * P]

        def flat(ap):
            return ap[:, :, :].rearrange("p t d -> p (t d)")

        def wrow_of(k, r):
            return wrow[:, k, r * P:(r + 1) * P]

        def scores_ap(u, n):
            return ps[:, 2 * (u % 2), 0:n] if n <= 512 else ps[:, 2 * (u % 2):2 * (u % 2) + 2, 0:n // 2]

        def tanh_ring(g):
            return hid[:, g % 4, :] if g % 4 < 2 else masked[:, g % 4 - 2, :]

        def mask_ap(spec, u):
            n = spec.keys(u)
            if spec.mask == "band":
                return C("band")
            at = CONST_AT[spec.mask][0] + (NT - 1 - u % NT) * P
            return cut(const[:, at:at + n], n)

        block = ctx.enter_context(nc.Block())

        @block.sync
        def _(sp):
            n = Tally("sync", per_turn)
            sp.dma_start(const[:, :], A["const"]).then_inc(S["consts_loaded"], 16)
            sp.dma_start(rows[:, :], A["rows"].broadcast_to([P, ROWS_END])).then_inc(S["consts_loaded"], 16)
            sp.dma_start(tv[:, :, :], A["tv"]).then_inc(S["consts_loaded"], 16)
            sp.sem_inc(S["h_free"], 1)

            def load(src, srow, at, k):
                sp.wait_ge(S["wts_free"], n.take("wts_free"))
                sp.dma_start(wts[:, k, 0:src.shape[2]], src[at, :, :]).then_inc(S[f"wts_loaded{k}"], 16)
                if srow is not None:
                    sp.dma_start(wrow[:, k, 0:srow.shape[1]], srow[at, :].partition_broadcast(P))\
                        .then_inc(S[f"wts_loaded{k}"], 16)

            with n.loop(sp, "batch", B, S["loop_entered"]) as b:
                sp.wait_ge(S["x_free"], n.take("x_free"))
                sp.dma_start(xT[:, 0:T_IN], A["xT"][b, :, :]).then_inc(S["x_loaded"], 16)
                for stage, src, srow in (("l1", A["l1"], A["l1_rows"]), ("l2", A["l2"], A["l2_rows"]),
                                         ("l3", A["l3"], None), ("l4", A["l4"], A["l4_rows"])):
                    with n.loop(sp, stage, E // 2, S["loop_entered"]) as pair:
                        for k in range(2):
                            load(src, srow, pair * 2 + k, k)
                sp.wait_ge(S["wts_free"], n.now("wts_free") + 2)
                full = (NT - 1) * P
                sp.dma_start(A["out"][b, 0:full, :].rearrange("(t p) d -> p t d", p=P), h[:, 0:NT - 1, :])\
                    .then_inc(S["h_stored"], 16)
                sp.dma_start(A["out"][b, full:T, :], h[0:T - full, NT - 1, :]).then_inc(S["h_stored"], 16)
                sp.wait_ge(S["h_stored"], n.take("h_stored", 32))
                sp.sem_inc(S["h_free"], 1)

        @block.gpsimd
        def _(pool):
            n = Tally("pool", per_turn)
            pool.memset(minus_half[:, :], -0.5)
            pool.drain()

            def power(times):
                for _ in range(times):
                    pool.wait_ge(S["var_ready"], n.take("var_ready"))
                    pool.tensor_tensor(rstd[:, :], var[:, :], minus_half[:, :], ALU.pow).then_inc(S["rstd_ready"], 1)

            with n.loop(pool, "batch", B, S["loop_entered"]):
                power(6)
                with n.loop(pool, "l1", E // 2, S["loop_entered"]):
                    power(4)
                power(4)

        @block.tensor
        def _(pe):
            n = Tally("tensor", per_turn)

            def turn(src):
                pe.wait_ge(S["operand_ready"], n.take("operand_ready"))
                for half in range(2):
                    for t in range(3):
                        mm = pe.transpose(ps[:, 4 + half, t * P:(t + 1) * P], src[:, 3 * half + t, :], ident)
                    mm.then_inc(S[f"turned{half}"], 1)
                for half in range(2):
                    pe.wait_ge(S[f"copied{half}"], n.take(f"copied{half}"))

            def feat(blocks, rhs):
                base = n.now("feat_done")
                i = 0
                for w in blocks:
                    m = w.shape[1]
                    for lo, hi in HALVES:
                        if i >= 4:
                            pe.wait_ge(S["feat_done"], base + (i - 3))
                        pe.matmul(ps[0:m, i % 4, 0:hi - lo], w, rhs[:, lo:hi], start=True, stop=True)\
                            .then_inc(S["feat_ready"], 1)
                        i += 1
                pe.wait_ge(S["feat_done"], n.take("feat_done", i))

            def tok(tiles, products, done, width=D):
                base = n.now(done)
                for t in range(tiles):
                    if t >= 4:
                        pe.wait_ge(S[done], base + (t - 3))
                    terms = products(t)
                    for i, (lhs, rhs) in enumerate(terms):
                        mm = pe.matmul(ps[:, 4 + t % 4, 0:width], lhs, rhs, start=(i == 0), stop=(i == len(terms) - 1))
                    mm.then_inc(S["tok_ready"], 1)
                pe.wait_ge(S[done], n.take(done, tiles))

            def attention(spec, query, key, value, dv):
                def scores(u):
                    keys = spec.keys(u)
                    width = keys if keys <= 512 else keys // 2
                    parts = range(keys // width)
                    for a in parts:
                        mm = pe.matmul(ps[:, 2 * (u % 2) + a, 0:width], query(u), key(u)[:, a * width:(a + 1) * width],
                                       start=True, stop=not spec.additive)
                    for g in range(P // 8 if spec.additive else 0):
                        pe.wait_ge(S["hidden_ready"], n.take("hidden_ready"))
                        for a in parts:
                            last = pe.matmul(ps[:, 2 * (u % 2) + a, 0:width], add_w[:, P - 8 * g:2 * P - 8 * g],
                                             tanh_ring(g)[:, a * width:(a + 1) * width], start=False,
                                             stop=(g == P // 8 - 1))
                        last.then_inc(S["hidden_used"], 1)
                    if spec.additive:
                        pe.drain().then_inc(S["scores_ready"], 1)
                    else:
                        mm.then_inc(S["scores_ready"], 1)

                def spread_out(u):
                    pe.wait_ge(S["probs_ready"], n.take("probs_ready"))
                    tiles = key_tiles(spec.keys(u))
                    for half in range(2):
                        for j in tiles[3 * half:3 * half + 3]:
                            mm = pe.transpose(ps[:, 4 + half, (j % 3) * P:(j % 3 + 1) * P],
                                              probs[:, u % 2, j * P:(j + 1) * P], ident)
                        if tiles[3 * half:]:
                            mm.then_inc(S[f"turned{half}"], 1)

                def weigh(u):
                    tiles = key_tiles(spec.keys(u))
                    for j in tiles:
                        if j % 3 == 0:
                            pe.wait_ge(S[f"copied{j // 3}"], n.take(f"copied{j // 3}"))
                        mm = pe.matmul(ps[:, 6 + u % 2, 0:dv], probsT[:, j, :], value(u, j),
                                       start=(j == 0), stop=(j == len(tiles) - 1))
                    mm.then_inc(S["heads_ready"], 1)

                scores(0)
                scores(1)
                for u in range(spec.units):
                    spread_out(u)
                    if u + 2 < spec.units:
                        scores(u + 2)
                    weigh(u)

            pe.wait_ge(S["setup_done"], 1)
            with n.loop(pe, "batch", B, S["loop_entered"]):
                pe.wait_ge(S["x_loaded"], n.take("x_loaded", 16))
                tw = C("tok_w")
                tok(NT, lambda t: [(onerow, row(R("tok_b")))] +
                    [(xT[:, t * P + i:(t + 1) * P + i], tw[:, i * P:(i + 1) * P]) for i in range(CONTEXT)], "tok_done_v")

                turn(xn)
                feat([C("expand_q"), C("expand_k"), C("expand_lin"), C("expand_pre")], xT_)
                tok(NT, lambda t: [(tile_of(xT_, t), C("expand_v"))], "tok_done_a", 2 * P)
                pe.wait_ge(S["operand_ready"], n.take("operand_ready"))
                attention(LAYER0, lambda u: QT[0:QK0, 0, u * P:(u + 1) * P], lambda u: KT[0:QK0, 0, :],
                          lambda u, j: V[:, j, :], D)
                turn(att)
                pj = C("project")
                tok(NT, lambda t: [(tile_of(hid[:, 2, :], t), pj[:, 0:P]), (tile_of(attT, t), pj[:, P:2 * P])],
                    "tok_done_v")

                turn(xn)
                feat([C("gfc1")], xT_)
                pe.wait_ge(S["operand_ready"], n.take("operand_ready"))
                pe.matmul(ps[:, 4, 0:8], spread[:, :], C("gfc2"), start=True, stop=True).then_inc(S["tok_ready"], 1)
                pe.wait_ge(S["operand_ready"], n.take("operand_ready"))
                feat([merged[:, f * P:(f + 1) * P] for f in range(FT)], xT_)
                tok(NT, lambda t: [(tile_of(hid[:, f, :], t), merged[:, F + f * P:F + (f + 1) * P]) for f in range(FT)],
                    "tok_done_v")

                turn(xn)
                feat([C("rope_qa"), C("rope_qb"), C("rope_ka"), C("rope_kb")], xT_)
                vrow = row(C("valid"))
                tok(NT + 1, lambda t: [(vrow[:, t * P:(t + 1) * P], row(R("bv1"))), (tile_of(xnT, t), C("v1"))],
                    "tok_done_v")
                pe.wait_ge(S["operand_ready"], n.take("operand_ready"))
                attention(LAYER1, lambda u: tile_of(QT[:, 0, :], u), lambda u: keyT[:, u * P:(u + 2) * P],
                          lambda u, j: V[:, u + j, :], D)
                turn(att)
                tok(NT, lambda t: [(onerow, row(R("bo1"))), (tile_of(attT, t), C("o1"))], "tok_done_v")

                turn(xn)
                feat([C("gate_k")], xT_)
                tok(NT, lambda t: [(tile_of(hid[:, 0, :], t), C("queries"))], "tok_done_v", 8)
                with n.loop(pe, "l1", E // 2, S["loop_entered"]):
                    for k in range(2):
                        w = wts[:, k, :]
                        pe.wait_ge(S[f"wts_loaded{k}"], n.take(f"wts_loaded{k}", 32))
                        feat([w[:, W1_Q + i * P:W1_Q + (i + 1) * P] for i in range(4)], xT_)
                        tok(NT, lambda t: [(onerow, row(wrow_of(k, R_BV))), (tile_of(xT_, t), w[:, W1_V:W1_V + P])],
                            "tok_done_v")

                        def head(ap, u):
                            q = 32 * ((u // NT) % 4)
                            return ap[q:q + HD, (u // NT) // 4, :]
                        attention(EXPERT, lambda u: tile_of(head(QT, u), u % NT), lambda u: head(KT, u),
                                  lambda u, j: V[:, j, (u // NT) * HD:(u // NT + 1) * HD], HD)
                        turn(att)
                        tok(NT, lambda t: [(onerow, row(wrow_of(k, R_BO))), (tile_of(attT, t), w[:, W1_O:W1_O + P])],
                            "tok_done_v")
                        turn(x1)
                        feat([w[:, W1_UP + f * P:W1_UP + (f + 1) * P] for f in range(FT)], attT)
                        tok(NT, lambda t: [(onerow, row(wrow_of(k, R_BF2)))] +
                            [(tile_of(hid[:, f, :], t), w[:, W1_DOWN + f * P:W1_DOWN + (f + 1) * P]) for f in range(FT)],
                            "tok_done_a")

                turn(xn)
                feat([C("q2"), C("k2")], xT_)
                tok(NT, lambda t: [(tile_of(xT_, t), C("v2"))], "tok_done_v")
                feat([C("hq2")], QT[:, 0, :])
                feat([C("hk2")], KT[:, 0, :])
                pe.wait_ge(S["operand_ready"], n.take("operand_ready"))
                attention(LAYER2, lambda u: tile_of(QT[:, 1, :], u), lambda u: KT[:, 0, :],
                          lambda u, j: V[:, j, :], D)

                turn(xn)
                feat([pool_w[:, :]], xT_)
                pe.wait_ge(S["operand_ready"], n.take("operand_ready"))
                pe.matmul(ps[:, 4, 0:8], spread[:, :], C("gate_w2"), start=True, stop=True).then_inc(S["tok_ready"], 1)
                pe.wait_ge(S["tok_done_v"], n.take("tok_done_v"))
                with n.loop(pe, "l2", E // 2, S["loop_entered"]):
                    for k in range(2):
                        w = wts[:, k, :]
                        pe.wait_ge(S[f"wts_loaded{k}"], n.take(f"wts_loaded{k}", 32))
                        feat([w[:, W2_UP + f * P:W2_UP + (f + 1) * P] for f in range(FT)], xT_)
                        tok(NT, lambda t: [(onerow, row(wrow_of(k, 0)))] +
                            [(tile_of(hid[:, f, :], t), w[:, W2_DOWN + f * P:W2_DOWN + (f + 1) * P]) for f in range(FT)],
                            "tok_done_a")

                turn(xn)
                with n.loop(pe, "l3", E // 2, S["loop_entered"]):
                    for k in range(2):
                        w = wts[:, k, :]
                        pe.wait_ge(S[f"wts_loaded{k}"], n.take(f"wts_loaded{k}", 16))
                        feat([w[:, W3_Q:W3_Q + P], w[:, W3_K:W3_K + P]], xT_)
                        tok(NT, lambda t: [(tile_of(xT_, t), w[:, W3_V:W3_V + P])], "tok_done_v")
                        attention(LAYER3, lambda u: tile_of(QT[:, 0, :], u), lambda u: KT[:, 0, :],
                                  lambda u, j: V[:, j, :], D)
                        turn(att)
                        tok(NT, lambda t: [(tile_of(attT, t), w[:, W3_O:W3_O + P])], "tok_done_v")

                turn(xn)
                tok(NT, lambda t: [(onerow, row(R("gate_b3"))), (tile_of(xT_, t), C("gate_w3"))], "tok_done_v", 8)
                with n.loop(pe, "l4", E // 2, S["loop_entered"]):
                    for k in range(2):
                        w = wts[:, k, :]
                        pe.wait_ge(S[f"wts_loaded{k}"], n.take(f"wts_loaded{k}", 32))
                        feat([w[:, W4_UP + f * P:W4_UP + (f + 1) * P] for f in range(F3 // P)], xT_)
                        tok(NT, lambda t: [(onerow, row(wrow_of(k, 0)))] +
                            [(tile_of(hid[:, f, :], t), w[:, W4_DOWN + f * P:W4_DOWN + (f + 1) * P])
                             for f in range(F3 // P)], "tok_done_v")

        @block.scalar
        def _(act):
            n = Tally("scalar", per_turn)

            def turned(dst):
                act.wait_ge(S["turned1"], n.take("turned1"))
                act.activation(dst[:, H0:T], ps[:, 5, 0:T - H0], ACT.Copy).then_inc(S["copied1"], 1)

            def feat(blocks):
                i = 0
                for func, dst, opts in blocks:
                    for half, (lo, hi) in enumerate(HALVES):
                        act.wait_ge(S["feat_ready"], n.take("feat_ready"))
                        more = {"accum_out": half_sum[:, half:half + 1]} if "sums" in opts else {}
                        act.activation(dst[:, lo:hi], ps[0:dst.shape[0], i % 4, 0:hi - lo], func,
                                       bias=opts.get("bias", 0.0), **more).then_inc(S["feat_done"], 1)
                        i += 1

            def gelu_rows(dst):
                for t in range(NT):
                    act.wait_ge(S["tok_ready"], n.take("tok_ready"))
                    act.activation(dst[:, t, :], ps[:, 4 + t % 4, 0:D], ACT.Gelu).then_inc(S["tok_done_a"], 1)

            def attention(spec):
                def tanh_layer(u):
                    for g in range(P // 8):
                        i = u * (P // 8) + g
                        if i >= 4:
                            act.wait_ge(S["hidden_used"], used + (i - 3))
                        act.activation(tanh_ring(g)[:, 0:T], hid[:, 2, 0:T], ACT.Tanh, bias=hqb[:, i:i + 1])\
                            .then_inc(S["hidden_ready"], 1)

                def exponentials(u):
                    act.wait_ge(S["max_ready"], n.take("max_ready"))
                    keys = spec.keys(u)
                    src = masked[:, u % 2, 0:keys] if spec.mask else scores_ap(u, keys)
                    dst = probs[:, u % 2, 0:keys] if spec.mask else cut(probs[:, u % 2, 0:keys], keys)
                    act.activation(dst, src, ACT.Exp, bias=neg_top[:, u % 2:u % 2 + 1],
                                   scale=1.0 if spec.mask else spec.scale,
                                   accum_out=total[:, u % 4:u % 4 + 1]).then_inc(S["probs_ready"], 1)

                def copy_half(u):
                    tiles = len(key_tiles(spec.keys(u)))
                    if tiles > 3:
                        act.wait_ge(S["turned1"], n.take("turned1"))
                        act.activation(flat(probsT[:, 3:tiles, :]), ps[:, 5, 0:(tiles - 3) * P], ACT.Copy)\
                            .then_inc(S["copied1"], 1)

                used = n.now("hidden_used")
                if spec.additive:
                    n.take("hidden_used", spec.units * P // 8)
                    act.wait_ge(S["query_part_ready"], n.take("query_part_ready"))
                    tanh_layer(0)
                    tanh_layer(1)
                exponentials(0)
                exponentials(1)
                for u in range(spec.units):
                    copy_half(u)
                    if u + 2 < spec.units:
                        if spec.additive:
                            tanh_layer(u + 2)
                        exponentials(u + 2)

            def gate_exponentials(tiles):
                act.wait_ge(S["logits_ready"], n.take("logits_ready"))
                act.activation(ex[:, 0:tiles, :], lg2[:, 0:tiles, :], ACT.Exp).then_inc(S["exps_ready"], 1)

            act.wait_ge(S["consts_loaded"], 48)
            act.activation(C("rel"), C("rel"), ACT.Sigmoid, bias=R("mult")).then_inc(S["decay_ready"], 1)
            with n.loop(act, "batch", B, S["loop_entered"]):
                n.take("tok_ready", NT)
                turned(xT_)
                feat([(ACT.Copy, QT[0:QK0, 0, :], {}), (ACT.Copy, KT[0:QK0, 0, :], {}),
                      (ACT.Copy, hid[:, 0, :], {}), (ACT.Gelu, hid[:, 1, :], {})])
                for t in range(NT):
                    act.wait_ge(S["tok_ready"], n.take("tok_ready"))
                    act.activation(y[:, t, :], ps[:, 4 + t % 4, P:2 * P], ACT.Gelu)
                    act.activation(V[:, t, :], ps[:, 4 + t % 4, 0:P], ACT.Copy).then_inc(S["tok_done_a"], 1)
                attention(LAYER0)
                turned(attT)
                n.take("tok_ready", NT)

                turned(xT_)
                feat([(ACT.Relu, hid[:, 0, :], {"bias": C("gfc1_b"), "sums": True})])
                n.take("tok_ready")
                feat([(ACT.Relu, hid[:, f, :], {"bias": merged_b1[:, f:f + 1]}) for f in range(FT)])
                n.take("tok_ready", NT)

                turned(xT_)
                rb = C("rope_bias")
                feat([(ACT.Identity, hid[:, i, :], {"bias": rb[:, i:i + 1]}) for i in range(4)])
                n.take("tok_ready", NT + 1)
                attention(LAYER1)
                turned(attT)
                n.take("tok_ready", NT)

                turned(xT_)
                feat([(ACT.Identity, hid[:, 0, :], {"bias": C("gate_kb")})])
                n.take("tok_ready", NT)
                gate_exponentials(NT)
                with n.loop(act, "l1", E // 2, S["loop_entered"]):
                    for k in range(2):
                        bias = wts[:, k, W1_BIAS:W1_BIAS + 8]
                        feat([(ACT.Identity, (QT, KT)[i // 2][:, i % 2, :], {"bias": bias[:, i:i + 1]})
                              for i in range(4)])
                        n.take("tok_ready", NT)
                        attention(EXPERT)
                        turned(attT)
                        n.take("tok_ready", NT)
                        turned(attT)
                        feat([(ACT.Gelu, hid[:, f, :], {"bias": bias[:, 4 + f:5 + f]}) for f in range(FT)])
                        gelu_rows(y)

                turned(xT_)
                feat([(ACT.Copy, QT[:, 0, :], {}), (ACT.Copy, KT[:, 0, :], {})])
                n.take("tok_ready", NT)
                feat([(ACT.Identity, hid[:, 3, :], {"bias": C("b1_2")})])
                feat([(ACT.Copy, hid[:, 2, :], {})])
                attention(LAYER2)

                turned(xT_)
                feat([(ACT.Copy, hid[:, 0, :], {})])
                act.wait_ge(S["logits_ready"], n.take("logits_ready"))
                act.activation(hid[:, 1, 0:T], hid[:, 0, 0:T], ACT.Exp, bias=pooled[:, 1:2],
                               accum_out=half_sum[:, 0:1]).then_inc(S["exps_ready"], 1)
                n.take("tok_ready")
                gate_exponentials(1)
                with n.loop(act, "l2", E // 2, S["loop_entered"]):
                    for k in range(2):
                        feat([(ACT.Gelu, hid[:, f, :], {"bias": wts[:, k, W2_BIAS + f:W2_BIAS + f + 1]})
                              for f in range(FT)])
                        gelu_rows((y, x1)[k])

                turned(xT_)
                with n.loop(act, "l3", E // 2, S["loop_entered"]):
                    for k in range(2):
                        feat([(ACT.Copy, QT[:, 0, :], {}), (ACT.Copy, KT[:, 0, :], {})])
                        n.take("tok_ready", NT)
                        attention(LAYER3)
                        turned(attT)
                        n.take("tok_ready", NT)

                turned(xT_)
                n.take("tok_ready", NT)
                gate_exponentials(NT)
                with n.loop(act, "l4", E // 2, S["loop_entered"]):
                    for k in range(2):
                        feat([(ACT.Relu, hid[:, f, :], {"bias": wts[:, k, W4_BIAS + f:W4_BIAS + f + 1]})
                              for f in range(F3 // P)])
                        n.take("tok_ready", NT)

        @block.vector
        def _(v):
            n = Tally("vector", per_turn)

            def over(ap, tiles, width):
                return ap.unsqueeze(1).to_broadcast([P, tiles, width])

            def ready():
                v.drain().then_inc(S["operand_ready"], 1)

            def norm(src, dst):
                for t in range(NT):
                    v.bn_stats(stats[:, t, :], src[:, t, :])
                v.drain()
                for t in range(NT):
                    v.bn_aggr(mv[:, t, :], stats[:, t, :])
                v.drain()
                v.tensor_scalar(var[:, :], mv[:, :, 1], EPS, None, ALU.add).then_inc(S["var_ready"], 1)
                v.wait_ge(S["rstd_ready"], n.take("rstd_ready"))
                for t in range(NT):
                    v.tensor_scalar(dst[:, t, :], src[:, t, :], mv[:, t, 0:1], rstd[:, t:t + 1],
                                    ALU.subtract, ALU.mult)
                v.drain()

            def turned(dst):
                v.wait_ge(S["turned0"], n.take("turned0"))
                v.tensor_copy(dst[:, 0:H0], ps[:, 4, 0:H0]).then_inc(S["copied0"], 1)

            def tok(tiles, use, done=True):
                for t in range(tiles):
                    v.wait_ge(S["tok_ready"], n.take("tok_ready"))
                    use(t, ps[:, 4 + t % 4, :]).then_inc(S["tok_done_v"], 1)

            def keep_values(t, product):
                return v.tensor_copy(V[:, t, :], product[:, 0:D])

            def add_to_h(t, product):
                return v.tensor_tensor(h[:, t, :], product[:, 0:D], h[:, t, :], ALU.add)

            def attention(spec, dst):
                def peak(u):
                    v.wait_ge(S["scores_ready"], n.take("scores_ready"))
                    keys, i = spec.keys(u), u % 2
                    if spec.mask:
                        v.scalar_tensor_tensor(cut(masked[:, i, 0:keys], keys), scores_ap(u, keys), spec.scale,
                                               mask_ap(spec, u), ALU.mult, ALU.add)
                        v.drain()
                        v.tensor_reduce(top[:, i:i + 1], masked[:, i, 0:keys], X, ALU.max)
                    else:
                        v.tensor_reduce(top[:, i:i + 1], scores_ap(u, keys), XY if keys > 512 else X, ALU.max)
                    v.drain()
                    if spec.additive:
                        v.tensor_scalar(top[:, i:i + 1], top[:, i:i + 1], R("b2_2"), None, ALU.add)
                        v.drain()
                        v.tensor_tensor(neg_top[:, i:i + 1], R("b2_2"), top[:, i:i + 1], ALU.subtract)\
                            .then_inc(S["max_ready"], 1)
                    else:
                        v.tensor_scalar(neg_top[:, i:i + 1], top[:, i:i + 1], -1.0 if spec.mask else -spec.scale,
                                        None, ALU.mult).then_inc(S["max_ready"], 1)

                def copy_half(u):
                    tiles = min(3, len(key_tiles(spec.keys(u))))
                    v.wait_ge(S["turned0"], n.take("turned0"))
                    v.tensor_copy(flat(probsT[:, 0:tiles, :]), ps[:, 4, 0:tiles * P]).then_inc(S["copied0"], 1)

                def divide(u):
                    v.reciprocal(rtotal[:, u % 2:u % 2 + 1], total[:, u % 4:u % 4 + 1])
                    v.drain()
                    v.wait_ge(S["heads_ready"], n.take("heads_ready"))
                    out = dst(u)
                    v.tensor_scalar(out, ps[:, 6 + u % 2, 0:out.shape[1]], rtotal[:, u % 2:u % 2 + 1], None, ALU.mult)

                peak(0)
                peak(1)
                for u in range(spec.units):
                    copy_half(u)
                    if u + 2 < spec.units:
                        peak(u + 2)
                    divide(u)
                v.drain()

            def gating(tiles, over_all):
                def wide(ap):
                    return ap.unsqueeze(2).to_broadcast([P, tiles, 8])

                L, L2, EX, PK, CD, M = lg[:, 0:tiles, :], lg2[:, 0:tiles, :], ex[:, 0:tiles, :], pick[:, 0:tiles, :], \
                    cand[:, 0:tiles, :], m1[:, 0:tiles]
                rank = over(C("rank8"), tiles, 8)

                def step(ins):
                    v.drain()
                    return ins

                def first_of_largest(src, picked):
                    step(v.tensor_reduce(M, src, X, ALU.max))
                    step(v.tensor_tensor(CD, src, wide(M), ALU.is_equal))
                    step(v.tensor_tensor(CD, CD, rank, ALU.mult))
                    step(v.tensor_reduce(M, CD, X, ALU.max))
                    step(v.tensor_tensor(picked, CD, wide(M), ALU.is_equal))

                def over_sum(dst, src, values, tiny):
                    step(v.tensor_reduce(M, values, X, ALU.add))
                    step(v.tensor_scalar(M, M, tiny, None, ALU.add))
                    step(v.reciprocal(M, M))
                    step(v.tensor_tensor(dst, src, wide(M), ALU.mult))

                step(v.tensor_reduce(M, L, X, ALU.max))
                step(v.tensor_tensor(L2, L, wide(M), ALU.subtract).then_inc(S["logits_ready"], 1))
                first_of_largest(L, PK)
                v.wait_ge(S["exps_ready"], n.take("exps_ready"))
                step(v.scalar_tensor_tensor(L2, PK, FAR, L, ALU.mult, ALU.add))
                if over_all:
                    over_sum(EX, EX, EX, 0.0)
                step(v.tensor_reduce(M, L2, X, ALU.max))
                step(v.tensor_tensor(CD, L2, wide(M), ALU.is_equal))
                step(v.tensor_tensor(CD, CD, rank, ALU.mult))
                step(v.tensor_reduce(M, CD, X, ALU.max))
                step(v.tensor_tensor(CD, CD, wide(M), ALU.is_equal))
                step(v.tensor_tensor(PK, PK, CD, ALU.add))
                step(v.tensor_tensor(EX, EX, PK, ALU.mult))
                over_sum(gates[:, :, 0:tiles].rearrange("p e t -> p t e"), EX, EX, 1e-9 if over_all else 0.0)

            def gate_column(e, tiles):
                v.tensor_copy(gcol[:, 0:tiles], gates[:, e, 0:tiles])
                v.drain()

            for buf in (xT, xnT, attT, keyT, add_w):
                v.memset(buf[:, :], 0.0)
            for buf in (QT, KT, hid, probs, masked):
                v.memset(buf[:, :, :], 0.0)
            v.drain()
            v.wait_ge(S["consts_loaded"], 48)
            v.tensor_scalar(add_w[:, P:P + 8], C("onehot8"), C("w2_2"), None, ALU.mult)
            v.tensor_scalar(pool_w[:, :], ones, C("pool_w"), None, ALU.mult)
            for out, base, tasks in ((lng, R("ln_g"), R("tv_ln_g")), (lnb, R("ln_b"), R("tv_ln_b"))):
                for e in range(E):
                    dst = out[:, :] if e == 0 else spread[:, :]
                    v.tensor_tensor(dst, tasks[:, e * P:(e + 1) * P], base, ALU.subtract)
                    v.drain()
                    if e:
                        v.tensor_tensor(out[:, :], out[:, :], spread[:, :], ALU.add)
                        v.drain()
                v.scalar_tensor_tensor(out[:, :], out[:, :], MERGE, base, ALU.mult, ALU.add)
            v.wait_ge(S["decay_ready"], 1)
            v.tensor_tensor(C("rel"), C("rel"), C("causal"), ALU.add)
            v.drain().then_inc(S["setup_done"], 1)
            v.sem_inc(S["x_free"], 1)
            v.sem_inc(S["wts_free"], 2)

            with n.loop(v, "batch", B, S["loop_entered"]):
                v.wait_ge(S["h_free"], n.take("h_free"))
                tok(NT, lambda t, product: v.tensor_scalar(h[:, t, :], product[:, 0:D], 0.0, None, ALU.max))
                v.drain().then_inc(S["x_free"], 1)

                norm(h, x1)
                norm(x1, xn)
                ready()
                turned(xT_)
                v.wait_ge(S["feat_done"], n.take("feat_done", 8))
                v.tensor_tensor(hid[:, 2, 0:T], hid[:, 0, 0:T], hid[:, 1, 0:T], ALU.mult)
                n.take("tok_ready", NT)
                v.wait_ge(S["tok_done_a"], n.take("tok_done_a", NT))
                v.tensor_tensor(V[:, 0:NT, :], V[:, 0:NT, :], y[:, :, :], ALU.mult)
                ready()
                attention(LAYER0, lambda u: att[:, u, :])
                ready()
                turned(attT)
                tok(NT, lambda t, product: v.tensor_tensor(x1[:, t, :], product[:, 0:D], x1[:, t, :], ALU.add))
                v.drain()
                v.tensor_tensor(flat(h), flat(h), flat(x1), ALU.add)
                v.drain()

                norm(h, xn)
                ready()
                turned(xT_)
                v.wait_ge(S["feat_done"], n.take("feat_done", 2))
                v.tensor_tensor(pooled[:, 0:1], half_sum[:, 0:1], half_sum[:, 1:2], ALU.add)
                v.drain()
                v.tensor_scalar(spread[:, :], ones, pooled[:, 0:1], 1.0 / T, ALU.mult, ALU.mult)
                ready()
                v.wait_ge(S["tok_ready"], n.take("tok_ready"))
                v.tensor_tensor(g8[:, :], ps[:, 4, 0:8], R("gfc2_b"), ALU.add)
                v.drain()
                for dst, base, tasks in ((merged, C("w1w2"), None), (merged_b1, C("b1"), C("tv_b1")),
                                         (merged_b2, R("b2"), R("tv_b2"))):
                    width = base.shape[1]
                    for e in range(E):
                        task = tv[:, e, :] if tasks is None else tasks[:, e * width:(e + 1) * width]
                        v.scalar_tensor_tensor(dst[:, :], task, g8[:, e:e + 1], base if e == 0 else dst[:, :],
                                               ALU.mult, ALU.add)
                        v.drain()
                ready()
                n.take("feat_done", 8)
                tok(NT, lambda t, product: v.tensor_tensor(y[:, t, :], product[:, 0:D], xn[:, t, :], ALU.add))
                v.drain()
                v.tensor_tensor(y[:, :, :], y[:, :, :], over(merged_b2[:, :], NT, D), ALU.add)
                v.drain()
                norm(y, y)
                v.tensor_tensor(y[:, :, :], y[:, :, :], over(lng[:, :], NT, D), ALU.mult)
                v.drain()
                v.tensor_tensor(y[:, :, :], y[:, :, :], over(lnb[:, :], NT, D), ALU.add)
                v.drain()
                v.tensor_tensor(flat(h), flat(h), flat(y), ALU.add)
                v.drain()

                norm(h, xn)
                ready()
                turned(xT_)
                v.wait_ge(S["feat_done"], n.take("feat_done", 8))
                for i, dst in ((0, QT[:, 0, 0:T]), (2, keyT[:, PAD:PAD + T])):
                    v.tensor_tensor(masked[:, 0, 0:T], hid[:, i, 0:T], C("rope_cos"), ALU.mult)
                    v.tensor_tensor(masked[:, 1, 0:T], hid[:, i + 1, 0:T], C("rope_sin"), ALU.mult)
                    v.drain()
                    v.tensor_tensor(dst, masked[:, 0, 0:T], masked[:, 1, 0:T], ALU.add)
                    v.drain()
                tok(NT + 1, keep_values)
                ready()
                attention(LAYER1, lambda u: att[:, u, :])
                ready()
                turned(attT)
                tok(NT, add_to_h)
                v.drain()

                norm(h, xn)
                ready()
                turned(xT_)
                n.take("feat_done", 2)
                tok(NT, lambda t, product: v.tensor_scalar(lg[:, t, :], product[:, 0:8], float(D) ** -0.5, None,
                                                           ALU.mult))
                v.drain()
                gating(NT, True)
                with n.loop(v, "l1", E // 2, S["loop_entered"]) as pair:
                    for k in range(2):
                        def rows_over(r):
                            return over(wrow_of(k, r), NT, D)
                        n.take("feat_done", 8)
                        tok(NT, keep_values)
                        attention(EXPERT, lambda u: att[:, u % NT, (u // NT) * HD:(u // NT + 1) * HD])
                        ready()
                        turned(attT)
                        tok(NT, lambda t, product: v.tensor_tensor(y[:, t, :], product[:, 0:D], xn[:, t, :], ALU.add))
                        v.drain()
                        norm(y, x1)
                        v.tensor_tensor(x1[:, :, :], x1[:, :, :], rows_over(R_G1), ALU.mult)
                        v.drain()
                        v.tensor_tensor(x1[:, :, :], x1[:, :, :], rows_over(R_BE1), ALU.add)
                        ready()
                        turned(attT)
                        n.take("feat_done", 8)
                        n.take("tok_ready", NT)
                        v.wait_ge(S["tok_done_a"], n.take("tok_done_a", NT))
                        v.tensor_tensor(flat(y), flat(y), flat(x1), ALU.add)
                        v.drain()
                        norm(y, y)
                        v.tensor_tensor(y[:, :, :], y[:, :, :], rows_over(R_G2), ALU.mult)
                        gate_column(pair * 2 + k, NT)
                        v.tensor_tensor(y[:, :, :], y[:, :, :], rows_over(R_BE2), ALU.add)
                        v.drain()
                        for t in range(NT):
                            v.scalar_tensor_tensor(h[:, t, :], y[:, t, :], gcol[:, t:t + 1], h[:, t, :],
                                                   ALU.mult, ALU.add)
                        v.drain().then_inc(S["wts_free"], 1)

                norm(h, xn)
                ready()
                turned(xT_)
                n.take("feat_done", 4)
                tok(NT, keep_values)
                v.wait_ge(S["feat_done"], n.take("feat_done", 4))
                v.tensor_scalar(QT[:, 1, 0:T], QT[:, 0, 0:T], float(D) ** -0.5, None, ALU.mult)
                pairs = flat(y).rearrange("p (g j) -> p g j", j=8)
                v.tensor_tensor(pairs, hid[:, 3, :].rearrange("p (g j) -> p g j", j=8),
                                over(C("onehot8"), TP // 8, 8), ALU.mult)
                v.drain()
                v.tensor_reduce(hqb[:, :], pairs, X, ALU.add).then_inc(S["query_part_ready"], 1)
                ready()
                attention(LAYER2, lambda u: att[:, u, :])
                v.tensor_tensor(flat(h), flat(h), flat(att), ALU.add)
                v.drain()

                norm(h, xn)
                ready()
                turned(xT_)
                v.wait_ge(S["feat_done"], n.take("feat_done", 2))
                v.tensor_reduce(pooled[:, 0:1], hid[:, 0, 0:T], X, ALU.max)
                v.drain()
                v.tensor_scalar(pooled[:, 0:1], pooled[:, 0:1], R("pool_b"), None, ALU.add)
                v.drain()
                v.tensor_tensor(pooled[:, 1:2], R("pool_b"), pooled[:, 0:1], ALU.subtract)\
                    .then_inc(S["logits_ready"], 1)
                v.wait_ge(S["exps_ready"], n.take("exps_ready"))
                v.tensor_tensor(hid[:, 2, 0:T], hid[:, 1, 0:T], xT_[:, 0:T], ALU.mult)
                v.reciprocal(rtotal[:, 0:1], half_sum[:, 0:1])
                v.drain()
                v.tensor_reduce(pooled[:, 2:3], hid[:, 2, 0:T], X, ALU.add)
                v.drain()
                v.tensor_scalar(pooled[:, 3:4], pooled[:, 2:3], rtotal[:, 0:1], None, ALU.mult)
                v.drain()
                v.tensor_scalar(spread[:, :], ones, pooled[:, 3:4], None, ALU.mult)
                ready()
                tok(1, lambda t, product: v.tensor_tensor(lg[:, 0, :], product[:, 0:8], R("gate_b2"), ALU.add))
                v.drain()
                gating(1, True)
                with n.loop(v, "l2", E // 2, S["loop_entered"]) as pair:
                    for k in range(2):
                        n.take("feat_done", 8)
                        n.take("tok_ready", NT)
                        gate_column(pair * 2 + k, 1)
                        v.wait_ge(S["tok_done_a"], n.take("tok_done_a", NT))
                        v.scalar_tensor_tensor(flat(h), flat((y, x1)[k]), gcol[:, 0:1], flat(h), ALU.mult, ALU.add)
                        v.drain().then_inc(S["wts_free"], 1)

                norm(h, xn)
                ready()
                turned(xT_)
                with n.loop(v, "l3", E // 2, S["loop_entered"]):
                    for k in range(2):
                        n.take("feat_done", 4)
                        tok(NT, keep_values)
                        attention(LAYER3, lambda u: att[:, u, :])
                        ready()
                        turned(attT)
                        tok(NT, add_to_h)
                        v.drain().then_inc(S["wts_free"], 1)

                norm(h, xn)
                ready()
                turned(xT_)
                tok(NT, lambda t, product: v.tensor_copy(lg[:, t, :], product[:, 0:8]))
                v.drain()
                gating(NT, False)
                with n.loop(v, "l4", E // 2, S["loop_entered"]) as pair:
                    for k in range(2):
                        gate_column(pair * 2 + k, NT)
                        n.take("feat_done", 4)
                        tok(NT, lambda t, product: v.scalar_tensor_tensor(
                            h[:, t, :], product[:, 0:D], gcol[:, t:t + 1], h[:, t, :], ALU.mult, ALU.add))
                        v.drain().then_inc(S["wts_free"], 1)


def _layout(a):
    import numpy as np

    f32 = np.float32

    def down(w, tiles):
        return w.T.reshape(tiles, P, -1).transpose(1, 0, 2).reshape(P, -1)

    def columns(b, tiles):
        return b.reshape(tiles, P).T

    x_off = np.arange(TP)[None, :] - (NT - 1) * P - np.arange(P)[:, None]
    win = np.arange(2 * P)[None, :] - np.arange(P)[:, None]
    inv = (f32(1.0) / f32(10000.0) ** (np.arange(0, D, 2, dtype=f32) / f32(D))).astype(f32)
    freqs = np.arange(T, dtype=f32)[:, None] * inv[None, :]
    emb = np.concatenate([np.sin(freqs), np.cos(freqs)], -1).astype(f32)
    sin, cos = emb[:, ::2].T, emb[:, 1::2].T
    even_odd = np.r_[0:D:2, 1:D:2]
    odd_even = np.r_[1:D:2, 0:D:2]
    valid = np.zeros((P, TPAD), f32)
    valid[:, PAD:PAD + T] = 1.0
    exp = a["L0_attn_expand"]
    lin0, pre0 = 2 * QK0, 2 * QK0 + 2 * D
    const = {
        "ident": np.eye(P, dtype=f32), "ones": np.ones((P, P), f32),
        "onehot8": (np.arange(P)[:, None] // 16 == np.arange(8)[None, :]).astype(f32),
        "rank8": np.broadcast_to(np.arange(8, 0, -1).astype(f32), (P, 8)),
        "tok_w": a["L0_tok_weight"].T.reshape(CONTEXT, P, P).transpose(1, 0, 2).reshape(P, -1),
        "expand_q": exp[:, 0:QK0], "expand_k": exp[:, QK0:2 * QK0],
        "expand_lin": exp[:, lin0:lin0 + D], "expand_pre": exp[:, pre0:pre0 + D],
        "expand_v": np.concatenate([exp[:, lin0 + D:pre0], exp[:, pre0 + D:]], 1),
        "project": a["L0_attn_project"].reshape(2, P, D).transpose(1, 0, 2).reshape(P, -1),
        "rel": x_off.astype(f32), "causal": np.where(x_off <= 0, 0.0, FAR).astype(f32), "valid": valid,
        "gfc1": a["L0_ffn_gfc1_w"].T, "gfc1_b": a["L0_ffn_gfc1_b"][:, None], "gfc2": a["L0_ffn_gfc2_w"].T,
        "w1w2": np.concatenate([a["L0_ffn_W1"].T, down(a["L0_ffn_W2"], FT)], 1),
        "b1": columns(a["L0_ffn_b1"], FT),
        "tv_b1": np.concatenate([columns(b, FT) for b in a["L0_ffn_tv_b1"]], 1),
        "rope_qa": a["L1_attn_Wq"][even_odd].T, "rope_qb": a["L1_attn_Wq"][odd_even].T,
        "rope_ka": a["L1_attn_Wk"][even_odd].T, "rope_kb": a["L1_attn_Wk"][odd_even].T,
        "rope_bias": np.stack([a["L1_attn_bq"][even_odd], a["L1_attn_bq"][odd_even],
                               a["L1_attn_bk"][even_odd], a["L1_attn_bk"][odd_even]], 1),
        "rope_cos": np.concatenate([cos, cos]), "rope_sin": np.concatenate([-sin, sin]),
        "v1": a["L1_attn_Wv"].T, "o1": a["L1_attn_Wo"].T,
        "band": np.where((win >= 0) & (win < WINDOW), 0.0, FAR).astype(f32),
        "gate_k": a["L1_ffn_gate_Wk"].T, "gate_kb": a["L1_ffn_gate_bk"][:, None],
        "queries": a["L1_ffn_expert_queries"].T,
        "q2": a["L2_attn_Wq"].T, "k2": a["L2_attn_Wk"].T, "v2": a["L2_attn_Wv"].T,
        "hq2": np.tile(a["L2_attn_W1"][:, :D].T, (1, 8)), "hk2": np.tile(a["L2_attn_W1"][:, D:].T, (1, 8)),
        "b1_2": np.tile(a["L2_attn_b1"], 8)[:, None], "w2_2": np.tile(a["L2_attn_W2"][0], 8)[:, None],
        "pool_w": a["L2_ffn_attn_w"], "gate_w2": a["L2_ffn_gate_w"], "gate_w3": a["L3_ffn_gate_w"],
    }
    rows = {
        "tok_b": a["L0_tok_bias"], "mult": a["L0_attn_position_bias_mult"].reshape(1), "gfc2_b": a["L0_ffn_gfc2_b"],
        "b2": a["L0_ffn_b2"], "tv_b2": a["L0_ffn_tv_b2"].reshape(-1), "ln_g": a["L0_ffn_ln_g"],
        "tv_ln_g": a["L0_ffn_tv_ln_g"].reshape(-1), "ln_b": a["L0_ffn_ln_b"],
        "tv_ln_b": a["L0_ffn_tv_ln_b"].reshape(-1), "bv1": a["L1_attn_bv"], "bo1": a["L1_attn_bo"],
        "b2_2": a["L2_attn_b2"], "pool_b": a["L2_ffn_attn_b"], "gate_b2": a["L2_ffn_gate_b"],
        "gate_b3": a["L3_ffn_gate_b"],
    }
    def heads_apart(w):
        out = np.zeros((E, 32) + w.shape[1:], f32)
        out[:, :HD] = w.reshape((E, HD) + w.shape[1:])
        return out.reshape((2, P) + w.shape[1:])

    l1, l1r = [], []
    for e in range(E):
        wq, wk, wv = a["L1_ffn_Wqkv"][e].reshape(3, D, D)
        bq, bk, bv = a["L1_ffn_bqkv"][e].reshape(3, D)
        l1.append(np.concatenate([heads_apart(wq).reshape(2 * P, D).T, heads_apart(wk).reshape(2 * P, D).T, wv.T,
                                  a["L1_ffn_Wo"][e].T, a["L1_ffn_W1"][e].T, down(a["L1_ffn_W2"][e], FT),
                                  heads_apart(bq).T, heads_apart(bk).T, columns(a["L1_ffn_bf1"][e], FT)], 1))
        l1r.append(np.concatenate([bv, a["L1_ffn_bo"][e], a["L1_ffn_bf2"][e], a["L1_ffn_g1"][e], a["L1_ffn_be1"][e],
                                   a["L1_ffn_g2"][e], a["L1_ffn_be2"][e]]))
    out = {
        "const": np.concatenate([const[name].reshape(P, width) for name, width in CONST], 1),
        "rows": np.concatenate([rows[name].reshape(width) for name, width in ROWS])[None],
        "tv": np.stack([np.concatenate([a["L0_ffn_tv_W1"][e].T, down(a["L0_ffn_tv_W2"][e], FT)], 1)
                        for e in range(E)], 1),
        "xT": a["x"].transpose(0, 2, 1),
        "l1": np.stack(l1), "l1_rows": np.stack(l1r),
        "l2": np.stack([np.concatenate([a["L2_ffn_w1"][e], down(a["L2_ffn_w2"][e].T, FT),
                                        columns(a["L2_ffn_b1"][e], FT)], 1) for e in range(E)]),
        "l2_rows": a["L2_ffn_b2"],
        "l3": np.stack([np.concatenate([a[f"L3_attn_W{c}"][e * D:(e + 1) * D].T for c in "qkv"] +
                                       [a["L3_attn_Wo"][:, e * D:(e + 1) * D].T], 1) for e in range(E)]),
        "l4": np.stack([np.concatenate([a["L3_ffn_w1"][e], down(a["L3_ffn_w2"][e].T, F3 // P),
                                        columns(a["L3_ffn_b1"][e], F3 // P)], 1) for e in range(E)]),
        "l4_rows": a["L3_ffn_b2"],
    }
    return {name: np.ascontiguousarray(value, dtype=f32) for name, value in out.items()}


def kernel(**inputs):
    import numpy as np
    import concourse.bacc as bacc
    from concourse.bass_utils import run_bass_kernel_spmd as run

    arrays = _layout({name: np.asarray(value) for name, value in inputs.items()})
    per_turn = {}
    for _ in range(2):
        nc = bacc.Bacc("TRN2", target_bir_lowering=False, num_devices=1)
        tensors = {name: nc.dram_tensor("in_" + name, value.shape, F32, kind="ExternalInput").ap()
                   for name, value in arrays.items()}
        tensors["out"] = nc.dram_tensor("out", (B, T, D), F32, kind="ExternalOutput").ap()
        audio_tower(nc, tensors, per_turn)
    r = run(nc, [{"in_" + name: value for name, value in arrays.items()}], core_ids=[0])
    return r.results[0]["out"]
```

```python
from contextlib import ExitStack, contextmanager

import concourse.bass as bass
from concourse import mybir

F32 = mybir.dt.float32
BF16 = mybir.dt.bfloat16
ALU = mybir.AluOpType
ACT = mybir.ActivationFunctionType
X = mybir.AxisListType.X
XY = mybir.AxisListType.XY

B, T_IN, D = 4, 750, 128
CONTEXT = 3
T = T_IN - CONTEXT + 1
P = 128
NT = (T + P - 1) // P
TP = NT * P
H0 = 3 * P
HALVES = ((0, H0), (H0, T))
E = 8
QK0 = 16
HD = D // E
F = 512
FT = F // P
F3 = 256
WINDOW = 128
PAD = WINDOW // 2
TPAD = TP + 2 * PAD
EPS = 1e-5
MERGE = 0.03
FAR = -1.0e30

W1_Q, W1_K, W1_V, W1_O, W1_UP, W1_DOWN = 0, 128, 256, 384, 512, 1024
W1_BIAS = 1536
W1_END = W1_BIAS + 7
R_BV, R_BO, R_G1, R_BE1, R_G2, R_BE2 = range(6)
W2_UP, W2_DOWN, W2_BIAS, W2_END = 0, 512, 1024, 1029
W3_Q, W3_K, W3_V, W3_O, W3_END = 0, 128, 256, 384, 512
W4_UP, W4_DOWN, W4_BIAS, W4_END = 0, 256, 512, 515

CONST = [
    ("ident", P), ("ones", P), ("onehot8", 8), ("rank8", 8),
    ("tok_w", 3 * P), ("expand_q", QK0), ("expand_k", QK0), ("expand_lin", P), ("expand_pre", P),
    ("expand_v", 2 * P), ("project", 2 * P), ("rel", TP), ("causal", TP), ("valid", TPAD),
    ("gfc1", P), ("gfc1_b", 1), ("gfc2", 8), ("w1w2", 2 * F), ("b1", FT), ("tv_b1", E * FT),
    ("rope_qa", P), ("rope_qb", P), ("rope_ka", P), ("rope_kb", P), ("rope_bias", 4),
    ("rope_cos", T), ("rope_sin", T), ("v1", P), ("o1", P), ("band", 2 * P),
    ("gate_k", P), ("gate_kb", 1), ("queries", 8),
    ("q2", P), ("k2", P), ("v2", P), ("hq2", P), ("hk2", P), ("b1_2", 1), ("w2_2", 1),
    ("pool_w", 1), ("gate_w2", 8), ("gate_w3", 8),
]
ROWS = [
    ("tok_b", P), ("mult", 1), ("gfc2_b", 8), ("b2", P), ("tv_b2", E * P), ("ln_g", P),
    ("ln_b", P), ("bv1", P), ("bo1", P), ("b2_2", 1), ("pool_b", 1), ("gate_b2", 8), ("gate_b3", 8),
]


def offsets(parts):
    at, out = 0, {}
    for name, width in parts:
        out[name] = (at, width)
        at += width
    return out, at


CONST_AT, CONST_END = offsets(CONST)
ROWS_AT, ROWS_END = offsets(ROWS)

SEMAPHORES = [
    "loop_entered", "consts_loaded", "decay_ready", "setup_done", "x_loaded", "x_free", "h_free", "h_final", "h_stored", "wts_free", "wts_loaded0", "wts_loaded1",
    "operand_ready",
    "feat_ready", "feat_done",
    "tok_ready", "tok_done_v", "tok_done_a",
    "turned0", "turned1", "copied0", "copied1",
    "var_ready", "rstd_ready",
    "scores_ready", "max_ready", "probs_ready", "heads_ready",
    "hidden_ready", "hidden_used",
    "expert_q_ready", "parts_ready", "stacks_loaded",
    "peak_ready", "peak_done",
    "shift_split",
    "ring_ready", "ring_done",
    "group_ready",
    "lifted",
    "query_part_ready",
    "logits_ready", "exps_ready",
]


class Tally:

    def __init__(self, engine, per_turn):
        self.engine, self.per_turn, self.n, self.loops = engine, per_turn, {}, []

    def now(self, name):
        value = self.n.get(name, 0)
        for register, loop in self.loops:
            per = self.per_turn.get((self.engine, loop, name), 0)
            if per:
                value = register * per + value
        return value

    def take(self, name, count=1):
        self.n[name] = self.n.get(name, 0) + count
        return self.now(name)

    @contextmanager
    def loop(self, eng, name, turns, entered):
        before = dict(self.n)
        eng.sem_inc(entered, 1)
        with eng.Fori(0, turns) as i:
            self.loops.append((i, name))
            yield i
            self.loops.pop()
        for key, n in list(self.n.items()):
            per = n - before.get(key, 0)
            self.per_turn[(self.engine, name, key)] = per
            self.n[key] = before.get(key, 0) + turns * per


def key_tiles(n):
    return list(range((n + P - 1) // P))


class Attention:

    def __init__(self, units, keys, scale, mask=None, product_mask=None, additive=False):
        self.units, self.keys, self.scale, self.mask = units, keys, scale, mask
        self.product_mask, self.additive = product_mask, additive


def causal_keys(tile):
    return min((tile + 1) * P, T)


LAYER0 = Attention(NT, lambda u: causal_keys(u % NT), 0.25, "rel")
LAYER1 = Attention(NT, lambda u: 2 * P, float(D) ** -0.5, product_mask="band")
LAYER2 = Attention(NT, lambda u: T, 1.0, additive=True)
LAYER3 = Attention(NT, lambda u: causal_keys(u % NT), float(D) ** -0.5, product_mask="diagonal")


Q_PARTS, K_PARTS = (0, 0, 1, 0, 1, 2), (0, 1, 0, 2, 1, 0)
STACK = len(Q_PARTS) * HD
SHIFT = 2
AHEAD = 9
PT_RING = 4
PLACE = 32
GROUP = P // PLACE


def expert_steps():
    units, lag = E * NT, 2
    for m in range(AHEAD):
        yield "peak", m
        if m == NT:
            yield "shift", 0
    for n in range(units + lag):
        if n < units:
            yield "scores", n
        if n + AHEAD < units:
            yield "peak", n + AHEAD
        if n % NT == 4 and n // NT + 1 < E:
            yield "shift", n // NT + 1
        if n >= lag:
            yield "weigh", n - lag
            if (n - lag) % (GROUP * NT) == 1 and n - lag > 1:
                yield "divide", n // (GROUP * NT) - 1
            if (n - lag) % (GROUP * NT) == GROUP * NT - 1:
                yield "lift", (n - lag) // (GROUP * NT)
    yield "divide", E // GROUP - 1


def additive_groups():
    return [4 * (i % 4) + i // 4 for i in range(P // 8)]


def cut(ap, n):
    return ap if n <= 512 else ap.rearrange("p (a n) -> p a n", a=2)


def audio_tower(nc, A, per_turn):
    with ExitStack() as ctx:
        def sb(name, shape, dt=F32):
            return ctx.enter_context(nc.sbuf_tensor(name, shape, dt))

        S = {name: ctx.enter_context(nc.semaphore(name)) for name in SEMAPHORES}
        ps = ctx.enter_context(nc.psum_tensor("ps", [P, 8, 512], F32))

        const = sb("const", [P, CONST_END])
        rows = sb("rows", [P, ROWS_END])
        tv = sb("tv", [P, E, 2 * F])
        wts = sb("wts", [P, 2, W1_END])
        wrow = sb("wrow", [P, 2, 6 * P])
        xT = sb("xT", [P, TP + CONTEXT - 1])
        h = sb("h", [P, NT, D])
        xn = sb("xn", [P, NT, D])
        x1 = sb("x1", [P, NT, D])
        y = sb("y", [P, NT, D])
        att = sb("att", [P, NT, D])
        xnT = sb("xnT", [P, TPAD])
        attT = sb("attT", [P, TP])
        QT = sb("QT", [P, 2, TP])
        KT = sb("KT", [P, 2, TP])
        V = sb("V", [P, NT + 1, D])
        hid = sb("hid", [P, FT, TP])
        masked = sb("masked", [P, 2, TP])
        probs = sb("probs", [P, 2, TP])
        probsT = sb("probsT", [P, 6, P])
        merged = sb("merged", [P, 2 * F])
        merged_b1 = sb("merged_b1", [P, FT])
        merged_b2 = sb("merged_b2", [P, P])
        stats = sb("stats", [P, NT, 6])
        mv = sb("mv", [P, NT, 2])
        var = sb("var", [P, NT])
        rstd = sb("rstd", [P, NT])
        minus_half = sb("minus_half", [P, NT])
        top = sb("top", [P, 2])
        neg_top = sb("neg_top", [P, 2])
        total = sb("total", [P, 4])
        rtotal = sb("rtotal", [P, 2])
        half_sum = sb("half_sum", [P, 2])
        pooled = sb("pooled", [P, 4])
        spread = sb("spread", [P, P])
        g8 = sb("g8", [P, 8])
        parts = sb("parts", [P, 2, 3, TP], BF16)
        q_stack = sb("q_stack", [P, E, TP], BF16)
        k_stack = sb("k_stack", [STACK + SHIFT, E, TP], BF16)
        maskb = sb("maskb", [P, 3 * P], BF16)
        identb = sb("identb", [P, P], BF16)
        V32 = sb("V32", [P, NT, E, PLACE])
        peaks = sb("peaks", [P, 2, NT])
        peaks2 = sb("peaks2", [P, 2, NT, SHIFT], BF16)
        rsum = sb("rsum", [P, 2, 3 * GROUP])
        add_w = sb("add_w", [P, 64])
        hqb = sb("hqb", [P, TP // 8])
        lng = sb("lng", [P, P])
        lnb = sb("lnb", [P, P])
        pool_w = sb("pool_w", [P, P])
        lg = sb("lg", [P, NT, 8])
        lg2 = sb("lg2", [P, NT, 8])
        ex = sb("ex", [P, NT, 8])
        pick = sb("pick", [P, NT, 8])
        cand = sb("cand", [P, NT, 8])
        m1 = sb("m1", [P, NT])
        gates = sb("gates", [P, 8, NT])
        gcol = sb("gcol", [P, NT])

        keyT = q_stack[:, :, :].rearrange("p e t -> p (e t)").bitcast(F32)[:, 0:TPAD]

        def C(name):
            at, width = CONST_AT[name]
            return const[:, at:at + width]

        def R(name):
            at, width = ROWS_AT[name]
            return rows[:, at:at + width]

        ident, ones = C("ident"), C("ones")
        xT_ = xnT[:, PAD:PAD + TP]
        onerow = const[0:1, CONST_AT["ones"][0]:CONST_AT["ones"][0] + P]

        def row(ap):
            return ap[0:1]

        def tile_of(ap, t):
            return ap[:, t * P:(t + 1) * P]

        def flat(ap):
            return ap[:, :, :].rearrange("p t d -> p (t d)")

        def wrow_of(k, r):
            return wrow[:, k, r * P:(r + 1) * P]

        def scores_ap(u, n):
            return ps[:, 2 * (u % 2), 0:n] if n <= 512 else ps[:, 2 * (u % 2):2 * (u % 2) + 2, 0:n // 2]

        def probsT_ring(n):
            return (probs, masked)[n % PT_RING // 2][:, n % 2, :]

        def keys_in(j):
            return min(P, T - j * P)

        def tanh_ring(i):
            return hid[:, i % 4, :] if i % 4 < 2 else masked[:, i % 4 - 2, :]

        def mask_ap(spec, u):
            n = spec.keys(u)
            at = CONST_AT[spec.mask][0] + (NT - 1 - u % NT) * P
            return cut(const[:, at:at + n], n)

        block = ctx.enter_context(nc.Block())

        @block.sync
        def _(sp):
            n = Tally("sync", per_turn)
            sp.dma_start(const[:, :], A["const"]).then_inc(S["consts_loaded"], 16)
            sp.dma_start(rows[:, :], A["rows"].broadcast_to([P, ROWS_END])).then_inc(S["consts_loaded"], 16)
            sp.dma_start(tv[:, :, :], A["tv"]).then_inc(S["consts_loaded"], 16)
            sp.dma_start(flat(hid)[:, 0:2 * E * P], A["merge_rows"].broadcast_to([P, 2 * E * P]))\
                .then_inc(S["consts_loaded"], 16)
            sp.sem_inc(S["h_free"], 1)

            def load(src, srow, at, k):
                sp.wait_ge(S["wts_free"], n.take("wts_free"))
                sp.dma_start(wts[:, k, 0:src.shape[2]], src[at, :, :]).then_inc(S[f"wts_loaded{k}"], 16)
                if srow is not None:
                    sp.dma_start(wrow[:, k, 0:srow.shape[1]], srow[at, :].partition_broadcast(P))\
                        .then_inc(S[f"wts_loaded{k}"], 16)

            def stacks():
                sp.wait_ge(S["parts_ready"], n.take("parts_ready"))
                for i, (stack, order) in enumerate(((q_stack, Q_PARTS), (k_stack, K_PARTS))):
                    for g, part in enumerate(order):
                        sp.dma_start(stack[g * HD:(g + 1) * HD, :, 0:T],
                                     parts[:, i, part, 0:T])\
                            .then_inc(S["stacks_loaded"], 16)

            with n.loop(sp, "batch", B, S["loop_entered"]) as b:
                sp.wait_ge(S["x_free"], n.take("x_free"))
                sp.dma_start(xT[:, 0:T_IN], A["xT"][b, :, :]).then_inc(S["x_loaded"], 16)
                load(A["l1"], A["l1_rows"], 0, 0)
                load(A["l1"], A["l1_rows"], 1, 1)
                stacks()
                with n.loop(sp, "l1", E // 2 - 1, S["loop_entered"]) as pair:
                    for k in range(2):
                        stacks()
                        load(A["l1"], A["l1_rows"], pair * 2 + (k + 2), k)
                stacks()
                for stage, src, srow in (("l2", A["l2"], None),
                                         ("l3", A["l3"], None), ("l4", A["l4"], None)):
                    with n.loop(sp, stage, E // 2, S["loop_entered"]) as pair:
                        for k in range(2):
                            load(src, srow, pair * 2 + k, k)
                sp.wait_ge(S["h_final"], n.take("h_final"))
                full = (NT - 1) * P
                sp.dma_start(A["out"][b, 0:full, :].rearrange("(t p) d -> p t d", p=P), h[:, 0:NT - 1, :])\
                    .then_inc(S["h_stored"], 16)
                sp.dma_start(A["out"][b, full:T, :], h[0:T - full, NT - 1, :]).then_inc(S["h_stored"], 16)
                sp.wait_ge(S["h_stored"], n.take("h_stored", 32))
                sp.sem_inc(S["h_free"], 1)

        @block.gpsimd
        def _(pool):
            n = Tally("pool", per_turn)
            pool.memset(minus_half[:, :], -0.5)
            pool.drain()

            def power(times):
                for _ in range(times):
                    pool.wait_ge(S["var_ready"], n.take("var_ready"))
                    pool.tensor_tensor(rstd[:, :], var[:, :], minus_half[:, :], ALU.pow).then_inc(S["rstd_ready"], 1)

            with n.loop(pool, "batch", B, S["loop_entered"]):
                power(6)
                with n.loop(pool, "l1", E // 2 - 1, S["loop_entered"]):
                    power(4)
                power(4 + 4)

        @block.tensor
        def _(pe):
            n = Tally("tensor", per_turn)

            def turn(src, waited=False):
                if not waited:
                    pe.wait_ge(S["operand_ready"], n.take("operand_ready"))
                for half in range(2):
                    for t in range(3):
                        mm = pe.transpose(ps[:, 4 + half, t * P:(t + 1) * P], src[:, 3 * half + t, :], ident)
                    mm.then_inc(S[f"turned{half}"], 1)
                for half in range(2):
                    pe.wait_ge(S[f"copied{half}"], n.take(f"copied{half}"))

            def feat(blocks, rhs):
                base = n.now("feat_done")
                i = 0
                for w in blocks:
                    m = w.shape[1]
                    for lo, hi in HALVES:
                        if i >= 4:
                            pe.wait_ge(S["feat_done"], base + (i - 3))
                        pe.matmul(ps[0:m, i % 4, 0:hi - lo], w, rhs[:, lo:hi], start=True, stop=True)\
                            .then_inc(S["feat_ready"], 1)
                        i += 1
                pe.wait_ge(S["feat_done"], n.take("feat_done", i))

            def stream(jobs, start):
                base = n.now("feat_done")
                for i, (reads, terms, (lo, hi)) in enumerate(jobs):
                    pe.wait_ge(S["feat_done"], base + max(reads, i - 3))
                    for c, (w, rhs) in enumerate(terms):
                        mm = pe.matmul(ps[:, (start + i) % 4, 0:hi - lo], w, rhs[:, lo:hi],
                                       start=(c == 0), stop=(c == len(terms) - 1))
                    mm.then_inc(S["feat_ready"], 1)
                n.take("feat_done", len(jobs))

            def up_down(w, up, down, tiles, rhs, plane=0):
                ups = [(0, [(w[:, up + f * P:up + (f + 1) * P], rhs)], half) for half in HALVES for f in range(tiles)]
                downs = [(tiles * (i + 1), [(w[:, down + f * P:down + (f + 1) * P], hid[:, plane + f, :])
                                            for f in range(tiles)], half) for i, half in enumerate(HALVES)]
                return ups + downs

            def back(src, reads):
                pe.wait_ge(S["feat_done"], reads)
                for half in range(2):
                    for t in range(3):
                        mm = pe.transpose(ps[:, 4 + half, t * P:(t + 1) * P], tile_of(src, 3 * half + t), ident)
                    mm.then_inc(S["tok_ready"], 1)

            def tok(tiles, products, done, width=D):
                base = n.now(done)
                for t in range(tiles):
                    if t >= 4:
                        pe.wait_ge(S[done], base + (t - 3))
                    terms = products(t)
                    for i, (lhs, rhs) in enumerate(terms):
                        mm = pe.matmul(ps[:, 4 + t % 4, 0:width], lhs, rhs, start=(i == 0), stop=(i == len(terms) - 1))
                    mm.then_inc(S["tok_ready"], 1)
                pe.wait_ge(S[done], n.take(done, tiles))

            def attention(spec, query, key, value, dv, between=None):
                def scores(u):
                    keys = spec.keys(u)
                    width = keys if keys <= 512 else keys // 2
                    parts = range(keys // width)
                    masked_by = {"band": maskb[:, 0:2 * P], "diagonal": maskb[:, 2 * P:3 * P]}.get(spec.product_mask)
                    for a in parts:
                        mm = pe.matmul(ps[:, 2 * (u % 2) + a, 0:width], query(u), key(u)[:, a * width:(a + 1) * width],
                                       start=True, stop=not (spec.additive or masked_by is not None),
                                       skip_group_check=True)
                    if masked_by is not None:
                        left = min(masked_by.shape[1], keys - u * P if spec.product_mask == "diagonal" else keys)
                        for a in parts:
                            lo, hi = max(a * width, keys - left), (a + 1) * width
                            if lo < hi:
                                at = lo - (keys - left)
                                mm = pe.matmul(ps[:, 2 * (u % 2) + a, lo - a * width:width], identb[:, :],
                                               masked_by[:, at:at + hi - lo], start=False, stop=True,
                                               skip_group_check=True)
                    for i, g in enumerate(additive_groups() if spec.additive else ()):
                        pe.wait_ge(S["hidden_ready"], n.take("hidden_ready"))
                        at = 32 * (g // 4)
                        for a in parts:
                            last = pe.matmul(ps[at:at + 32, 2 * (u % 2) + a, 0:width],
                                             add_w[:, 32 - 8 * (g % 4):64 - 8 * (g % 4)],
                                             tanh_ring(i)[:, a * width:(a + 1) * width], start=False,
                                             stop=(i >= P // 8 - 4), skip_group_check=True)
                        last.then_inc(S["hidden_used"], 1)
                    if spec.additive:
                        pe.drain().then_inc(S["scores_ready"], 1)
                    else:
                        mm.then_inc(S["scores_ready"], 1)

                def spread_out(u):
                    pe.wait_ge(S["probs_ready"], n.take("probs_ready"))
                    tiles = key_tiles(spec.keys(u))
                    for half in range(2):
                        for j in tiles[3 * half:3 * half + 3]:
                            mm = pe.transpose(ps[:, 4 + half, (j % 3) * P:(j % 3 + 1) * P],
                                              probs[:, u % 2, j * P:(j + 1) * P], ident)
                        if tiles[3 * half:]:
                            mm.then_inc(S[f"turned{half}"], 1)

                def weigh(u):
                    tiles = key_tiles(spec.keys(u))
                    for j in tiles:
                        if j % 3 == 0:
                            pe.wait_ge(S[f"copied{j // 3}"], n.take(f"copied{j // 3}"))
                        mm = pe.matmul(ps[:, 6 + u % 2, 0:dv], probsT[:, j, :], value(u, j),
                                       start=(j == 0), stop=(j == len(tiles) - 1))
                    mm.then_inc(S["heads_ready"], 1)

                scores(0)
                scores(1)
                if between:
                    between()
                for u in range(spec.units):
                    spread_out(u)
                    if u + 2 < spec.units:
                        scores(u + 2)
                    weigh(u)

            def expert_attention():
                ring0, peak0, lift0 = n.now("ring_done"), n.now("peak_done"), n.now("lifted")
                entry = {}
                turns = 0
                pe.wait_ge(S["stacks_loaded"], n.take("stacks_loaded", 2 * len(Q_PARTS) * 16))

                def bank():
                    i = len(entry)
                    if i >= 2:
                        pe.wait_ge(S["ring_done"], ring0 + (i - 1))
                    return ps[:, i % 2, :]

                def pair():
                    if turns >= 2:
                        pe.wait_ge(S["peak_done"], peak0 + (turns - 1))
                    return 2 + 2 * (turns % 2)

                for what, n_ in expert_steps():
                    head, j = n_ // NT, n_ % NT
                    if what == "peak":
                        first, m = pair(), keys_in(j)
                        turns += 1
                        for a in range(2):
                            mm = pe.matmul(ps[0:m, first + a, 0:T // 2], q_stack[0:STACK, head, j * P:j * P + m],
                                           k_stack[0:STACK, head, a * T // 2:(a + 1) * T // 2], start=True, stop=True)
                        mm.then_inc(S["peak_ready"], 1)
                    elif what == "shift":
                        pe.wait_ge(S["shift_split"], n.take("shift_split"))
                        for half in range(2):
                            out = bank()
                            for t in range(3):
                                mm = pe.matmul(out[STACK:STACK + SHIFT, t * P:(t + 1) * P],
                                               peaks2[:, n_ % 2, 3 * half + t, :], identb[:, :], start=True, stop=True)
                            mm.then_inc(S["ring_ready"], 1)
                            entry[("shift", n_, half)] = len(entry)
                    elif what == "scores":
                        if j == 0:
                            pe.wait_ge(S["ring_done"], ring0 + (entry[("shift", head, 1)] + 1))
                        m = keys_in(j)
                        for half, (lo, hi) in enumerate(HALVES):
                            out = bank()
                            pe.matmul(out[0:m, 0:hi - lo], k_stack[:, head, j * P:j * P + m], q_stack[0:STACK + SHIFT, head, lo:hi],
                                      start=True, stop=True).then_inc(S["ring_ready"], 1)
                            entry[("scores", n_, half)] = len(entry)
                    elif what == "weigh":
                        pe.wait_ge(S["ring_done"], ring0 + (entry[("scores", n_, 1)] + 1))
                        if j == 0 and head == GROUP:
                            pe.wait_ge(S["lifted"], lift0 + 2)
                        m, at = keys_in(j), PLACE * (head % GROUP)
                        for half, (lo, hi) in enumerate(HALVES):
                            mm = pe.matmul(ps[at:at + PLACE, 6 + half, 0:hi - lo], V32[0:m, j, head, :],
                                           probsT_ring(n_)[0:m, lo:hi], start=(j == 0), stop=(j == NT - 1))
                            if j == NT - 1 and head % GROUP == GROUP - 1:
                                mm.then_inc(S["group_ready"], 1)
                    elif what == "divide":
                        pe.wait_ge(S["lifted"], lift0 + 2 * (n_ + 1))
                        first = pair()
                        turns += 1
                        for t in range(NT):
                            mm = pe.transpose(ps[:, first + t // 3, (t % 3) * P:(t % 3 + 1) * P],
                                              tile_of(hid[:, n_, :], t), ident)
                        mm.then_inc(S["peak_ready"], 1)
                n.take("ring_done", len(entry))
                n.take("lifted", 2 * E // GROUP)
                pe.wait_ge(S["peak_done"], n.take("peak_done", turns))

            pe.wait_ge(S["setup_done"], 1)
            with n.loop(pe, "batch", B, S["loop_entered"]):
                pe.wait_ge(S["x_loaded"], n.take("x_loaded", 16))
                tw = C("tok_w")
                tok(NT, lambda t: [(onerow, row(R("tok_b")))] +
                    [(xT[:, t * P + i:(t + 1) * P + i], tw[:, i * P:(i + 1) * P]) for i in range(CONTEXT)], "tok_done_v")

                turn(xn)
                feat([C("expand_q"), C("expand_k"), C("expand_lin"), C("expand_pre")], xT_)
                tok(NT, lambda t: [(tile_of(xT_, t), C("expand_v"))], "tok_done_a", 2 * P)
                pe.wait_ge(S["operand_ready"], n.take("operand_ready"))
                attention(LAYER0, lambda u: QT[0:QK0, 0, u * P:(u + 1) * P], lambda u: KT[0:QK0, 0, :],
                          lambda u, j: V[:, j, :], D)
                turn(att)
                pj = C("project")
                tok(NT, lambda t: [(tile_of(hid[:, 2, :], t), pj[:, 0:P]), (tile_of(attT, t), pj[:, P:2 * P])],
                    "tok_done_v")

                turn(xn)
                feat([C("gfc1")], xT_)
                pe.wait_ge(S["operand_ready"], n.take("operand_ready"))
                pe.matmul(ps[:, 4, 0:8], spread[:, :], C("gfc2"), start=True, stop=True).then_inc(S["tok_ready"], 1)
                pe.wait_ge(S["operand_ready"], n.take("operand_ready"))
                feat([merged[:, f * P:(f + 1) * P] for f in range(FT)], xT_)
                tok(NT, lambda t: [(tile_of(hid[:, f, :], t), merged[:, F + f * P:F + (f + 1) * P]) for f in range(FT)],
                    "tok_done_v")

                turn(xn)
                feat([C("rope_qa"), C("rope_qb"), C("rope_ka"), C("rope_kb")], xT_)
                vrow = row(C("valid"))
                tok(NT + 1, lambda t: [(vrow[:, t * P:(t + 1) * P], row(R("bv1"))), (tile_of(xnT, t), C("v1"))],
                    "tok_done_v")
                pe.wait_ge(S["operand_ready"], n.take("operand_ready"))
                attention(LAYER1, lambda u: tile_of(QT[:, 0, :], u), lambda u: keyT[:, u * P:(u + 2) * P],
                          lambda u, j: V[:, u + j, :], D)
                turn(att)
                tok(NT, lambda t: [(onerow, row(R("bo1"))), (tile_of(attT, t), C("o1"))], "tok_done_v")

                turn(xn)
                feat([C("gate_k")], xT_)
                tok(NT, lambda t: [(tile_of(hid[:, 0, :], t), C("queries"))], "tok_done_v", 8)
                def project(k):
                    w = wts[:, k, :]
                    pe.wait_ge(S[f"wts_loaded{k}"], n.take(f"wts_loaded{k}", 32))
                    feat([w[:, W1_Q:W1_Q + P], w[:, W1_K:W1_K + P]], xT_)
                    tok(NT, lambda t: [(onerow, row(wrow_of(k, R_BV))), (tile_of(xT_, t), w[:, W1_V:W1_V + P])],
                        "tok_done_a")

                def finish(k, more):
                    w = wts[:, k, :]
                    turn(att)
                    tok(NT, lambda t: [(onerow, row(wrow_of(k, R_BO))), (tile_of(attT, t), w[:, W1_O:W1_O + P])],
                        "tok_done_v")
                    if more:
                        project(1 - k)
                    turn(x1)
                    stream(up_down(w, W1_UP, W1_DOWN, FT, attT), 0)
                    back(KT[:, 1, :], n.now("feat_done"))
                    pe.wait_ge(S["tok_done_v"], n.take("tok_done_v", 2))

                project(0)
                expert_attention()
                finish(0, True)
                with n.loop(pe, "l1", E // 2 - 1, S["loop_entered"]):
                    for k in (1, 0):
                        expert_attention()
                        finish(k, True)
                expert_attention()
                finish(1, False)

                turn(xn)
                feat([C("q2"), C("k2")], xT_)
                tok(NT, lambda t: [(tile_of(xT_, t), C("v2"))], "tok_done_v")
                feat([C("hq2")], QT[:, 0, :])
                feat([C("hk2")], KT[:, 0, :])
                pe.wait_ge(S["operand_ready"], n.take("operand_ready"))
                attention(LAYER2, lambda u: tile_of(QT[:, 1, :], u), lambda u: KT[:, 0, :],
                          lambda u, j: V[:, j, :], D)

                turn(xn)
                feat([pool_w[:, :]], xT_)
                pe.wait_ge(S["operand_ready"], n.take("operand_ready"))
                pe.matmul(ps[:, 4, 0:8], spread[:, :], C("gate_w2"), start=True, stop=True).then_inc(S["tok_ready"], 1)
                pe.wait_ge(S["tok_done_v"], n.take("tok_done_v"))
                with n.loop(pe, "l2", E // 2, S["loop_entered"]):
                    for k in range(2):
                        jobs = up_down(wts[:, k, :], W2_UP, W2_DOWN, FT, xT_)
                        pe.wait_ge(S[f"wts_loaded{k}"], n.take(f"wts_loaded{k}", 16))
                        stream(jobs, k * len(jobs))
                pe.wait_ge(S["operand_ready"], n.take("operand_ready"))
                back(KT[:, 0, :], n.now("feat_done"))
                pe.wait_ge(S["tok_done_v"], n.take("tok_done_v", 2))

                turn(xn)
                def third(k, first=False):
                    w = wts[:, k, :]
                    pe.wait_ge(S[f"wts_loaded{k}"], n.take(f"wts_loaded{k}", 16))
                    feat([w[:, W3_Q:W3_Q + P], w[:, W3_K:W3_K + P]], xT_)
                    if not first:
                        pe.wait_ge(S["operand_ready"], n.take("operand_ready"))
                    tok(NT, lambda t: [(tile_of(xT_, t), w[:, W3_V:W3_V + P])], "tok_done_a")

                def third_out(k, waited=True):
                    turn(att, waited)
                    tok(NT, lambda t: [(tile_of(attT, t), wts[:, k, W3_O:W3_O + P])], "tok_done_v")

                def third_attention(k, between=None):
                    attention(LAYER3, lambda u: tile_of(QT[:, k, :], u), lambda u: KT[:, k, :],
                              lambda u, j: (V, x1)[k][:, j, :], D, between)

                third(0, True)
                third_attention(0)
                with n.loop(pe, "l3", E // 2 - 1, S["loop_entered"]):
                    for k in (1, 0):
                        third(k)
                        third_attention(k, lambda: third_out(1 - k))
                third(1)
                third_attention(1, lambda: third_out(0))
                third_out(1, False)

                turn(xn)
                tok(NT, lambda t: [(onerow, row(R("gate_b3"))), (tile_of(xT_, t), C("gate_w3"))], "tok_done_v", 8)
                def fourth(k):
                    jobs = up_down(wts[:, k, :], W4_UP, W4_DOWN, F3 // P, xT_, 2 * k)
                    pe.wait_ge(S[f"wts_loaded{k}"], n.take(f"wts_loaded{k}", 16))
                    stream(jobs, k * len(jobs))

                def fourth_back(k, reads):
                    back((attT[:, :], QT[:, 0, :])[k], reads)
                    pe.wait_ge(S["tok_done_v"], n.take("tok_done_v", 2))

                def fourth_turn(k):
                    before = n.now("feat_done")
                    fourth(k)
                    fourth_back(1 - k, before)

                fourth(0)
                with n.loop(pe, "l4", E // 2 - 1, S["loop_entered"]):
                    for k in (1, 0):
                        fourth_turn(k)
                fourth_turn(1)
                fourth_back(1, n.now("feat_done"))

        @block.scalar
        def _(act):
            n = Tally("scalar", per_turn)

            def turned(dst):
                act.wait_ge(S["turned1"], n.take("turned1"))
                act.activation(dst[:, H0:T], ps[:, 5, 0:T - H0], ACT.Copy).then_inc(S["copied1"], 1)

            def feat(blocks):
                i = 0
                for func, dst, opts in blocks:
                    for half, (lo, hi) in enumerate(HALVES):
                        act.wait_ge(S["feat_ready"], n.take("feat_ready"))
                        more = {"accum_out": half_sum[:, half:half + 1]} if "sums" in opts else {}
                        act.activation(dst[:, lo:hi], ps[0:dst.shape[0], i % 4, 0:hi - lo], func,
                                       bias=opts.get("bias", 0.0), **more).then_inc(S["feat_done"], 1)
                        i += 1

            def stream(start, out, func, bias, plane, final):
                tiles = len(bias) - 1
                jobs = [(half, f) for half in HALVES for f in range(tiles)] + [(half, None) for half in HALVES]
                for i, ((lo, hi), f) in enumerate(jobs):
                    act.wait_ge(S["feat_ready"], n.take("feat_ready"))
                    dst = out if f is None else hid[:, plane + f, :]
                    act.activation(dst[:, lo:hi], ps[:, (start + i) % 4, 0:hi - lo], final if f is None else func,
                                   bias=bias[-1] if f is None else bias[f]).then_inc(S["feat_done"], 1)

            def values(dst):
                for t in range(NT):
                    act.wait_ge(S["tok_ready"], n.take("tok_ready"))
                    act.activation(dst[:, t, :], ps[:, 4 + t % 4, 0:D], ACT.Copy).then_inc(S["tok_done_a"], 1)

            def attention(spec, between=None):
                def tanh_layer(u):
                    for order, g in enumerate(additive_groups()):
                        i = u * (P // 8) + order
                        if i >= 4:
                            act.wait_ge(S["hidden_used"], used + (i - 3))
                        act.activation(tanh_ring(order)[:, 0:T], hid[:, 2, 0:T], ACT.Tanh,
                                       bias=hqb[:, u * (P // 8) + g:u * (P // 8) + g + 1])\
                            .then_inc(S["hidden_ready"], 1)

                def exponentials(u):
                    act.wait_ge(S["max_ready"], n.take("max_ready"))
                    keys = spec.keys(u)
                    src = masked[:, u % 2, 0:keys] if spec.mask else scores_ap(u, keys)
                    dst = probs[:, u % 2, 0:keys] if spec.mask else cut(probs[:, u % 2, 0:keys], keys)
                    act.activation(dst, src, ACT.Exp, bias=neg_top[:, u % 2:u % 2 + 1],
                                   scale=1.0 if spec.mask else spec.scale,
                                   accum_out=total[:, u % 4:u % 4 + 1]).then_inc(S["probs_ready"], 1)

                def copy_half(u):
                    tiles = len(key_tiles(spec.keys(u)))
                    if tiles > 3:
                        act.wait_ge(S["turned1"], n.take("turned1"))
                        act.activation(flat(probsT[:, 3:tiles, :]), ps[:, 5, 0:(tiles - 3) * P], ACT.Copy)\
                            .then_inc(S["copied1"], 1)

                used = n.now("hidden_used")
                if spec.additive:
                    n.take("hidden_used", spec.units * P // 8)
                    act.wait_ge(S["query_part_ready"], n.take("query_part_ready"))
                    tanh_layer(0)
                    tanh_layer(1)
                exponentials(0)
                exponentials(1)
                if between:
                    between()
                for u in range(spec.units):
                    copy_half(u)
                    if u + 2 < spec.units:
                        if spec.additive:
                            tanh_layer(u + 2)
                        exponentials(u + 2)

            def gate_exponentials(tiles):
                act.wait_ge(S["logits_ready"], n.take("logits_ready"))
                act.activation(ex[:, 0:tiles, :], lg2[:, 0:tiles, :], ACT.Exp).then_inc(S["exps_ready"], 1)

            act.wait_ge(S["consts_loaded"], 64)
            act.activation(C("rel"), C("rel"), ACT.Sigmoid, bias=R("mult")).then_inc(S["decay_ready"], 1)
            with n.loop(act, "batch", B, S["loop_entered"]):
                n.take("tok_ready", NT)
                turned(xT_)
                feat([(ACT.Copy, QT[0:QK0, 0, :], {}), (ACT.Copy, KT[0:QK0, 0, :], {}),
                      (ACT.Copy, hid[:, 0, :], {}), (ACT.Gelu, hid[:, 1, :], {})])
                for t in range(NT):
                    act.wait_ge(S["tok_ready"], n.take("tok_ready"))
                    act.activation(y[:, t, :], ps[:, 4 + t % 4, P:2 * P], ACT.Gelu)
                    act.activation(V[:, t, :], ps[:, 4 + t % 4, 0:P], ACT.Copy).then_inc(S["tok_done_a"], 1)
                attention(LAYER0)
                turned(attT)
                n.take("tok_ready", NT)

                turned(xT_)
                feat([(ACT.Relu, hid[:, 0, :], {"bias": C("gfc1_b"), "sums": True})])
                n.take("tok_ready")
                feat([(ACT.Relu, hid[:, f, :], {"bias": merged_b1[:, f:f + 1]}) for f in range(FT)])
                n.take("tok_ready", NT)

                turned(xT_)
                rb = C("rope_bias")
                feat([(ACT.Identity, hid[:, i, :], {"bias": rb[:, i:i + 1]}) for i in range(4)])
                n.take("tok_ready", NT + 1)
                attention(LAYER1)
                turned(attT)
                n.take("tok_ready", NT)

                turned(xT_)
                feat([(ACT.Identity, hid[:, 0, :], {"bias": C("gate_kb")})])
                n.take("tok_ready", NT)
                gate_exponentials(NT)
                def columns(k, at, count):
                    return [wts[:, k, at + i:at + i + 1] for i in range(count)]

                def project(k):
                    bias = columns(k, W1_BIAS, 2)
                    feat([(ACT.Identity, (QT, KT)[i][:, 0, :], {"bias": bias[i]}) for i in range(2)])
                    for t in range(NT):
                        act.wait_ge(S["tok_ready"], n.take("tok_ready"))
                        act.activation(V32[:, t, :, 0:HD], ps[:, 4 + t % 4, 0:D].rearrange("p (h d) -> p h d", h=E),
                                       ACT.Copy).then_inc(S["tok_done_a"], 1)

                def finish(k, more):
                    turned(attT)
                    n.take("tok_ready", NT)
                    if more:
                        project(1 - k)
                    turned(attT)
                    stream(0, KT[:, 1, :], ACT.Gelu, columns(k, W1_BIAS + 2, FT + 1), 0, ACT.Gelu)
                    n.take("tok_ready", 2)

                def expert_attention():
                    i = 0
                    for what, n_ in expert_steps():
                        if what == "lift":
                            for half, (lo, hi) in enumerate(HALVES):
                                act.wait_ge(S["group_ready"], n.take("group_ready"))
                                act.activation(hid[:, n_, lo:hi], ps[:, 6 + half, 0:hi - lo], ACT.Copy)\
                                    .then_inc(S["lifted"], 1)
                        if what not in ("scores", "shift"):
                            continue
                        for lo, hi in HALVES:
                            act.wait_ge(S["ring_ready"], n.take("ring_ready"))
                            if what == "shift":
                                act.activation(q_stack[STACK:STACK + SHIFT, n_, lo:hi],
                                               ps[STACK:STACK + SHIFT, i % 2, 0:hi - lo], ACT.Copy)\
                                    .then_inc(S["ring_done"], 1)
                            else:
                                m = keys_in(n_ % NT)
                                act.activation(probsT_ring(n_)[0:m, lo:hi], ps[0:m, i % 2, 0:hi - lo], ACT.Exp,
                                               scale=float(HD) ** -0.5).then_inc(S["ring_done"], 1)
                            i += 1

                project(0)
                expert_attention()
                finish(0, True)
                with n.loop(act, "l1", E // 2 - 1, S["loop_entered"]):
                    for k in (1, 0):
                        expert_attention()
                        finish(k, True)
                expert_attention()
                finish(1, False)

                turned(xT_)
                feat([(ACT.Copy, QT[:, 0, :], {}), (ACT.Copy, KT[:, 0, :], {})])
                n.take("tok_ready", NT)
                feat([(ACT.Identity, hid[:, 3, :], {"bias": C("b1_2")})])
                feat([(ACT.Copy, hid[:, 2, :], {})])
                attention(LAYER2)

                turned(xT_)
                feat([(ACT.Copy, hid[:, 0, :], {})])
                act.wait_ge(S["logits_ready"], n.take("logits_ready"))
                act.activation(hid[:, 1, 0:T], hid[:, 0, 0:T], ACT.Exp, bias=pooled[:, 1:2],
                               accum_out=half_sum[:, 0:1]).then_inc(S["exps_ready"], 1)
                n.take("tok_ready")
                gate_exponentials(1)
                with n.loop(act, "l2", E // 2, S["loop_entered"]):
                    for k in range(2):
                        stream(k * 2 * (FT + 1), (attT[:, :], QT[:, 0, :])[k], ACT.Gelu,
                               columns(k, W2_BIAS, FT + 1), 0, ACT.Gelu)
                n.take("tok_ready", 2)

                turned(xT_)
                def third(k):
                    feat([(ACT.Copy, QT[:, k, :], {}), (ACT.Copy, KT[:, k, :], {})])
                    values((V, x1)[k])

                def third_out():
                    turned(attT)
                    n.take("tok_ready", NT)

                third(0)
                attention(LAYER3)
                with n.loop(act, "l3", E // 2 - 1, S["loop_entered"]):
                    for k in (1, 0):
                        third(k)
                        attention(LAYER3, third_out)
                third(1)
                attention(LAYER3, third_out)
                third_out()

                turned(xT_)
                n.take("tok_ready", NT)
                gate_exponentials(NT)
                def fourth(k):
                    stream(k * 2 * (F3 // P + 1), (attT[:, :], QT[:, 0, :])[k], ACT.Relu,
                           columns(k, W4_BIAS, F3 // P + 1), 2 * k, ACT.Identity)
                    act.drain().then_inc(S["wts_free"], 1)
                    n.take("tok_ready", 2)

                fourth(0)
                with n.loop(act, "l4", E // 2 - 1, S["loop_entered"]):
                    for k in (1, 0):
                        fourth(k)
                fourth(1)

        @block.vector
        def _(v):
            n = Tally("vector", per_turn)

            def over(ap, tiles, width):
                return ap.unsqueeze(1).to_broadcast([P, tiles, width])

            def ready():
                v.drain().then_inc(S["operand_ready"], 1)

            def norm_parts(src, dst):
                for t in range(NT):
                    v.bn_stats(stats[:, t, :], src[:, t, :])
                    if t % 3 == 2:
                        v.drain()
                        yield
                for t in range(NT):
                    v.bn_aggr(mv[:, t, :], stats[:, t, :])
                    if t % 3 == 2:
                        v.drain()
                        yield
                v.tensor_scalar(var[:, :], mv[:, :, 1], EPS, None, ALU.add).then_inc(S["var_ready"], 1)
                yield
                v.wait_ge(S["rstd_ready"], n.take("rstd_ready"))
                for t in range(NT):
                    v.tensor_scalar(dst[:, t, :], src[:, t, :], mv[:, t, 0:1], rstd[:, t:t + 1],
                                    ALU.subtract, ALU.mult)
                    if t % 3 == 2:
                        v.drain()
                        yield

            def norm(src, dst):
                for _ in norm_parts(src, dst):
                    pass

            def turned(dst):
                v.wait_ge(S["turned0"], n.take("turned0"))
                v.tensor_copy(dst[:, 0:H0], ps[:, 4, 0:H0]).then_inc(S["copied0"], 1)

            def tok(tiles, use, done=True):
                for t in range(tiles):
                    v.wait_ge(S["tok_ready"], n.take("tok_ready"))
                    use(t, ps[:, 4 + t % 4, :]).then_inc(S["tok_done_v"], 1)

            def keep_values(t, product):
                return v.tensor_copy(V[:, t, :], product[:, 0:D])

            def add_to_h(t, product):
                return v.tensor_tensor(h[:, t, :], product[:, 0:D], h[:, t, :], ALU.add)

            def add_back(dst, src):
                for half in range(2):
                    v.wait_ge(S["tok_ready"], n.take("tok_ready"))
                    some = slice(3 * half, 3 * half + 3)
                    v.tensor_tensor(flat(dst[:, some, :]), ps[:, 4 + half, 0:H0], flat(src[:, some, :]), ALU.add)\
                        .then_inc(S["tok_done_v"], 1)

            def attention(spec, dst, between=None):
                def peak(u):
                    v.wait_ge(S["scores_ready"], n.take("scores_ready"))
                    keys, i = spec.keys(u), u % 2
                    if spec.mask:
                        v.scalar_tensor_tensor(cut(masked[:, i, 0:keys], keys), scores_ap(u, keys), spec.scale,
                                               mask_ap(spec, u), ALU.mult, ALU.add)
                        v.drain()
                        v.tensor_reduce(top[:, i:i + 1], masked[:, i, 0:keys], X, ALU.max)
                    else:
                        v.tensor_reduce(top[:, i:i + 1], scores_ap(u, keys), XY if keys > 512 else X, ALU.max)
                    v.drain()
                    if spec.additive:
                        v.tensor_scalar(top[:, i:i + 1], top[:, i:i + 1], R("b2_2"), None, ALU.add)
                        v.drain()
                        v.tensor_tensor(neg_top[:, i:i + 1], R("b2_2"), top[:, i:i + 1], ALU.subtract)\
                            .then_inc(S["max_ready"], 1)
                    else:
                        v.tensor_scalar(neg_top[:, i:i + 1], top[:, i:i + 1], -1.0 if spec.mask else -spec.scale,
                                        None, ALU.mult).then_inc(S["max_ready"], 1)

                def copy_half(u):
                    tiles = min(3, len(key_tiles(spec.keys(u))))
                    v.wait_ge(S["turned0"], n.take("turned0"))
                    v.tensor_copy(flat(probsT[:, 0:tiles, :]), ps[:, 4, 0:tiles * P]).then_inc(S["copied0"], 1)

                def divide(u):
                    v.reciprocal(rtotal[:, u % 2:u % 2 + 1], total[:, u % 4:u % 4 + 1])
                    v.drain()
                    v.wait_ge(S["heads_ready"], n.take("heads_ready"))
                    out = dst(u)
                    v.tensor_scalar(out, ps[:, 6 + u % 2, 0:out.shape[1]], rtotal[:, u % 2:u % 2 + 1], None, ALU.mult)

                peak(0)
                peak(1)
                if between:
                    between()
                for u in range(spec.units):
                    copy_half(u)
                    if u + 2 < spec.units:
                        peak(u + 2)
                    divide(u)
                v.drain()

            def gating(tiles, over_all):
                def wide(ap):
                    return ap.unsqueeze(2).to_broadcast([P, tiles, 8])

                L, L2, EX, PK, CD, M = lg[:, 0:tiles, :], lg2[:, 0:tiles, :], ex[:, 0:tiles, :], pick[:, 0:tiles, :], \
                    cand[:, 0:tiles, :], m1[:, 0:tiles]
                rank = over(C("rank8"), tiles, 8)

                def step(ins):
                    v.drain()
                    return ins

                def first_of_largest(src, picked):
                    step(v.tensor_reduce(M, src, X, ALU.max))
                    step(v.tensor_tensor(CD, src, wide(M), ALU.is_equal))
                    step(v.tensor_tensor(CD, CD, rank, ALU.mult))
                    step(v.tensor_reduce(M, CD, X, ALU.max))
                    step(v.tensor_tensor(picked, CD, wide(M), ALU.is_equal))

                def over_sum(dst, src, values, tiny):
                    step(v.tensor_reduce(M, values, X, ALU.add))
                    step(v.tensor_scalar(M, M, tiny, None, ALU.add))
                    step(v.reciprocal(M, M))
                    step(v.tensor_tensor(dst, src, wide(M), ALU.mult))

                step(v.tensor_reduce(M, L, X, ALU.max))
                step(v.tensor_tensor(L2, L, wide(M), ALU.subtract).then_inc(S["logits_ready"], 1))
                first_of_largest(L, PK)
                v.wait_ge(S["exps_ready"], n.take("exps_ready"))
                step(v.scalar_tensor_tensor(L2, PK, FAR, L, ALU.mult, ALU.add))
                if over_all:
                    over_sum(EX, EX, EX, 0.0)
                step(v.tensor_reduce(M, L2, X, ALU.max))
                step(v.tensor_tensor(CD, L2, wide(M), ALU.is_equal))
                step(v.tensor_tensor(CD, CD, rank, ALU.mult))
                step(v.tensor_reduce(M, CD, X, ALU.max))
                step(v.tensor_tensor(CD, CD, wide(M), ALU.is_equal))
                step(v.tensor_tensor(PK, PK, CD, ALU.add))
                step(v.tensor_tensor(EX, EX, PK, ALU.mult))
                over_sum(gates[:, :, 0:tiles].rearrange("p e t -> p t e"), EX, EX, 1e-9 if over_all else 0.0)

            def gate_column(e, tiles):
                v.tensor_copy(gcol[:, 0:tiles], gates[:, e, 0:tiles])
                v.drain()

            for buf in (xT, xnT, attT, add_w):
                v.memset(buf[:, :], 0.0)
            v.memset(peaks[:, :, :], 0.0)
            v.memset(V32[:, :, :, HD:PLACE], 0.0)
            v.drain()
            v.memset(V32[:, :, :, HD:HD + 1], 1.0)
            v.memset(k_stack[STACK:STACK + SHIFT, :, :], -1.0)
            for buf in (QT, KT, probs, masked):
                v.memset(buf[:, :, :], 0.0)
            v.drain()
            v.wait_ge(S["consts_loaded"], 64)
            v.tensor_copy(identb[:, :], ident)
            v.tensor_copy(maskb[:, 0:2 * P], C("band"))
            v.tensor_copy(maskb[:, 2 * P:3 * P], C("causal")[:, (NT - 1) * P:NT * P])
            v.tensor_scalar(add_w[:, 32:40], C("onehot8"), C("w2_2"), None, ALU.mult)
            v.tensor_scalar(pool_w[:, :], ones, C("pool_w"), None, ALU.mult)
            for out, base, at in ((lng, R("ln_g"), 0), (lnb, R("ln_b"), E * P)):
                tasks = flat(hid)[:, at:at + E * P]
                for e in range(E):
                    dst = out[:, :] if e == 0 else spread[:, :]
                    v.tensor_tensor(dst, tasks[:, e * P:(e + 1) * P], base, ALU.subtract)
                    v.drain()
                    if e:
                        v.tensor_tensor(out[:, :], out[:, :], spread[:, :], ALU.add)
                        v.drain()
                v.scalar_tensor_tensor(out[:, :], out[:, :], MERGE, base, ALU.mult, ALU.add)
            v.drain()
            v.memset(hid[:, :, :], 0.0)
            v.wait_ge(S["decay_ready"], 1)
            v.tensor_tensor(C("rel"), C("rel"), C("causal"), ALU.add)
            v.drain().then_inc(S["setup_done"], 1)
            v.sem_inc(S["x_free"], 1)
            v.sem_inc(S["wts_free"], 2)

            with n.loop(v, "batch", B, S["loop_entered"]):
                v.wait_ge(S["h_free"], n.take("h_free"))
                tok(NT, lambda t, product: v.tensor_scalar(h[:, t, :], product[:, 0:D], 0.0, None, ALU.max))
                v.drain().then_inc(S["x_free"], 1)

                norm(h, x1)
                norm(x1, xn)
                ready()
                turned(xT_)
                v.wait_ge(S["feat_done"], n.take("feat_done", 8))
                v.tensor_tensor(hid[:, 2, 0:T], hid[:, 0, 0:T], hid[:, 1, 0:T], ALU.mult)
                n.take("tok_ready", NT)
                v.wait_ge(S["tok_done_a"], n.take("tok_done_a", NT))
                v.tensor_tensor(V[:, 0:NT, :], V[:, 0:NT, :], y[:, :, :], ALU.mult)
                ready()
                attention(LAYER0, lambda u: att[:, u, :])
                ready()
                turned(attT)
                tok(NT, lambda t, product: v.tensor_tensor(x1[:, t, :], product[:, 0:D], x1[:, t, :], ALU.add))
                v.drain()
                v.tensor_tensor(flat(h), flat(h), flat(x1), ALU.add)
                v.drain()

                norm(h, xn)
                ready()
                turned(xT_)
                v.wait_ge(S["feat_done"], n.take("feat_done", 2))
                v.tensor_tensor(pooled[:, 0:1], half_sum[:, 0:1], half_sum[:, 1:2], ALU.add)
                v.drain()
                v.tensor_scalar(spread[:, :], ones, pooled[:, 0:1], 1.0 / T, ALU.mult, ALU.mult)
                ready()
                v.wait_ge(S["tok_ready"], n.take("tok_ready"))
                v.tensor_tensor(g8[:, :], ps[:, 4, 0:8], R("gfc2_b"), ALU.add)
                v.drain()
                for dst, base, tasks in ((merged, C("w1w2"), None), (merged_b1, C("b1"), C("tv_b1")),
                                         (merged_b2, R("b2"), R("tv_b2"))):
                    width = base.shape[1]
                    for e in range(E):
                        task = tv[:, e, :] if tasks is None else tasks[:, e * width:(e + 1) * width]
                        v.scalar_tensor_tensor(dst[:, :], task, g8[:, e:e + 1], base if e == 0 else dst[:, :],
                                               ALU.mult, ALU.add)
                        v.drain()
                ready()
                n.take("feat_done", 8)
                tok(NT, lambda t, product: v.tensor_tensor(y[:, t, :], product[:, 0:D], xn[:, t, :], ALU.add))
                v.drain()
                v.tensor_tensor(y[:, :, :], y[:, :, :], over(merged_b2[:, :], NT, D), ALU.add)
                v.drain()
                norm(y, y)
                v.tensor_tensor(y[:, :, :], y[:, :, :], over(lng[:, :], NT, D), ALU.mult)
                v.drain()
                v.tensor_tensor(y[:, :, :], y[:, :, :], over(lnb[:, :], NT, D), ALU.add)
                v.drain()
                v.tensor_tensor(flat(h), flat(h), flat(y), ALU.add)
                v.drain()

                norm(h, xn)
                ready()
                turned(xT_)
                v.wait_ge(S["feat_done"], n.take("feat_done", 8))
                v.memset(keyT[:, 0:PAD], 0.0)
                v.memset(keyT[:, PAD + T:TPAD], 0.0)
                for i, dst in ((0, QT[:, 0, 0:T]), (2, keyT[:, PAD:PAD + T])):
                    v.tensor_tensor(masked[:, 0, 0:T], hid[:, i, 0:T], C("rope_cos"), ALU.mult)
                    v.tensor_tensor(masked[:, 1, 0:T], hid[:, i + 1, 0:T], C("rope_sin"), ALU.mult)
                    v.drain()
                    v.tensor_tensor(dst, masked[:, 0, 0:T], masked[:, 1, 0:T], ALU.add)
                    v.drain()
                tok(NT + 1, keep_values)
                ready()
                attention(LAYER1, lambda u: att[:, u, :])
                ready()
                turned(attT)
                tok(NT, add_to_h)
                v.drain()

                norm(h, xn)
                ready()
                turned(xT_)
                n.take("feat_done", 2)
                tok(NT, lambda t, product: v.tensor_scalar(lg[:, t, :], product[:, 0:8], float(D) ** -0.5, None,
                                                           ALU.mult))
                v.drain()
                gating(NT, True)
                def project():
                    v.wait_ge(S["feat_done"], n.take("feat_done", 4))
                    for i, src in ((0, QT), (1, KT)):
                        v.tensor_copy(parts[:, i, 0, 0:T], src[:, 0, 0:T])
                    v.drain()
                    for i, src in ((0, QT), (1, KT)):
                        v.tensor_tensor(src[:, 0, 0:T], src[:, 0, 0:T], parts[:, i, 0, 0:T], ALU.subtract)
                    v.drain()
                    for i, src in ((0, QT), (1, KT)):
                        v.tensor_copy(parts[:, i, 1, 0:T], src[:, 0, 0:T])
                    v.drain()
                    for i, src in ((0, QT), (1, KT)):
                        v.tensor_tensor(parts[:, i, 2, 0:T], src[:, 0, 0:T], parts[:, i, 1, 0:T], ALU.subtract)
                    v.drain().then_inc(S["parts_ready"], 1)
                    n.take("tok_ready", NT)
                    n.take("tok_done_a", NT)

                def expert_attention(rest=()):
                    turns, rest = 0, iter(rest)
                    for what, n_ in expert_steps():
                        head, j, first = n_ // NT, n_ % NT, 2 + 2 * (turns % 2)
                        if what in ("peak", "divide"):
                            v.wait_ge(S["peak_ready"], n.take("peak_ready"))
                            turns += 1
                        if what == "peak":
                            m = keys_in(j)
                            v.tensor_reduce(peaks[0:m, head % 2, j:j + 1], ps[0:m, first:first + 2, 0:T // 2], XY,
                                            ALU.max).then_inc(S["peak_done"], 1)
                            if j == NT - 1:
                                v.drain()
                                v.tensor_copy(peaks2[:, head % 2, :, 0], peaks[:, head % 2, :])
                                v.drain()
                                v.tensor_tensor(peaks2[:, head % 2, :, 1], peaks[:, head % 2, :],
                                                peaks2[:, head % 2, :, 0], ALU.subtract).then_inc(S["shift_split"], 1)
                            next(rest, None)
                        elif what == "divide":
                            sums = ps[:, first:first + 2, 0:3 * P].rearrange("p a (c w) -> p a c w", w=PLACE)
                            v.tensor_scalar(rsum[:, :, :], sums[:, :, :, HD], 1e-30, None, ALU.max)
                            v.drain()
                            v.reciprocal(rsum[:, :, :], rsum[:, :, :])
                            v.drain()
                            for a in range(2):
                                last = v.tensor_tensor(
                                    att[:, 3 * a:3 * a + 3, n_ * D // 2:(n_ + 1) * D // 2]
                                    .rearrange("p t (g d) -> p t g d", d=HD),
                                    sums[:, a, :, 0:HD].rearrange("p (t g) d -> p t g d", g=GROUP),
                                    rsum[:, a, :].rearrange("p (t g) -> p t g", g=GROUP).unsqueeze(3)
                                    .to_broadcast([P, 3, GROUP, HD]), ALU.mult)
                            last.then_inc(S["peak_done"], 1)
                    v.drain()

                def finish(k, more):
                    def rows_over(r):
                        return over(wrow_of(k, r), NT, D)
                    ready()
                    turned(attT)
                    tok(NT, lambda t, product: v.tensor_tensor(y[:, t, :], product[:, 0:D], xn[:, t, :], ALU.add))
                    v.drain()
                    norm(y, x1)
                    v.tensor_tensor(x1[:, :, :], x1[:, :, :], rows_over(R_G1), ALU.mult)
                    v.drain()
                    v.tensor_tensor(x1[:, :, :], x1[:, :, :], rows_over(R_BE1), ALU.add)
                    ready()
                    turned(attT)
                    if more:
                        project()
                    n.take("feat_done", 2 * (FT + 1))
                    add_back(y, x1)
                    v.drain()

                def second_norm(e, k):
                    yield from norm_parts(y, y)
                    for some in (slice(0, 3), slice(3, NT)):
                        v.tensor_tensor(y[:, some, :], y[:, some, :], over(wrow_of(k, R_G2), 3, D), ALU.mult)
                        yield
                    gate_column(e, NT)
                    for some in (slice(0, 3), slice(3, NT)):
                        v.tensor_tensor(y[:, some, :], y[:, some, :], over(wrow_of(k, R_BE2), 3, D), ALU.add)
                        v.drain()
                        yield
                    for t in range(NT):
                        last = v.scalar_tensor_tensor(h[:, t, :], y[:, t, :], gcol[:, t:t + 1], h[:, t, :],
                                                      ALU.mult, ALU.add)
                        if t % 2 and t < NT - 1:
                            yield
                    v.drain().then_inc(S["wts_free"], 1)

                project()
                expert_attention()
                finish(0, True)
                with n.loop(v, "l1", E // 2 - 1, S["loop_entered"]) as pair:
                    for k in (1, 0):
                        expert_attention(second_norm(pair * 2 + (1 - k), 1 - k))
                        finish(k, True)
                expert_attention(second_norm(E - 2, 0))
                finish(1, False)
                for _ in second_norm(E - 1, 1):
                    pass

                norm(h, xn)
                ready()
                turned(xT_)
                n.take("feat_done", 4)
                tok(NT, keep_values)
                v.wait_ge(S["feat_done"], n.take("feat_done", 4))
                v.tensor_scalar(QT[:, 1, 0:T], QT[:, 0, 0:T], float(D) ** -0.5, None, ALU.mult)
                pairs = flat(y).rearrange("p (g j) -> p g j", j=8)
                v.tensor_tensor(pairs, hid[:, 3, :].rearrange("p (g j) -> p g j", j=8),
                                over(C("onehot8"), TP // 8, 8), ALU.mult)
                v.drain()
                v.tensor_reduce(hqb[:, :], pairs, X, ALU.add).then_inc(S["query_part_ready"], 1)
                ready()
                attention(LAYER2, lambda u: att[:, u, :])
                v.tensor_tensor(flat(h), flat(h), flat(att), ALU.add)
                v.drain()

                norm(h, xn)
                ready()
                turned(xT_)
                v.wait_ge(S["feat_done"], n.take("feat_done", 2))
                v.tensor_reduce(pooled[:, 0:1], hid[:, 0, 0:T], X, ALU.max)
                v.drain()
                v.tensor_scalar(pooled[:, 0:1], pooled[:, 0:1], R("pool_b"), None, ALU.add)
                v.drain()
                v.tensor_tensor(pooled[:, 1:2], R("pool_b"), pooled[:, 0:1], ALU.subtract)\
                    .then_inc(S["logits_ready"], 1)
                v.wait_ge(S["exps_ready"], n.take("exps_ready"))
                v.tensor_tensor(hid[:, 2, 0:T], hid[:, 1, 0:T], xT_[:, 0:T], ALU.mult)
                v.reciprocal(rtotal[:, 0:1], half_sum[:, 0:1])
                v.drain()
                v.tensor_reduce(pooled[:, 2:3], hid[:, 2, 0:T], X, ALU.add)
                v.drain()
                v.tensor_scalar(pooled[:, 3:4], pooled[:, 2:3], rtotal[:, 0:1], None, ALU.mult)
                v.drain()
                v.tensor_scalar(spread[:, :], ones, pooled[:, 3:4], None, ALU.mult)
                ready()
                tok(1, lambda t, product: v.tensor_tensor(lg[:, 0, :], product[:, 0:8], R("gate_b2"), ALU.add))
                v.drain()
                v.memset(KT[:, 0, 0:T], 0.0)
                gating(1, True)
                with n.loop(v, "l2", E // 2, S["loop_entered"]) as pair:
                    for k in range(2):
                        gate_column(pair * 2 + k, 1)
                        v.wait_ge(S["feat_done"], n.take("feat_done", 2 * (FT + 1)))
                        v.scalar_tensor_tensor(KT[:, 0, 0:T], (attT[:, 0:T], QT[:, 0, 0:T])[k], gcol[:, 0:1],
                                               KT[:, 0, 0:T], ALU.mult, ALU.add)
                        v.drain().then_inc(S["wts_free"], 1)
                ready()
                add_back(h, h)
                v.drain()

                norm(h, xn)
                ready()
                turned(xT_)
                def third():
                    n.take("feat_done", 4)
                    n.take("tok_ready", NT)
                    n.take("tok_done_a", NT)

                def third_out():
                    turned(attT)
                    tok(NT, add_to_h)
                    v.drain().then_inc(S["wts_free"], 1)

                def third_attention(between=None):
                    attention(LAYER3, lambda u: att[:, u, :], between)
                    ready()

                third()
                third_attention()
                with n.loop(v, "l3", E // 2 - 1, S["loop_entered"]):
                    for _ in (1, 0):
                        third()
                        third_attention(third_out)
                third()
                third_attention(third_out)
                third_out()

                norm(h, xn)
                ready()
                turned(xT_)
                tok(NT, lambda t, product: v.tensor_copy(lg[:, t, :], product[:, 0:8]))
                v.drain()
                gating(NT, False)
                n.take("feat_done", 2 * (F3 // P + 1) * E)

                def fourth_back(e):
                    gate_column(e, NT)
                    for half in range(2):
                        v.wait_ge(S["tok_ready"], n.take("tok_ready"))
                        for i in range(3):
                            t = 3 * half + i
                            last = v.scalar_tensor_tensor(h[:, t, :], ps[:, 4 + half, i * P:(i + 1) * P],
                                                          gcol[:, t:t + 1], h[:, t, :], ALU.mult, ALU.add)
                        last.then_inc(S["tok_done_v"], 1)
                    v.drain()

                with n.loop(v, "l4", E // 2 - 1, S["loop_entered"]) as pair:
                    for k in range(2):
                        fourth_back(pair * 2 + k)
                fourth_back(E - 2)
                fourth_back(E - 1)
                v.drain().then_inc(S["h_final"], 1)


def _layout(a):
    import numpy as np

    f32 = np.float32

    def down(w, tiles):
        return w.T.reshape(tiles, P, -1).transpose(1, 0, 2).reshape(P, -1)

    def columns(b, tiles):
        return b.reshape(tiles, P).T

    x_off = np.arange(TP)[None, :] - (NT - 1) * P - np.arange(P)[:, None]
    win = np.arange(2 * P)[None, :] - np.arange(P)[:, None]
    inv = (f32(1.0) / f32(10000.0) ** (np.arange(0, D, 2, dtype=f32) / f32(D))).astype(f32)
    freqs = np.arange(T, dtype=f32)[:, None] * inv[None, :]
    emb = np.concatenate([np.sin(freqs), np.cos(freqs)], -1).astype(f32)
    sin, cos = emb[:, ::2].T, emb[:, 1::2].T
    even_odd = np.r_[0:D:2, 1:D:2]
    odd_even = np.r_[1:D:2, 0:D:2]
    valid = np.zeros((P, TPAD), f32)
    valid[:, PAD:PAD + T] = 1.0
    exp = a["L0_attn_expand"]
    lin0, pre0 = 2 * QK0, 2 * QK0 + 2 * D
    const = {
        "ident": np.eye(P, dtype=f32), "ones": np.ones((P, P), f32),
        "onehot8": (np.arange(P)[:, None] // 16 == np.arange(8)[None, :]).astype(f32),
        "rank8": np.broadcast_to(np.arange(8, 0, -1).astype(f32), (P, 8)),
        "tok_w": a["L0_tok_weight"].T.reshape(CONTEXT, P, P).transpose(1, 0, 2).reshape(P, -1),
        "expand_q": exp[:, 0:QK0], "expand_k": exp[:, QK0:2 * QK0],
        "expand_lin": exp[:, lin0:lin0 + D], "expand_pre": exp[:, pre0:pre0 + D],
        "expand_v": np.concatenate([exp[:, lin0 + D:pre0], exp[:, pre0 + D:]], 1),
        "project": a["L0_attn_project"].reshape(2, P, D).transpose(1, 0, 2).reshape(P, -1),
        "rel": x_off.astype(f32), "causal": np.where(x_off <= 0, 0.0, FAR).astype(f32), "valid": valid,
        "gfc1": a["L0_ffn_gfc1_w"].T, "gfc1_b": a["L0_ffn_gfc1_b"][:, None], "gfc2": a["L0_ffn_gfc2_w"].T,
        "w1w2": np.concatenate([a["L0_ffn_W1"].T, down(a["L0_ffn_W2"], FT)], 1),
        "b1": columns(a["L0_ffn_b1"], FT),
        "tv_b1": np.concatenate([columns(b, FT) for b in a["L0_ffn_tv_b1"]], 1),
        "rope_qa": a["L1_attn_Wq"][even_odd].T, "rope_qb": a["L1_attn_Wq"][odd_even].T,
        "rope_ka": a["L1_attn_Wk"][even_odd].T, "rope_kb": a["L1_attn_Wk"][odd_even].T,
        "rope_bias": np.stack([a["L1_attn_bq"][even_odd], a["L1_attn_bq"][odd_even],
                               a["L1_attn_bk"][even_odd], a["L1_attn_bk"][odd_even]], 1),
        "rope_cos": np.concatenate([cos, cos]), "rope_sin": np.concatenate([-sin, sin]),
        "v1": a["L1_attn_Wv"].T, "o1": a["L1_attn_Wo"].T,
        "band": np.where((win >= 0) & (win < WINDOW), 0.0, FAR).astype(f32),
        "gate_k": a["L1_ffn_gate_Wk"].T, "gate_kb": a["L1_ffn_gate_bk"][:, None],
        "queries": a["L1_ffn_expert_queries"].T,
        "q2": a["L2_attn_Wq"].T, "k2": a["L2_attn_Wk"].T, "v2": a["L2_attn_Wv"].T,
        "hq2": np.tile(a["L2_attn_W1"][:, :D].T, (1, 8)), "hk2": np.tile(a["L2_attn_W1"][:, D:].T, (1, 8)),
        "b1_2": np.tile(a["L2_attn_b1"], 8)[:, None], "w2_2": np.tile(a["L2_attn_W2"][0], 8)[:, None],
        "pool_w": a["L2_ffn_attn_w"], "gate_w2": a["L2_ffn_gate_w"], "gate_w3": a["L3_ffn_gate_w"],
    }
    rows = {
        "tok_b": a["L0_tok_bias"], "mult": a["L0_attn_position_bias_mult"].reshape(1), "gfc2_b": a["L0_ffn_gfc2_b"],
        "b2": a["L0_ffn_b2"], "tv_b2": a["L0_ffn_tv_b2"].reshape(-1), "ln_g": a["L0_ffn_ln_g"],
        "ln_b": a["L0_ffn_ln_b"], "bv1": a["L1_attn_bv"], "bo1": a["L1_attn_bo"],
        "b2_2": a["L2_attn_b2"], "pool_b": a["L2_ffn_attn_b"], "gate_b2": a["L2_ffn_gate_b"],
        "gate_b3": a["L3_ffn_gate_b"],
    }
    def places_first(w):
        return w.reshape((E, HD) + w.shape[1:]).swapaxes(0, 1).reshape(w.shape)

    l1, l1r = [], []
    for e in range(E):
        wq, wk, wv = a["L1_ffn_Wqkv"][e].reshape(3, D, D)
        bq, bk, bv = a["L1_ffn_bqkv"][e].reshape(3, D)
        l1.append(np.concatenate([places_first(wq).T, places_first(wk).T, wv.T,
                                  a["L1_ffn_Wo"][e].T, a["L1_ffn_W1"][e].T, down(a["L1_ffn_W2"][e], FT),
                                  places_first(bq)[:, None], places_first(bk)[:, None], columns(a["L1_ffn_bf1"][e], FT), a["L1_ffn_bf2"][e][:, None]], 1))
        l1r.append(np.concatenate([bv, a["L1_ffn_bo"][e], a["L1_ffn_g1"][e], a["L1_ffn_be1"][e],
                                   a["L1_ffn_g2"][e], a["L1_ffn_be2"][e]]))
    out = {
        "const": np.concatenate([const[name].reshape(P, width) for name, width in CONST], 1),
        "rows": np.concatenate([rows[name].reshape(width) for name, width in ROWS])[None],
        "tv": np.stack([np.concatenate([a["L0_ffn_tv_W1"][e].T, down(a["L0_ffn_tv_W2"][e], FT)], 1)
                        for e in range(E)], 1),
        "merge_rows": np.concatenate([a["L0_ffn_tv_ln_g"].reshape(-1), a["L0_ffn_tv_ln_b"].reshape(-1)])[None],
        "xT": a["x"].transpose(0, 2, 1),
        "l1": np.stack(l1), "l1_rows": np.stack(l1r),
        "l2": np.stack([np.concatenate([a["L2_ffn_w1"][e], down(a["L2_ffn_w2"][e].T, FT),
                                        columns(a["L2_ffn_b1"][e], FT), a["L2_ffn_b2"][e][:, None]], 1) for e in range(E)]),
        "l3": np.stack([np.concatenate([a[f"L3_attn_W{c}"][e * D:(e + 1) * D].T for c in "qkv"] +
                                       [a["L3_attn_Wo"][:, e * D:(e + 1) * D].T], 1) for e in range(E)]),
        "l4": np.stack([np.concatenate([a["L3_ffn_w1"][e], down(a["L3_ffn_w2"][e].T, F3 // P),
                                        columns(a["L3_ffn_b1"][e], F3 // P), a["L3_ffn_b2"][e][:, None]], 1) for e in range(E)]),
    }
    return {name: np.ascontiguousarray(value, dtype=f32) for name, value in out.items()}


def kernel(**inputs):
    import numpy as np
    import concourse.bacc as bacc
    from concourse.bass_utils import run_bass_kernel_spmd as run

    arrays = _layout({name: np.asarray(value) for name, value in inputs.items()})
    per_turn = {}
    for _ in range(2):
        nc = bacc.Bacc("TRN2", target_bir_lowering=False, num_devices=1)
        tensors = {name: nc.dram_tensor("in_" + name, value.shape, F32, kind="ExternalInput").ap()
                   for name, value in arrays.items()}
        tensors["out"] = nc.dram_tensor("out", (B, T, D), F32, kind="ExternalOutput").ap()
        audio_tower(nc, tensors, per_turn)
    r = run(nc, [{"in_" + name: value for name, value in arrays.items()}], core_ids=[0])
    return r.results[0]["out"]
```

```python
from contextlib import ExitStack, contextmanager

import concourse.bass as bass
from concourse import mybir

F32 = mybir.dt.float32
BF16 = mybir.dt.bfloat16
ALU = mybir.AluOpType
ACT = mybir.ActivationFunctionType
X = mybir.AxisListType.X
XY = mybir.AxisListType.XY

B, T_IN, D = 4, 750, 128
CONTEXT = 3
T = T_IN - CONTEXT + 1
P = 128
NT = (T + P - 1) // P
TP = NT * P
H0 = 3 * P
HALVES = ((0, H0), (H0, T))
E = 8
QK0 = 16
HD = D // E
F = 512
FT = F // P
F3 = 256
WINDOW = 128
PAD = WINDOW // 2
TPAD = TP + 2 * PAD
EPS = 1e-5
MERGE = 0.03
FAR = -1.0e30

W1_Q, W1_K, W1_V, W1_O, W1_UP, W1_DOWN = 0, 128, 256, 384, 512, 1024
W1_BIAS = 1536
W1_NORM = W1_BIAS + 7
W1_END = W1_NORM + 2
R_BV, R_BO, R_G1, R_BE1, R_G2, R_BE2 = range(6)
W2_UP, W2_DOWN, W2_BIAS, W2_END = 0, 512, 1024, 1029
W3_Q, W3_K, W3_V, W3_O, W3_END = 0, 128, 256, 384, 512
W4_UP, W4_DOWN, W4_BIAS, W4_END = 0, 256, 512, 515

CONST = [
    ("ident", P), ("ones", P), ("onehot8", 8), ("rank8", 8),
    ("tok_w", 3 * P), ("expand_q", QK0), ("expand_k", QK0), ("expand_lin", P), ("expand_pre", P),
    ("expand_v", 2 * P), ("project", 2 * P), ("rel", TP), ("causal", TP), ("valid", TPAD),
    ("gfc1", P), ("gfc1_b", 1), ("gfc2", 8), ("w1w2", 2 * F), ("b1", FT), ("tv_b1", E * FT),
    ("rope_qa", P), ("rope_qb", P), ("rope_ka", P), ("rope_kb", P), ("rope_bias", 4),
    ("rope_cos", T), ("rope_sin", T), ("v1", P), ("o1", P), ("band", 2 * P),
    ("gate_k", P), ("gate_kb", 1), ("queries", 8),
    ("q2", P), ("k2", P), ("v2", P), ("hq2", P), ("hk2", P), ("b1_2", 1), ("w2_2", 1),
    ("pool_w", 1), ("gate_w2", 8), ("gate_w3", 8),
]
ROWS = [
    ("tok_b", P), ("mult", 1), ("gfc2_b", 8), ("b2", P), ("tv_b2", E * P), ("ln_g", P),
    ("ln_b", P), ("bv1", P), ("bo1", P), ("b2_2", 1), ("pool_b", 1), ("gate_b2", 8), ("gate_b3", 8),
]


def offsets(parts):
    at, out = 0, {}
    for name, width in parts:
        out[name] = (at, width)
        at += width
    return out, at


CONST_AT, CONST_END = offsets(CONST)
ROWS_AT, ROWS_END = offsets(ROWS)

SEMAPHORES = [
    "loop_entered", "consts_loaded", "tasks_loaded", "decay_ready", "setup_done", "x_loaded", "x_free",
    "h_free", "h_final", "h_stored", "wts_free", "wts_loaded0", "wts_loaded1",
    "operand_ready",
    "feat_ready", "feat_done",
    "tok_ready", "tok_done_v", "tok_done_a",
    "turned0", "turned1", "copied0", "copied1",
    "var_ready", "rstd_ready",
    "scores_ready", "max_ready", "probs_ready", "heads_ready",
    "hidden_ready", "hidden_used",
    "rounded_ready", "parts_ready", "stacks_loaded",
    "peak_ready", "peak_done",
    "shift_split",
    "ring_ready", "ring_done",
    "group_ready",
    "lifted",
    "query_part_ready",
    "logits_ready", "exps_ready",
]


class Tally:

    def __init__(self, engine, per_turn):
        self.engine, self.per_turn, self.n, self.loops = engine, per_turn, {}, []

    def now(self, name):
        value = self.n.get(name, 0)
        for register, loop in self.loops:
            per = self.per_turn.get((self.engine, loop, name), 0)
            if per:
                value = register * per + value
        return value

    def take(self, name, count=1):
        self.n[name] = self.n.get(name, 0) + count
        return self.now(name)

    @contextmanager
    def loop(self, eng, name, turns, entered):
        before = dict(self.n)
        eng.sem_inc(entered, 1)
        with eng.Fori(0, turns) as i:
            self.loops.append((i, name))
            yield i
            self.loops.pop()
        for key, n in list(self.n.items()):
            per = n - before.get(key, 0)
            self.per_turn[(self.engine, name, key)] = per
            self.n[key] = before.get(key, 0) + turns * per


def key_tiles(n):
    return list(range((n + P - 1) // P))


class Attention:

    def __init__(self, units, keys, scale, mask=None, product_mask=None, additive=False):
        self.units, self.keys, self.scale, self.mask = units, keys, scale, mask
        self.product_mask, self.additive = product_mask, additive


def causal_keys(tile):
    return min((tile + 1) * P, T)


LAYER0 = Attention(NT, lambda u: causal_keys(u % NT), 0.25, "rel")
LAYER1 = Attention(NT, lambda u: 2 * P, float(D) ** -0.5, product_mask="band")
LAYER2 = Attention(NT, lambda u: T, 1.0, additive=True)
LAYER3 = Attention(NT, lambda u: causal_keys(u % NT), float(D) ** -0.5, product_mask="diagonal")


Q_PARTS, K_PARTS = (0, 0, 1, 0, 1, 2), (0, 1, 0, 2, 1, 0)
STACK = len(Q_PARTS) * HD
SHIFT = 2
PT_RING = 4
PLACE = 32
GROUP = P // PLACE


def expert_steps():
    units, lag, group = E * NT, 2, GROUP * NT
    peaks = [("peak", m) for m in range(units)] + [("shift", E - 1)]
    for h in range(E - 1):
        peaks.insert(peaks.index(("peak", (h + 1) * NT)) + 1, ("shift", h))
    peaks = iter(peaks)

    def ahead(count):
        for _ in range(count):
            for what, m in peaks:
                yield what, m
                if what == "peak":
                    break

    yield "before", 0
    yield from ahead(2)
    yield "before", 1
    yield from ahead(4)
    yield "before", 2
    yield from ahead(NT - 3)
    for n in range(units + lag):
        if n < units:
            yield "scores", n
        yield from ahead(1)
        if lag <= n % group < lag + NT or n > units - NT:
            yield "rest", n
        if n >= lag:
            yield "weigh", n - lag
            if (n - lag) % group == 1 and n - lag > 1:
                yield "divide", n // group - 1
            if (n - lag) % group == group - 1:
                yield "lift", (n - lag) // group
    yield "divide", E // GROUP - 1


def ring_banks():
    steps = [what for what, _ in expert_steps()]
    last_peak = max(i for i, what in enumerate(steps) if what == "peak")
    entry_of, out = {}, []
    for i, what in enumerate(steps):
        for _ in range(2 if what in ("scores", "shift") else 0):
            banks = range(2 if i < last_peak else 6)
            bank = min(banks, key=lambda x: (entry_of.get(x, -1), -x))
            out.append((bank, entry_of.get(bank)))
            entry_of[bank] = len(out) - 1
    return out


def additive_groups():
    return [4 * (i % 4) + i // 4 for i in range(P // 8)]


def cut(ap, n):
    return ap if n <= 512 else ap.rearrange("p (a n) -> p a n", a=2)


def audio_tower(nc, A, per_turn):
    with ExitStack() as ctx:
        def sb(name, shape, dt=F32):
            return ctx.enter_context(nc.sbuf_tensor(name, shape, dt))

        S = {name: ctx.enter_context(nc.semaphore(name)) for name in SEMAPHORES}
        ps = ctx.enter_context(nc.psum_tensor("ps", [P, 8, 512], F32))

        const = sb("const", [P, CONST_END])
        rows = sb("rows", [P, ROWS_END])
        tv = sb("tv", [P, E, 2 * F])
        wts = sb("wts", [P, 2, W1_END])
        wrow = sb("wrow", [P, 2, 6 * P])
        xT = sb("xT", [P, TP + CONTEXT - 1])
        h = sb("h", [P, NT, D])
        xn = sb("xn", [P, NT, D])
        x1 = sb("x1", [P, NT, D])
        y = sb("y", [P, NT, D])
        att = sb("att", [P, NT, D])
        xnT = sb("xnT", [P, TPAD])
        attT = sb("attT", [P, TP])
        QT = sb("QT", [P, 2, TP])
        KT = sb("KT", [P, 2, TP])
        V = sb("V", [P, NT + 1, D])
        hid = sb("hid", [P, FT, TP])
        masked = sb("masked", [P, 2, TP])
        probs = sb("probs", [P, 2, TP])
        probsT = sb("probsT", [P, 6, P])
        merged = sb("merged", [P, 2 * F])
        merged_b1 = sb("merged_b1", [P, FT])
        merged_b2 = sb("merged_b2", [P, P])
        stats = sb("stats", [P, NT, 6])
        mv = sb("mv", [P, NT, 2])
        var = sb("var", [P, NT])
        rstd = sb("rstd", [P, NT])
        minus_half = sb("minus_half", [P, NT])
        top = sb("top", [P, 2])
        neg_top = sb("neg_top", [P, 2])
        total = sb("total", [P, 4])
        rtotal = sb("rtotal", [P, 2])
        half_sum = sb("half_sum", [P, 2])
        pooled = sb("pooled", [P, 4])
        spread = sb("spread", [P, P])
        g8 = sb("g8", [P, 8])
        exp_of_one = sb("exp_of_one", [P, 1])
        parts = sb("parts", [P, 2, 3, TP], BF16)
        q_stack = sb("q_stack", [P, E, TP], BF16)
        k_stack = sb("k_stack", [STACK + SHIFT, E, TP], BF16)
        maskb = sb("maskb", [P, 3 * P], BF16)
        identb = sb("identb", [P, P], BF16)
        V32 = sb("V32", [P, NT, E, PLACE])
        peaks = sb("peaks", [P, 2, NT])
        peaks2 = sb("peaks2", [P, 2, NT, SHIFT], BF16)
        rsum = sb("rsum", [P, 2, 3 * GROUP])
        add_w = sb("add_w", [P, 64])
        hqb = sb("hqb", [P, TP // 8])
        lng = sb("lng", [P, P])
        lnb = sb("lnb", [P, P])
        pool_w = sb("pool_w", [P, P])
        lg = sb("lg", [P, NT, 8])
        lg2 = sb("lg2", [P, NT, 8])
        ex = sb("ex", [P, NT, 8])
        pick = sb("pick", [P, NT, 8])
        cand = sb("cand", [P, NT, 8])
        m1 = sb("m1", [P, NT])
        gates = sb("gates", [P, 8, NT])
        gcol = sb("gcol", [P, NT])

        keyT = q_stack[:, :, :].rearrange("p e t -> p (e t)").bitcast(F32)[:, 0:TPAD]

        def C(name):
            at, width = CONST_AT[name]
            return const[:, at:at + width]

        def R(name):
            at, width = ROWS_AT[name]
            return rows[:, at:at + width]

        ident, ones = C("ident"), C("ones")
        xT_ = xnT[:, PAD:PAD + TP]
        onerow = const[0:1, CONST_AT["ones"][0]:CONST_AT["ones"][0] + P]

        def row(ap):
            return ap[0:1]

        def tile_of(ap, t):
            return ap[:, t * P:(t + 1) * P]

        def flat(ap):
            return ap[:, :, :].rearrange("p t d -> p (t d)")

        def wrow_of(k, r):
            return wrow[:, k, r * P:(r + 1) * P]

        def scores_ap(u, n):
            return ps[:, 2 * (u % 2), 0:n] if n <= 512 else ps[:, 2 * (u % 2):2 * (u % 2) + 2, 0:n // 2]

        def probsT_ring(n):
            return (probs, masked)[n % PT_RING // 2][:, n % 2, :]

        def keys_in(j):
            return min(P, T - j * P)

        def tanh_ring(i):
            return hid[:, i % 4, :] if i % 4 < 2 else masked[:, i % 4 - 2, :]

        def mask_ap(spec, u):
            n = spec.keys(u)
            at = CONST_AT[spec.mask][0] + (NT - 1 - u % NT) * P
            return cut(const[:, at:at + n], n)

        block = ctx.enter_context(nc.Block())

        @block.sync
        def _(sp):
            n = Tally("sync", per_turn)
            sp.dma_start(const[:, :], A["const"]).then_inc(S["consts_loaded"], 16)
            sp.dma_start(rows[:, :], A["rows"].broadcast_to([P, ROWS_END])).then_inc(S["consts_loaded"], 16)
            sp.dma_start(flat(hid)[:, 0:2 * E * P], A["merge_rows"].broadcast_to([P, 2 * E * P]))\
                .then_inc(S["consts_loaded"], 16)
            sp.dma_start(tv[:, :, :], A["tv"]).then_inc(S["tasks_loaded"], 16)
            sp.sem_inc(S["h_free"], 1)

            def load(src, srow, at, k):
                sp.wait_ge(S["wts_free"], n.take("wts_free"))
                sp.dma_start(wts[:, k, 0:src.shape[2]], src[at, :, :]).then_inc(S[f"wts_loaded{k}"], 16)
                if srow is not None:
                    sp.dma_start(wrow[:, k, 0:srow.shape[1]], srow[at, :].partition_broadcast(P))\
                        .then_inc(S[f"wts_loaded{k}"], 16)

            def stacks():
                for part in range(3):
                    ready = "parts_ready" if part else "rounded_ready"
                    sp.wait_ge(S[ready], n.take(ready))
                    for i, (stack, order) in enumerate(((q_stack, Q_PARTS), (k_stack, K_PARTS))):
                        for g in range(len(order)):
                            if order[g] == part:
                                sp.dma_start(stack[g * HD:(g + 1) * HD, :, 0:T], parts[:, i, part, 0:T])\
                                    .then_inc(S["stacks_loaded"], 16)

            with n.loop(sp, "batch", B, S["loop_entered"]) as b:
                sp.wait_ge(S["x_free"], n.take("x_free"))
                sp.dma_start(xT[:, 0:T_IN], A["xT"][b, :, :]).then_inc(S["x_loaded"], 16)
                load(A["l1"], A["l1_rows"], 0, 0)
                load(A["l1"], A["l1_rows"], 1, 1)
                stacks()
                with n.loop(sp, "l1", E // 2 - 1, S["loop_entered"]) as pair:
                    for k in range(2):
                        stacks()
                        load(A["l1"], A["l1_rows"], pair * 2 + (k + 2), k)
                stacks()
                for stage, src, srow in (("l2", A["l2"], None),
                                         ("l3", A["l3"], None), ("l4", A["l4"], None)):
                    with n.loop(sp, stage, E // 2, S["loop_entered"]) as pair:
                        for k in range(2):
                            load(src, srow, pair * 2 + k, k)
                sp.wait_ge(S["h_final"], n.take("h_final"))
                full = (NT - 1) * P
                sp.dma_start(A["out"][b, 0:full, :].rearrange("(t p) d -> p t d", p=P), h[:, 0:NT - 1, :])\
                    .then_inc(S["h_stored"], 16)
                sp.dma_start(A["out"][b, full:T, :], h[0:T - full, NT - 1, :]).then_inc(S["h_stored"], 16)
                sp.wait_ge(S["h_stored"], n.take("h_stored", 32))
                sp.sem_inc(S["h_free"], 1)

        @block.gpsimd
        def _(pool):
            n = Tally("pool", per_turn)
            pool.memset(minus_half[:, :], -0.5)
            pool.drain()

            def power(times):
                for _ in range(times):
                    pool.wait_ge(S["var_ready"], n.take("var_ready"))
                    pool.tensor_tensor(rstd[:, :], var[:, :], minus_half[:, :], ALU.pow).then_inc(S["rstd_ready"], 1)

            with n.loop(pool, "batch", B, S["loop_entered"]):
                power(6)
                with n.loop(pool, "l1", E // 2 - 1, S["loop_entered"]):
                    power(4)
                power(4 + 4)

        @block.tensor
        def _(pe):
            n = Tally("tensor", per_turn)

            def turn(src, waited=False):
                if not waited:
                    pe.wait_ge(S["operand_ready"], n.take("operand_ready"))
                for half in range(2):
                    for t in range(3):
                        mm = pe.transpose(ps[:, 4 + half, t * P:(t + 1) * P], src[:, 3 * half + t, :], ident)
                    mm.then_inc(S[f"turned{half}"], 1)
                for half in range(2):
                    pe.wait_ge(S[f"copied{half}"], n.take(f"copied{half}"))

            def feat(blocks, rhs, wait=True):
                base = n.now("feat_done")
                i = 0
                for w in blocks:
                    m = w.shape[1]
                    for lo, hi in HALVES:
                        if i >= 4:
                            pe.wait_ge(S["feat_done"], base + (i - 3))
                        pe.matmul(ps[0:m, i % 4, 0:hi - lo], w, rhs[:, lo:hi], start=True, stop=True)\
                            .then_inc(S["feat_ready"], 1)
                        i += 1
                n.take("feat_done", i)
                if wait:
                    pe.wait_ge(S["feat_done"], n.now("feat_done"))

            def stream(jobs, start, first=0):
                base = n.now("feat_done") - first
                for i, (reads, terms, (lo, hi)) in enumerate(jobs, first):
                    pe.wait_ge(S["feat_done"], base + (max(reads, i - 3) if reads else i - 3))
                    for c, (w, rhs) in enumerate(terms):
                        mm = pe.matmul(ps[:, (start + i) % 4, 0:hi - lo], w, rhs[:, lo:hi],
                                       start=(c == 0), stop=(c == len(terms) - 1))
                    mm.then_inc(S["feat_ready"], 1)
                n.take("feat_done", len(jobs))

            def up_down(w, up, down, tiles, rhs, plane=0):
                ups = [(0, [(w[:, up + f * P:up + (f + 1) * P], rhs)], half) for half in HALVES for f in range(tiles)]
                downs = [(tiles * (i + 1), [(w[:, down + f * P:down + (f + 1) * P], hid[:, plane + f, :])
                                            for f in range(tiles)], half) for i, half in enumerate(HALVES)]
                return ups + downs

            def back(src, reads, bank=4):
                pe.wait_ge(S["feat_done"], reads)
                for half in range(2):
                    for t in range(3):
                        mm = pe.transpose(ps[:, bank + half, t * P:(t + 1) * P], tile_of(src, 3 * half + t), ident)
                    mm.then_inc(S["tok_ready"], 1)

            def tok(tiles, products, done, width=D):
                base = n.now(done)
                for t in range(tiles):
                    if t >= 4:
                        pe.wait_ge(S[done], base + (t - 3))
                    terms = products(t)
                    for i, (lhs, rhs) in enumerate(terms):
                        mm = pe.matmul(ps[:, 4 + t % 4, 0:width], lhs, rhs, start=(i == 0), stop=(i == len(terms) - 1))
                    mm.then_inc(S["tok_ready"], 1)
                pe.wait_ge(S[done], n.take(done, tiles))

            def attention(spec, query, key, value, dv, between=None, ahead=None):
                def scores(u):
                    keys = spec.keys(u)
                    width = keys if keys <= 512 else keys // 2
                    parts = range(keys // width)
                    masked_by = {"band": maskb[:, 0:2 * P], "diagonal": maskb[:, 2 * P:3 * P]}.get(spec.product_mask)
                    for a in parts:
                        mm = pe.matmul(ps[:, 2 * (u % 2) + a, 0:width], query(u), key(u)[:, a * width:(a + 1) * width],
                                       start=True, stop=not (spec.additive or masked_by is not None),
                                       skip_group_check=True)
                    if masked_by is not None:
                        left = min(masked_by.shape[1], keys - u * P if spec.product_mask == "diagonal" else keys)
                        for a in parts:
                            lo, hi = max(a * width, keys - left), (a + 1) * width
                            if lo < hi:
                                at = lo - (keys - left)
                                mm = pe.matmul(ps[:, 2 * (u % 2) + a, lo - a * width:width], identb[:, :],
                                               masked_by[:, at:at + hi - lo], start=False, stop=True,
                                               skip_group_check=True)
                    for i, g in enumerate(additive_groups() if spec.additive else ()):
                        pe.wait_ge(S["hidden_ready"], n.take("hidden_ready"))
                        at = 32 * (g // 4)
                        for a in parts:
                            last = pe.matmul(ps[at:at + 32, 2 * (u % 2) + a, 0:width],
                                             add_w[:, 32 - 8 * (g % 4):64 - 8 * (g % 4)],
                                             tanh_ring(i)[:, a * width:(a + 1) * width], start=False,
                                             stop=(i >= P // 8 - 4), skip_group_check=True)
                        last.then_inc(S["hidden_used"], 1)
                    if spec.additive:
                        pe.drain().then_inc(S["scores_ready"], 1)
                    else:
                        mm.then_inc(S["scores_ready"], 1)

                def spread_out(u):
                    pe.wait_ge(S["probs_ready"], n.take("probs_ready"))
                    tiles = key_tiles(spec.keys(u))
                    for half in range(2):
                        for j in tiles[3 * half:3 * half + 3]:
                            mm = pe.transpose(ps[:, 4 + half, (j % 3) * P:(j % 3 + 1) * P],
                                              probs[:, u % 2, j * P:(j + 1) * P], ident)
                        if tiles[3 * half:]:
                            mm.then_inc(S[f"turned{half}"], 1)

                def weigh(u):
                    tiles = key_tiles(spec.keys(u))
                    for j in tiles:
                        if j % 3 == 0:
                            pe.wait_ge(S[f"copied{j // 3}"], n.take(f"copied{j // 3}"))
                        mm = pe.matmul(ps[:, 6 + u % 2, 0:dv], probsT[:, j, :], value(u, j),
                                       start=(j == 0), stop=(j == len(tiles) - 1))
                    mm.then_inc(S["heads_ready"], 1)

                scores(0)
                scores(1)
                if between:
                    between()
                for u in range(spec.units):
                    spread_out(u)
                    if u + 2 < spec.units:
                        scores(u + 2)
                    elif u + 1 == spec.units and ahead:
                        ahead()
                    weigh(u)

            def expert_attention(before=None):
                ring = ring_banks()
                ring0, peak0, lift0 = n.now("ring_done"), n.now("peak_done"), n.now("lifted")
                entry = {}
                turns = 0
                def bank():
                    at, last = ring[len(entry)]
                    if last is not None:
                        pe.wait_ge(S["ring_done"], ring0 + (last + 1))
                    elif at >= 2:
                        pe.wait_ge(S["peak_done"], peak0 + (turns - (at // 2 - 1 != (turns - 1) % 2)))
                    return ps[:, at, :]

                def pair():
                    if turns >= 2:
                        pe.wait_ge(S["peak_done"], peak0 + (turns - 1))
                    return 2 + 2 * (turns % 2)

                for what, n_ in expert_steps():
                    head, j = n_ // NT, n_ % NT
                    if what == "before" and before:
                        before(n_)
                    elif what == "peak":
                        if n_ == 0:
                            pe.wait_ge(S["stacks_loaded"], n.take("stacks_loaded", 2 * len(Q_PARTS) * 16))
                        first, m = pair(), keys_in(j)
                        turns += 1
                        for a in range(2):
                            mm = pe.matmul(ps[0:m, first + a, 0:T // 2], q_stack[0:STACK, head, j * P:j * P + m],
                                           k_stack[0:STACK, head, a * T // 2:(a + 1) * T // 2], start=True, stop=True)
                        mm.then_inc(S["peak_ready"], 1)
                    elif what == "shift":
                        pe.wait_ge(S["shift_split"], n.take("shift_split"))
                        for half in range(2):
                            out = bank()
                            for t in range(3):
                                mm = pe.matmul(out[STACK:STACK + SHIFT, t * P:(t + 1) * P],
                                               peaks2[:, n_ % 2, 3 * half + t, :], identb[:, :], start=True, stop=True)
                            mm.then_inc(S["ring_ready"], 1)
                            entry[("shift", n_, half)] = len(entry)
                    elif what == "scores":
                        if j == 0:
                            pe.wait_ge(S["ring_done"], ring0 + (entry[("shift", head, 1)] + 1))
                        m = keys_in(j)
                        for half, (lo, hi) in enumerate(HALVES):
                            out = bank()
                            pe.matmul(out[0:m, 0:hi - lo], k_stack[:, head, j * P:j * P + m], q_stack[0:STACK + SHIFT, head, lo:hi],
                                      start=True, stop=True).then_inc(S["ring_ready"], 1)
                            entry[("scores", n_, half)] = len(entry)
                    elif what == "weigh":
                        pe.wait_ge(S["ring_done"], ring0 + (entry[("scores", n_, 1)] + 1))
                        if n_ == 0 and before:
                            pe.wait_ge(S["tok_done_v"], n.take("tok_done_v", 2))
                        if j == 0 and head == GROUP:
                            pe.wait_ge(S["lifted"], lift0 + 2)
                        m, at = keys_in(j), PLACE * (head % GROUP)
                        for half, (lo, hi) in enumerate(HALVES):
                            mm = pe.matmul(ps[at:at + PLACE, 6 + half, 0:hi - lo], V32[0:m, j, head, :],
                                           probsT_ring(n_)[0:m, lo:hi], start=(j == 0), stop=(j == NT - 1))
                            if j == NT - 1 and head % GROUP == GROUP - 1:
                                mm.then_inc(S["group_ready"], 1)
                    elif what == "divide":
                        first = pair()
                        turns += 1
                        for t in range(NT):
                            if t % 3 == 0:
                                pe.wait_ge(S["lifted"], lift0 + 2 * n_ + t // 3 + 1)
                            mm = pe.transpose(ps[:, first + t // 3, (t % 3) * P:(t % 3 + 1) * P],
                                              tile_of(hid[:, n_, :], t), ident)
                        mm.then_inc(S["peak_ready"], 1)
                n.take("ring_done", len(entry))
                n.take("lifted", 2 * E // GROUP)
                pe.wait_ge(S["peak_done"], n.take("peak_done", turns))

            pe.wait_ge(S["setup_done"], 1)
            with n.loop(pe, "batch", B, S["loop_entered"]):
                pe.wait_ge(S["x_loaded"], n.take("x_loaded", 16))
                tw = C("tok_w")
                tok(NT, lambda t: [(onerow, row(R("tok_b")))] +
                    [(xT[:, t * P + i:(t + 1) * P + i], tw[:, i * P:(i + 1) * P]) for i in range(CONTEXT)], "tok_done_v")

                turn(xn)
                feat([C("expand_q"), C("expand_k"), C("expand_lin"), C("expand_pre")], xT_, False)
                tok(NT, lambda t: [(tile_of(xT_, t), C("expand_v"))], "tok_done_a", 2 * P)
                pe.wait_ge(S["feat_done"], n.now("feat_done"))
                pe.wait_ge(S["operand_ready"], n.take("operand_ready"))
                attention(LAYER0, lambda u: QT[0:QK0, 0, u * P:(u + 1) * P], lambda u: KT[0:QK0, 0, :],
                          lambda u, j: V[:, j, :], D)
                turn(att)
                pj = C("project")
                tok(NT, lambda t: [(tile_of(hid[:, 2, :], t), pj[:, 0:P]), (tile_of(attT, t), pj[:, P:2 * P])],
                    "tok_done_v")

                turn(xn)
                feat([C("gfc1")], xT_)
                pe.wait_ge(S["operand_ready"], n.take("operand_ready"))
                pe.matmul(ps[:, 4, 0:8], spread[:, :], C("gfc2"), start=True, stop=True).then_inc(S["tok_ready"], 1)
                pe.wait_ge(S["operand_ready"], n.take("operand_ready"))
                feat([merged[:, f * P:(f + 1) * P] for f in range(FT)], xT_)
                pe.wait_ge(S["operand_ready"], n.take("operand_ready"))
                tok(NT, lambda t: [(tile_of(hid[:, f, :], t), merged[:, F + f * P:F + (f + 1) * P]) for f in range(FT)],
                    "tok_done_v")

                turn(xn)
                feat([C("rope_qa"), C("rope_qb"), C("rope_ka"), C("rope_kb")], xT_, False)
                vrow = row(C("valid"))
                tok(NT + 1, lambda t: [(vrow[:, t * P:(t + 1) * P], row(R("bv1"))), (tile_of(xnT, t), C("v1"))],
                    "tok_done_v")
                pe.wait_ge(S["feat_done"], n.now("feat_done"))
                pe.wait_ge(S["operand_ready"], n.take("operand_ready"))
                attention(LAYER1, lambda u: tile_of(QT[:, 0, :], u), lambda u: keyT[:, u * P:(u + 2) * P],
                          lambda u, j: V[:, u + j, :], D)
                turn(att)
                tok(NT, lambda t: [(tile_of(attT, t), C("o1"))], "tok_done_v")

                turn(xn)
                feat([C("gate_k")], xT_)
                tok(NT, lambda t: [(tile_of(hid[:, 0, :], t), C("queries"))], "tok_done_v", 8)
                def project(k):
                    w = wts[:, k, :]
                    pe.wait_ge(S[f"wts_loaded{k}"], n.take(f"wts_loaded{k}", 32))
                    feat([w[:, W1_Q:W1_Q + P], w[:, W1_K:W1_K + P]], xT_, False)
                    tok(NT, lambda t: [(onerow, row(wrow_of(k, R_BV))), (tile_of(xT_, t), w[:, W1_V:W1_V + P])],
                        "tok_done_a")

                def finish(k, more):
                    w = wts[:, k, :]
                    turn(att)
                    tok(NT, lambda t: [(tile_of(attT, t), w[:, W1_O:W1_O + P])], "tok_done_v")
                    if more:
                        project(1 - k)
                    turn(x1)
                    stream(up_down(w, W1_UP, W1_DOWN, FT, attT)[0:2 * FT], 0)

                def ending(k):
                    def step(i):
                        if i < 2:
                            job = 2 * FT + i
                            stream(up_down(wts[:, k, :], W1_UP, W1_DOWN, FT, attT)[job:job + 1], 0, job)
                            pe.wait_ge(S["feat_done"], n.now("feat_done") - 1 - i)
                        else:
                            back(KT[:, 1, :], n.now("feat_done"), 6)
                    return step

                project(0)
                expert_attention()
                finish(0, True)
                with n.loop(pe, "l1", E // 2 - 1, S["loop_entered"]):
                    for k in (1, 0):
                        expert_attention(ending(1 - k))
                        finish(k, True)
                expert_attention(ending(0))
                finish(1, False)
                for i in range(3):
                    ending(1)(i)
                pe.wait_ge(S["tok_done_v"], n.take("tok_done_v", 2))

                turn(xn)
                feat([C("q2"), C("k2")], xT_, False)
                tok(NT, lambda t: [(tile_of(xT_, t), C("v2"))], "tok_done_v")
                pe.wait_ge(S["feat_done"], n.now("feat_done"))
                feat([C("hq2")], QT[:, 0, :])
                feat([C("hk2")], KT[:, 0, :])
                pe.wait_ge(S["operand_ready"], n.take("operand_ready"))
                attention(LAYER2, lambda u: tile_of(QT[:, 1, :], u), lambda u: KT[:, 0, :],
                          lambda u, j: V[:, j, :], D)

                turn(xn)
                feat([pool_w[:, :]], xT_)
                pe.wait_ge(S["operand_ready"], n.take("operand_ready"))
                pe.matmul(ps[:, 4, 0:8], spread[:, :], C("gate_w2"), start=True, stop=True).then_inc(S["tok_ready"], 1)
                pe.wait_ge(S["tok_done_v"], n.take("tok_done_v"))
                with n.loop(pe, "l2", E // 2, S["loop_entered"]):
                    for k in range(2):
                        jobs = up_down(wts[:, k, :], W2_UP, W2_DOWN, FT, xT_)
                        pe.wait_ge(S[f"wts_loaded{k}"], n.take(f"wts_loaded{k}", 16))
                        stream(jobs, k * len(jobs))
                pe.wait_ge(S["operand_ready"], n.take("operand_ready"))
                back(KT[:, 0, :], n.now("feat_done"))
                pe.wait_ge(S["tok_done_v"], n.take("tok_done_v", 2))

                turn(xn)
                def third(k):
                    w = wts[:, k, :]
                    pe.wait_ge(S[f"wts_loaded{k}"], n.take(f"wts_loaded{k}", 16))
                    feat([w[:, W3_Q:W3_Q + P], w[:, W3_K:W3_K + P]], xT_, False)

                def third_values(k, first=False):
                    if not first:
                        pe.wait_ge(S["operand_ready"], n.take("operand_ready"))
                    tok(NT, lambda t: [(tile_of(xT_, t), wts[:, k, W3_V:W3_V + P])], "tok_done_a")

                def third_out(k, waited=True):
                    turn(att, waited)
                    tok(NT, lambda t: [(tile_of(attT, t), wts[:, k, W3_O:W3_O + P])], "tok_done_v")

                def third_attention(k, first=False, last=False):
                    def between():
                        third_values(k, first)
                        if not first:
                            third_out(1 - k)

                    pe.wait_ge(S["feat_done"], n.now("feat_done"))
                    attention(LAYER3, lambda u: tile_of(QT[:, k, :], u), lambda u: KT[:, k, :],
                              lambda u, j: (V, x1)[k][:, j, :], D, between, None if last else lambda: third(1 - k))

                third(0)
                third_attention(0, first=True)
                with n.loop(pe, "l3", E // 2 - 1, S["loop_entered"]):
                    for k in (1, 0):
                        third_attention(k)
                third_attention(1, last=True)
                third_out(1, False)

                turn(xn)
                tok(NT, lambda t: [(onerow, row(R("gate_b3"))), (tile_of(xT_, t), C("gate_w3"))], "tok_done_v", 8)
                def fourth(k):
                    jobs = up_down(wts[:, k, :], W4_UP, W4_DOWN, F3 // P, xT_, 2 * k)
                    pe.wait_ge(S[f"wts_loaded{k}"], n.take(f"wts_loaded{k}", 16))
                    stream(jobs, k * len(jobs))

                def fourth_back(k, reads):
                    pe.wait_ge(S["tok_done_v"], n.now("tok_done_v"))
                    back((attT[:, :], QT[:, 0, :])[k], reads)
                    n.take("tok_done_v", 2)

                def fourth_turn(k):
                    before = n.now("feat_done")
                    fourth(k)
                    fourth_back(1 - k, before)

                fourth(0)
                with n.loop(pe, "l4", E // 2 - 1, S["loop_entered"]):
                    for k in (1, 0):
                        fourth_turn(k)
                fourth_turn(1)
                fourth_back(1, n.now("feat_done"))
                pe.wait_ge(S["tok_done_v"], n.now("tok_done_v"))

        @block.scalar
        def _(act):
            n = Tally("scalar", per_turn)

            def turned(dst, k=None):
                act.wait_ge(S["turned1"], n.take("turned1"))
                if k is not None:
                    w = wts[:, k, W1_NORM:W1_NORM + 2]
                    act.activation(dst[:, H0:T], ps[:, 5, 0:T - H0], ACT.Identity, scale=w[:, 0:1], bias=w[:, 1:2])\
                        .then_inc(S["copied1"], 1)
                    return
                act.activation(dst[:, H0:T], ps[:, 5, 0:T - H0], ACT.Copy).then_inc(S["copied1"], 1)

            def feat(blocks):
                i = 0
                for func, dst, opts in blocks:
                    for half, (lo, hi) in enumerate(HALVES):
                        act.wait_ge(S["feat_ready"], n.take("feat_ready"))
                        more = {"accum_out": half_sum[:, half:half + 1]} if "sums" in opts else {}
                        for out in [dst] + opts.get("also", []):
                            last = act.activation(out[:, lo:hi], ps[0:dst.shape[0], i % 4, 0:hi - lo], func,
                                                  bias=opts.get("bias", 0.0), **more)
                        last.then_inc(S["feat_done"], 1)
                        i += 1

            def stream(start, out, func, bias, plane, final):
                tiles = len(bias) - 1
                jobs = [(half, f) for half in HALVES for f in range(tiles)] + [(half, None) for half in HALVES]
                for i, ((lo, hi), f) in enumerate(jobs):
                    act.wait_ge(S["feat_ready"], n.take("feat_ready"))
                    dst = out if f is None else hid[:, plane + f, :]
                    act.activation(dst[:, lo:hi], ps[:, (start + i) % 4, 0:hi - lo], final if f is None else func,
                                   bias=bias[-1] if f is None else bias[f]).then_inc(S["feat_done"], 1)

            def load_exp():
                act.activation(exp_of_one[:, :], ones[:, 0:1], ACT.Exp)
                act.drain()

            def values(dst):
                for t in range(NT):
                    act.wait_ge(S["tok_ready"], n.take("tok_ready"))
                    act.activation(dst[:, t, :], ps[:, 4 + t % 4, 0:D], ACT.Copy).then_inc(S["tok_done_a"], 1)

            def attention(spec, between=None, ahead=None):
                def tanh_layer(u):
                    for order, g in enumerate(additive_groups()):
                        i = u * (P // 8) + order
                        if i >= 4:
                            act.wait_ge(S["hidden_used"], used + (i - 3))
                        act.activation(tanh_ring(order)[:, 0:T], hid[:, 2, 0:T], ACT.Tanh,
                                       bias=hqb[:, u * (P // 8) + g:u * (P // 8) + g + 1])\
                            .then_inc(S["hidden_ready"], 1)

                def exponentials(u):
                    act.wait_ge(S["max_ready"], n.take("max_ready"))
                    keys = spec.keys(u)
                    src = masked[:, u % 2, 0:keys] if spec.mask else scores_ap(u, keys)
                    dst = probs[:, u % 2, 0:keys] if spec.mask else cut(probs[:, u % 2, 0:keys], keys)
                    act.activation(dst, src, ACT.Exp, bias=neg_top[:, u % 2:u % 2 + 1],
                                   scale=1.0 if spec.mask else spec.scale,
                                   accum_out=total[:, u % 4:u % 4 + 1]).then_inc(S["probs_ready"], 1)

                def copy_half(u):
                    tiles = len(key_tiles(spec.keys(u)))
                    if tiles > 3:
                        act.wait_ge(S["turned1"], n.take("turned1"))
                        act.activation(flat(probsT[:, 3:tiles, :]), ps[:, 5, 0:(tiles - 3) * P], ACT.Copy)\
                            .then_inc(S["copied1"], 1)

                used = n.now("hidden_used")
                if spec.additive:
                    n.take("hidden_used", spec.units * P // 8)
                    act.wait_ge(S["query_part_ready"], n.take("query_part_ready"))
                    tanh_layer(0)
                    tanh_layer(1)
                exponentials(0)
                exponentials(1)
                if between:
                    between()
                for u in range(spec.units):
                    copy_half(u)
                    if u + 2 < spec.units:
                        if spec.additive:
                            tanh_layer(u + 2)
                        exponentials(u + 2)
                    elif u + 1 == spec.units and ahead:
                        ahead()

            def gate_exponentials(tiles):
                act.wait_ge(S["logits_ready"], n.take("logits_ready"))
                act.activation(ex[:, 0:tiles, :], lg2[:, 0:tiles, :], ACT.Exp).then_inc(S["exps_ready"], 1)

            act.wait_ge(S["consts_loaded"], 48)
            act.activation(C("rel"), C("rel"), ACT.Sigmoid, bias=R("mult")).then_inc(S["decay_ready"], 1)
            with n.loop(act, "batch", B, S["loop_entered"]):
                n.take("tok_ready", NT)
                turned(xT_)
                feat([(ACT.Copy, QT[0:QK0, 0, :], {}), (ACT.Copy, KT[0:QK0, 0, :], {}),
                      (ACT.Copy, hid[:, 0, :], {}), (ACT.Gelu, hid[:, 1, :], {})])
                for t in range(NT):
                    act.wait_ge(S["tok_ready"], n.take("tok_ready"))
                    act.activation(y[:, t, :], ps[:, 4 + t % 4, P:2 * P], ACT.Gelu)
                    act.activation(V[:, t, :], ps[:, 4 + t % 4, 0:P], ACT.Copy).then_inc(S["tok_done_a"], 1)
                attention(LAYER0)
                turned(attT)
                n.take("tok_ready", NT)

                turned(xT_)
                feat([(ACT.Relu, hid[:, 0, :], {"bias": C("gfc1_b"), "sums": True})])
                n.take("tok_ready")
                feat([(ACT.Relu, hid[:, f, :], {"bias": merged_b1[:, f:f + 1]}) for f in range(FT)])
                n.take("tok_ready", NT)

                turned(xT_)
                rb = C("rope_bias")
                feat([(ACT.Identity, hid[:, i, :], {"bias": rb[:, i:i + 1]}) for i in range(4)])
                n.take("tok_ready", NT + 1)
                attention(LAYER1)
                turned(attT)
                n.take("tok_ready", NT)

                turned(xT_)
                feat([(ACT.Identity, hid[:, 0, :], {"bias": C("gate_kb")})])
                n.take("tok_ready", NT)
                gate_exponentials(NT)
                def columns(k, at, count):
                    return [wts[:, k, at + i:at + i + 1] for i in range(count)]

                def project(k):
                    bias = columns(k, W1_BIAS, 2)
                    feat([(ACT.Identity, (QT, KT)[i][:, 0, :], {"bias": bias[i], "also": [parts[:, i, 0, :]]})
                          for i in range(2)])
                    act.drain().then_inc(S["rounded_ready"], 1)
                    for t in range(NT):
                        act.wait_ge(S["tok_ready"], n.take("tok_ready"))
                        act.activation(V32[:, t, :, 0:HD], ps[:, 4 + t % 4, 0:D].rearrange("p (h d) -> p h d", h=E),
                                       ACT.Copy).then_inc(S["tok_done_a"], 1)

                def finish(k, more):
                    turned(attT)
                    n.take("tok_ready", NT)
                    if more:
                        project(1 - k)
                    turned(attT, k)
                    stream(0, KT[:, 1, :], ACT.Gelu, columns(k, W1_BIAS + 2, FT + 1), 0, ACT.Gelu)
                    if more:
                        load_exp()
                    n.take("tok_ready", 2)

                def expert_attention():
                    i, ring = 0, ring_banks()
                    for what, n_ in expert_steps():
                        if what == "lift":
                            for half, (lo, hi) in enumerate(HALVES):
                                act.wait_ge(S["group_ready"], n.take("group_ready"))
                                act.activation(hid[:, n_, lo:hi], ps[:, 6 + half, 0:hi - lo], ACT.Copy)\
                                    .then_inc(S["lifted"], 1)
                        if what not in ("scores", "shift"):
                            continue
                        for lo, hi in HALVES:
                            act.wait_ge(S["ring_ready"], n.take("ring_ready"))
                            if what == "shift":
                                act.activation(q_stack[STACK:STACK + SHIFT, n_, lo:hi],
                                               ps[STACK:STACK + SHIFT, ring[i][0], 0:hi - lo], ACT.Copy)\
                                    .then_inc(S["ring_done"], 1)
                            else:
                                m = keys_in(n_ % NT)
                                act.activation(probsT_ring(n_)[0:m, lo:hi], ps[0:m, ring[i][0], 0:hi - lo], ACT.Exp,
                                               scale=float(HD) ** -0.5).then_inc(S["ring_done"], 1)
                            i += 1

                project(0)
                expert_attention()
                finish(0, True)
                with n.loop(act, "l1", E // 2 - 1, S["loop_entered"]):
                    for k in (1, 0):
                        expert_attention()
                        finish(k, True)
                expert_attention()
                finish(1, False)

                turned(xT_)
                feat([(ACT.Copy, QT[:, 0, :], {}), (ACT.Copy, KT[:, 0, :], {})])
                n.take("tok_ready", NT)
                feat([(ACT.Identity, hid[:, 3, :], {"bias": C("b1_2")})])
                feat([(ACT.Copy, hid[:, 2, :], {})])
                attention(LAYER2)

                turned(xT_)
                feat([(ACT.Copy, hid[:, 0, :], {})])
                act.wait_ge(S["logits_ready"], n.take("logits_ready"))
                act.activation(hid[:, 1, 0:T], hid[:, 0, 0:T], ACT.Exp, bias=pooled[:, 1:2],
                               accum_out=half_sum[:, 0:1]).then_inc(S["exps_ready"], 1)
                n.take("tok_ready")
                gate_exponentials(1)
                with n.loop(act, "l2", E // 2, S["loop_entered"]):
                    for k in range(2):
                        stream(k * 2 * (FT + 1), (attT[:, :], QT[:, 0, :])[k], ACT.Gelu,
                               columns(k, W2_BIAS, FT + 1), 0, ACT.Gelu)
                load_exp()
                n.take("tok_ready", 2)

                turned(xT_)
                def third(k):
                    feat([(ACT.Copy, QT[:, k, :], {}), (ACT.Copy, KT[:, k, :], {})])

                def third_out():
                    turned(attT)
                    n.take("tok_ready", NT)

                def third_attention(k, between=None, ahead=None):
                    values((V, x1)[k])
                    attention(LAYER3, between, ahead)

                third(0)
                third_attention(0, None, lambda: third(1))
                with n.loop(act, "l3", E // 2 - 1, S["loop_entered"]):
                    for k in (1, 0):
                        third_attention(k, third_out, lambda: third(1 - k))
                third_attention(1, third_out)
                third_out()

                turned(xT_)
                n.take("tok_ready", NT)
                gate_exponentials(NT)
                def fourth(k):
                    stream(k * 2 * (F3 // P + 1), (attT[:, :], QT[:, 0, :])[k], ACT.Relu,
                           columns(k, W4_BIAS, F3 // P + 1), 2 * k, ACT.Identity)
                    act.drain().then_inc(S["wts_free"], 1)
                    n.take("tok_ready", 2)

                fourth(0)
                with n.loop(act, "l4", E // 2 - 1, S["loop_entered"]):
                    for k in (1, 0):
                        fourth(k)
                fourth(1)

        @block.vector
        def _(v):
            n = Tally("vector", per_turn)

            def over(ap, tiles, width):
                return ap.unsqueeze(1).to_broadcast([P, tiles, width])

            def ready():
                v.drain().then_inc(S["operand_ready"], 1)

            def norm_parts(src, dst, measured=False):
                for t in range(0 if measured else NT):
                    v.bn_stats(stats[:, t, :], src[:, t, :])
                    if t == 2:
                        yield
                v.drain()
                yield
                for t in range(NT):
                    v.bn_aggr(mv[:, t, :], stats[:, t, :])
                v.drain()
                v.tensor_scalar(var[:, :], mv[:, :, 1], EPS, None, ALU.add).then_inc(S["var_ready"], 1)
                yield
                v.wait_ge(S["rstd_ready"], n.take("rstd_ready"))
                for t in range(NT):
                    v.tensor_scalar(dst[:, t, :], src[:, t, :], mv[:, t, 0:1], rstd[:, t:t + 1],
                                    ALU.subtract, ALU.mult)
                    if t == 2:
                        yield
                v.drain()
                yield

            def norm(src, dst, measured=False):
                for _ in norm_parts(src, dst, measured):
                    pass

            def turned(dst, k=None):
                v.wait_ge(S["turned0"], n.take("turned0"))
                if k is not None:
                    w = wts[:, k, W1_NORM:W1_NORM + 2]
                    v.tensor_scalar(dst[:, 0:H0], ps[:, 4, 0:H0], w[:, 0:1], w[:, 1:2], ALU.mult, ALU.add)\
                        .then_inc(S["copied0"], 1)
                    return
                v.tensor_copy(dst[:, 0:H0], ps[:, 4, 0:H0]).then_inc(S["copied0"], 1)

            def tok(tiles, use, done=True):
                for t in range(tiles):
                    v.wait_ge(S["tok_ready"], n.take("tok_ready"))
                    use(t, ps[:, 4 + t % 4, :]).then_inc(S["tok_done_v"], 1)

            def tok_measured(use, dst):
                for t in range(NT):
                    v.wait_ge(S["tok_ready"], n.take("tok_ready"))
                    use(t, ps[:, 4 + t % 4, :]).then_inc(S["tok_done_v"], 1)
                    if t % 2:
                        v.drain()
                        for tile in (t - 1, t):
                            v.bn_stats(stats[:, tile, :], dst[:, tile, :])

            def keep_values(t, product):
                return v.tensor_copy(V[:, t, :], product[:, 0:D])

            def add_to_h(t, product):
                return v.tensor_tensor(h[:, t, :], product[:, 0:D], h[:, t, :], ALU.add)

            def add_back(dst, src, bank=4):
                for half in range(2):
                    v.wait_ge(S["tok_ready"], n.take("tok_ready"))
                    some = slice(3 * half, 3 * half + 3)
                    v.tensor_tensor(flat(dst[:, some, :]), ps[:, bank + half, 0:H0], flat(src[:, some, :]), ALU.add)\
                        .then_inc(S["tok_done_v"], 1)

            def attention(spec, dst, between=None):
                def peak(u):
                    v.wait_ge(S["scores_ready"], n.take("scores_ready"))
                    keys, i = spec.keys(u), u % 2
                    if spec.mask:
                        v.scalar_tensor_tensor(cut(masked[:, i, 0:keys], keys), scores_ap(u, keys), spec.scale,
                                               mask_ap(spec, u), ALU.mult, ALU.add)
                        v.drain()
                        v.tensor_reduce(top[:, i:i + 1], masked[:, i, 0:keys], X, ALU.max)
                    else:
                        v.tensor_reduce(top[:, i:i + 1], scores_ap(u, keys), XY if keys > 512 else X, ALU.max)
                    v.drain()
                    if spec.additive:
                        v.tensor_scalar(top[:, i:i + 1], top[:, i:i + 1], R("b2_2"), None, ALU.add)
                        v.drain()
                        v.tensor_tensor(neg_top[:, i:i + 1], R("b2_2"), top[:, i:i + 1], ALU.subtract)\
                            .then_inc(S["max_ready"], 1)
                    else:
                        v.tensor_scalar(neg_top[:, i:i + 1], top[:, i:i + 1], -1.0 if spec.mask else -spec.scale,
                                        None, ALU.mult).then_inc(S["max_ready"], 1)

                def copy_half(u):
                    tiles = min(3, len(key_tiles(spec.keys(u))))
                    v.wait_ge(S["turned0"], n.take("turned0"))
                    v.tensor_copy(flat(probsT[:, 0:tiles, :]), ps[:, 4, 0:tiles * P]).then_inc(S["copied0"], 1)

                def divide(u):
                    v.reciprocal(rtotal[:, u % 2:u % 2 + 1], total[:, u % 4:u % 4 + 1])
                    v.drain()
                    v.wait_ge(S["heads_ready"], n.take("heads_ready"))
                    out, product, over_total = dst(u), ps[:, 6 + u % 2, 0:D], rtotal[:, u % 2:u % 2 + 1]
                    if spec.additive:
                        v.scalar_tensor_tensor(out, product, over_total, out, ALU.mult, ALU.add)
                    else:
                        v.tensor_scalar(out, product, over_total, None, ALU.mult)

                peak(0)
                peak(1)
                if between:
                    between()
                for u in range(spec.units):
                    copy_half(u)
                    if u + 2 < spec.units:
                        peak(u + 2)
                    divide(u)
                v.drain()

            def gating(tiles, over_all):
                def wide(ap):
                    return ap.unsqueeze(2).to_broadcast([P, tiles, 8])

                L, L2, EX, PK, CD, M = lg[:, 0:tiles, :], lg2[:, 0:tiles, :], ex[:, 0:tiles, :], pick[:, 0:tiles, :], \
                    cand[:, 0:tiles, :], m1[:, 0:tiles]
                rank = over(C("rank8"), tiles, 8)

                def step(ins):
                    v.drain()
                    return ins

                def first_of_largest(src, picked):
                    step(v.tensor_reduce(M, src, X, ALU.max))
                    step(v.tensor_tensor(CD, src, wide(M), ALU.is_equal))
                    step(v.tensor_tensor(CD, CD, rank, ALU.mult))
                    step(v.tensor_reduce(M, CD, X, ALU.max))
                    step(v.tensor_tensor(picked, CD, wide(M), ALU.is_equal))

                def over_sum(dst, src, values, tiny):
                    step(v.tensor_reduce(M, values, X, ALU.add))
                    step(v.tensor_scalar(M, M, tiny, None, ALU.add))
                    step(v.reciprocal(M, M))
                    step(v.tensor_tensor(dst, src, wide(M), ALU.mult))

                step(v.tensor_reduce(M, L, X, ALU.max))
                step(v.tensor_tensor(L2, L, wide(M), ALU.subtract).then_inc(S["logits_ready"], 1))
                first_of_largest(L, PK)
                v.wait_ge(S["exps_ready"], n.take("exps_ready"))
                step(v.scalar_tensor_tensor(L2, PK, FAR, L, ALU.mult, ALU.add))
                if over_all:
                    over_sum(EX, EX, EX, 0.0)
                step(v.tensor_reduce(M, L2, X, ALU.max))
                step(v.tensor_tensor(CD, L2, wide(M), ALU.is_equal))
                step(v.tensor_tensor(CD, CD, rank, ALU.mult))
                step(v.tensor_reduce(M, CD, X, ALU.max))
                step(v.tensor_tensor(CD, CD, wide(M), ALU.is_equal))
                step(v.tensor_tensor(PK, PK, CD, ALU.add))
                step(v.tensor_tensor(EX, EX, PK, ALU.mult))
                over_sum(gates[:, :, 0:tiles].rearrange("p e t -> p t e"), EX, EX, 1e-9 if over_all else 0.0)

            def gate_column(e, tiles):
                v.tensor_copy(gcol[:, 0:tiles], gates[:, e, 0:tiles])
                v.drain()

            for buf in (xT, xnT, attT, add_w):
                v.memset(buf[:, :], 0.0)
            v.memset(peaks[:, :, :], 0.0)
            v.memset(V32[:, :, :, HD:PLACE], 0.0)
            v.drain()
            v.memset(V32[:, :, :, HD:HD + 1], 1.0)
            v.memset(k_stack[STACK:STACK + SHIFT, :, :], -1.0)
            for buf in (QT, KT, probs, masked):
                v.memset(buf[:, :, :], 0.0)
            v.drain()
            v.wait_ge(S["consts_loaded"], 48)
            v.tensor_copy(identb[:, :], ident)
            v.tensor_copy(maskb[:, 0:2 * P], C("band"))
            v.tensor_copy(maskb[:, 2 * P:3 * P], C("causal")[:, (NT - 1) * P:NT * P])
            v.tensor_scalar(add_w[:, 32:40], C("onehot8"), C("w2_2"), None, ALU.mult)
            v.tensor_scalar(pool_w[:, :], ones, C("pool_w"), None, ALU.mult)
            for out, base, at in ((lng, R("ln_g"), 0), (lnb, R("ln_b"), E * P)):
                tasks = flat(hid)[:, at:at + E * P]
                for e in range(E):
                    dst = out[:, :] if e == 0 else spread[:, :]
                    v.tensor_tensor(dst, tasks[:, e * P:(e + 1) * P], base, ALU.subtract)
                    v.drain()
                    if e:
                        v.tensor_tensor(out[:, :], out[:, :], spread[:, :], ALU.add)
                        v.drain()
                v.scalar_tensor_tensor(out[:, :], out[:, :], MERGE, base, ALU.mult, ALU.add)
            v.drain()
            v.memset(hid[:, :, :], 0.0)
            v.wait_ge(S["decay_ready"], 1)
            v.tensor_tensor(C("rel"), C("rel"), C("causal"), ALU.add)
            v.drain().then_inc(S["setup_done"], 1)
            v.sem_inc(S["x_free"], 1)
            v.sem_inc(S["wts_free"], 2)

            with n.loop(v, "batch", B, S["loop_entered"]):
                v.wait_ge(S["h_free"], n.take("h_free"))
                tok_measured(lambda t, product: v.tensor_scalar(h[:, t, :], product[:, 0:D], 0.0, None, ALU.max), h)
                v.drain().then_inc(S["x_free"], 1)

                norm(h, x1, True)
                norm(x1, xn)
                ready()
                turned(xT_)
                v.tensor_tensor(flat(h), flat(h), flat(x1), ALU.add)
                v.wait_ge(S["feat_done"], n.take("feat_done", 8))
                v.tensor_tensor(hid[:, 2, 0:T], hid[:, 0, 0:T], hid[:, 1, 0:T], ALU.mult)
                n.take("tok_ready", NT)
                v.wait_ge(S["tok_done_a"], n.take("tok_done_a", NT))
                v.tensor_tensor(V[:, 0:NT, :], V[:, 0:NT, :], y[:, :, :], ALU.mult)
                ready()
                attention(LAYER0, lambda u: att[:, u, :])
                ready()
                turned(attT)
                tok_measured(add_to_h, h)

                norm(h, xn, True)
                ready()
                turned(xT_)
                v.wait_ge(S["feat_done"], n.take("feat_done", 2))
                v.tensor_tensor(pooled[:, 0:1], half_sum[:, 0:1], half_sum[:, 1:2], ALU.add)
                v.drain()
                v.tensor_scalar(spread[:, :], ones, pooled[:, 0:1], 1.0 / T, ALU.mult, ALU.mult)
                ready()
                v.wait_ge(S["tok_ready"], n.take("tok_ready"))
                v.tensor_tensor(g8[:, :], ps[:, 4, 0:8], R("gfc2_b"), ALU.add)
                v.drain()
                v.wait_ge(S["tasks_loaded"], 16)
                for layer, bias, out_bias, tasks_bias in ((0, C("b1"), merged_b1, C("tv_b1")),
                                                          (1, R("b2"), merged_b2, R("tv_b2"))):
                    cols = slice(layer * F, (layer + 1) * F)
                    width = bias.shape[1]
                    for e in range(E):
                        for dst, base, task in (
                                (merged[:, cols], C("w1w2")[:, cols], tv[:, e, cols]),
                                (out_bias[:, :], bias, tasks_bias[:, e * width:(e + 1) * width])):
                            v.scalar_tensor_tensor(dst, task, g8[:, e:e + 1], base if e == 0 else dst,
                                                   ALU.mult, ALU.add)
                        v.drain()
                    v.drain().then_inc(S["operand_ready"], 1)
                n.take("feat_done", 8)
                v.tensor_tensor(y[:, :, :], xn[:, :, :], over(merged_b2[:, :], NT, D), ALU.add)
                v.tensor_tensor(h[:, :, :], h[:, :, :], over(lnb[:, :], NT, D), ALU.add)
                v.drain()
                tok_measured(lambda t, product: v.tensor_tensor(y[:, t, :], product[:, 0:D], y[:, t, :], ALU.add), y)
                norm(y, y, True)
                v.tensor_tensor(y[:, :, :], y[:, :, :], over(lng[:, :], NT, D), ALU.mult)
                v.drain()
                v.tensor_tensor(flat(h), flat(h), flat(y), ALU.add)
                v.drain()

                norm(h, xn)
                ready()
                turned(xT_)
                v.tensor_tensor(h[:, :, :], h[:, :, :], over(R("bo1"), NT, D), ALU.add)
                v.memset(keyT[:, 0:PAD], 0.0)
                v.memset(keyT[:, PAD + T:TPAD], 0.0)
                for i, dst in ((0, QT[:, 0, 0:T]), (2, keyT[:, PAD:PAD + T])):
                    v.wait_ge(S["feat_done"], n.take("feat_done", 4))
                    v.tensor_tensor(masked[:, 0, 0:T], hid[:, i, 0:T], C("rope_cos"), ALU.mult)
                    v.tensor_tensor(masked[:, 1, 0:T], hid[:, i + 1, 0:T], C("rope_sin"), ALU.mult)
                    v.drain()
                    v.tensor_tensor(dst, masked[:, 0, 0:T], masked[:, 1, 0:T], ALU.add)
                    v.drain()
                tok(NT + 1, keep_values)
                ready()
                attention(LAYER1, lambda u: att[:, u, :])
                ready()
                turned(attT)
                tok_measured(add_to_h, h)

                norm(h, xn, True)
                ready()
                turned(xT_)
                n.take("feat_done", 2)
                tok(NT, lambda t, product: v.tensor_scalar(lg[:, t, :], product[:, 0:8], float(D) ** -0.5, None,
                                                           ALU.mult))
                v.drain()
                gating(NT, True)
                def project():
                    v.wait_ge(S["feat_done"], n.take("feat_done", 4))
                    both = ((0, QT[:, 0, 0:T]), (1, KT[:, 0, 0:T]))
                    for i, src in both:
                        v.tensor_tensor(src, src, parts[:, i, 0, 0:T], ALU.subtract)
                    v.drain()
                    for i, src in both:
                        v.tensor_copy(parts[:, i, 1, 0:T], src)
                    v.drain().then_inc(S["parts_ready"], 1)
                    for i, src in both:
                        v.tensor_tensor(parts[:, i, 2, 0:T], src, parts[:, i, 1, 0:T], ALU.subtract)
                    v.drain().then_inc(S["parts_ready"], 1)
                    n.take("tok_ready", NT)
                    n.take("tok_done_a", NT)

                def expert_attention(k, rest=(), before=False):
                    turns, rest = 0, iter(rest)
                    first_rest = next(n_ for what, n_ in expert_steps() if what == "rest")
                    for what, n_ in expert_steps():
                        head, j, first = n_ // NT, n_ % NT, 2 + 2 * (turns % 2)
                        if what in ("peak", "divide"):
                            v.wait_ge(S["peak_ready"], n.take("peak_ready"))
                            turns += 1
                        if what == "peak":
                            m = keys_in(j)
                            v.tensor_reduce(peaks[0:m, head % 2, j:j + 1], ps[0:m, first:first + 2, 0:T // 2], XY,
                                            ALU.max).then_inc(S["peak_done"], 1)
                            if j == NT - 1:
                                v.drain()
                                v.tensor_copy(peaks2[:, head % 2, :, 0], peaks[:, head % 2, :])
                                v.drain()
                                v.tensor_tensor(peaks2[:, head % 2, :, 1], peaks[:, head % 2, :],
                                                peaks2[:, head % 2, :, 0], ALU.subtract).then_inc(S["shift_split"], 1)
                        elif what == "divide":
                            sums = ps[:, first:first + 2, 0:3 * P].rearrange("p a (c w) -> p a c w", w=PLACE)
                            v.tensor_scalar(rsum[:, :, :], sums[:, :, :, HD], 1e-30, None, ALU.max)
                            v.drain()
                            v.reciprocal(rsum[:, :, :], rsum[:, :, :])
                            v.drain()
                            for a in range(2):
                                last = v.tensor_tensor(
                                    att[:, 3 * a:3 * a + 3, n_ * D // 2:(n_ + 1) * D // 2]
                                    .rearrange("p t (g d) -> p t g d", d=HD),
                                    sums[:, a, :, 0:HD].rearrange("p (t g) d -> p t g d", g=GROUP),
                                    rsum[:, a, :].rearrange("p (t g) -> p t g", g=GROUP).unsqueeze(3)
                                    .to_broadcast([P, 3, GROUP, HD]), ALU.mult)
                            last.then_inc(S["peak_done"], 1)
                        elif what == "before" and n_ == 2 and before:
                            add_back(y, x1, 6)
                            v.drain()
                        elif what == "rest" and n_ == first_rest:
                            v.tensor_tensor(x1[:, :, :], xn[:, :, :], over(wrow_of(k, R_BO), NT, D), ALU.add)
                        elif what == "rest":
                            next(rest, None)
                    for _ in rest:
                        pass
                    v.drain()

                def finish(k, more):
                    def rows_over(r):
                        return over(wrow_of(k, r), NT, D)
                    ready()
                    turned(attT)
                    tok_measured(lambda t, product: v.tensor_tensor(y[:, t, :], product[:, 0:D], x1[:, t, :], ALU.add),
                                 y)
                    norm(y, x1, True)
                    ready()
                    turned(attT, k)
                    if more:
                        project()
                    v.wait_ge(S["feat_done"], n.now("feat_done") + 1)
                    v.tensor_tensor(x1[:, :, :], x1[:, :, :], rows_over(R_G1), ALU.mult)
                    v.drain()
                    v.tensor_tensor(x1[:, :, :], x1[:, :, :], rows_over(R_BE1), ALU.add)
                    v.drain()
                    n.take("feat_done", 2 * (FT + 1))

                def second_norm(e, k):
                    yield from norm_parts(y, y)
                    for some in (slice(0, 3), slice(3, NT)):
                        v.tensor_tensor(y[:, some, :], y[:, some, :], over(wrow_of(k, R_G2), 3, D), ALU.mult)
                        yield
                    gate_column(e, NT)
                    for some in (slice(0, 3), slice(3, NT)):
                        v.tensor_tensor(y[:, some, :], y[:, some, :], over(wrow_of(k, R_BE2), 3, D), ALU.add)
                        v.drain()
                        yield
                    for t in range(NT):
                        last = v.scalar_tensor_tensor(h[:, t, :], y[:, t, :], gcol[:, t:t + 1], h[:, t, :],
                                                      ALU.mult, ALU.add)
                        if t % 2 and t < NT - 1:
                            yield
                    v.drain().then_inc(S["wts_free"], 1)

                project()
                expert_attention(0)
                finish(0, True)
                with n.loop(v, "l1", E // 2 - 1, S["loop_entered"]) as pair:
                    for k in (1, 0):
                        expert_attention(k, second_norm(pair * 2 + (1 - k), 1 - k), True)
                        finish(k, True)
                expert_attention(1, second_norm(E - 2, 0), True)
                finish(1, False)
                add_back(y, x1, 6)
                v.drain()
                for _ in second_norm(E - 1, 1):
                    pass

                norm(h, xn)
                ready()
                turned(xT_)
                n.take("feat_done", 4)
                tok(NT, keep_values)
                v.wait_ge(S["feat_done"], n.take("feat_done", 4))
                v.tensor_scalar(QT[:, 1, 0:T], QT[:, 0, 0:T], float(D) ** -0.5, None, ALU.mult)
                pairs = flat(y).rearrange("p (g j) -> p g j", j=8)
                v.tensor_tensor(pairs, hid[:, 3, :].rearrange("p (g j) -> p g j", j=8),
                                over(C("onehot8"), TP // 8, 8), ALU.mult)
                v.drain()
                v.tensor_reduce(hqb[:, :], pairs, X, ALU.add).then_inc(S["query_part_ready"], 1)
                ready()
                attention(LAYER2, lambda u: h[:, u, :])

                norm(h, xn)
                ready()
                turned(xT_)
                v.wait_ge(S["feat_done"], n.take("feat_done", 2))
                v.tensor_reduce(pooled[:, 0:1], hid[:, 0, 0:T], X, ALU.max)
                v.drain()
                v.tensor_scalar(pooled[:, 0:1], pooled[:, 0:1], R("pool_b"), None, ALU.add)
                v.drain()
                v.tensor_tensor(pooled[:, 1:2], R("pool_b"), pooled[:, 0:1], ALU.subtract)\
                    .then_inc(S["logits_ready"], 1)
                v.wait_ge(S["exps_ready"], n.take("exps_ready"))
                v.tensor_tensor(hid[:, 2, 0:T], hid[:, 1, 0:T], xT_[:, 0:T], ALU.mult)
                v.reciprocal(rtotal[:, 0:1], half_sum[:, 0:1])
                v.drain()
                v.tensor_reduce(pooled[:, 2:3], hid[:, 2, 0:T], X, ALU.add)
                v.drain()
                v.tensor_scalar(pooled[:, 3:4], pooled[:, 2:3], rtotal[:, 0:1], None, ALU.mult)
                v.drain()
                v.tensor_scalar(spread[:, :], ones, pooled[:, 3:4], None, ALU.mult)
                ready()
                tok(1, lambda t, product: v.tensor_tensor(lg[:, 0, :], product[:, 0:8], R("gate_b2"), ALU.add))
                v.drain()
                v.memset(KT[:, 0, 0:T], 0.0)
                gating(1, True)
                with n.loop(v, "l2", E // 2, S["loop_entered"]) as pair:
                    for k in range(2):
                        gate_column(pair * 2 + k, 1)
                        v.wait_ge(S["feat_done"], n.take("feat_done", 2 * (FT + 1)))
                        v.scalar_tensor_tensor(KT[:, 0, 0:T], (attT[:, 0:T], QT[:, 0, 0:T])[k], gcol[:, 0:1],
                                               KT[:, 0, 0:T], ALU.mult, ALU.add)
                        v.drain().then_inc(S["wts_free"], 1)
                ready()
                add_back(h, h)
                v.drain()

                norm(h, xn)
                ready()
                turned(xT_)
                def third():
                    n.take("feat_done", 4)
                    n.take("tok_ready", NT)
                    n.take("tok_done_a", NT)

                def third_out():
                    turned(attT)
                    tok(NT, add_to_h)
                    v.drain().then_inc(S["wts_free"], 1)

                def third_attention(between=None):
                    attention(LAYER3, lambda u: att[:, u, :], between)
                    ready()

                third()
                third_attention()
                with n.loop(v, "l3", E // 2 - 1, S["loop_entered"]):
                    for _ in (1, 0):
                        third()
                        third_attention(third_out)
                third()
                third_attention(third_out)
                third_out()

                norm(h, xn)
                ready()
                turned(xT_)
                tok(NT, lambda t, product: v.tensor_copy(lg[:, t, :], product[:, 0:8]))
                v.drain()
                gating(NT, False)
                n.take("feat_done", 2 * (F3 // P + 1) * E)

                def fourth_back(e):
                    gate_column(e, NT)
                    for half in range(2):
                        v.wait_ge(S["tok_ready"], n.take("tok_ready"))
                        for i in range(3):
                            t = 3 * half + i
                            last = v.scalar_tensor_tensor(h[:, t, :], ps[:, 4 + half, i * P:(i + 1) * P],
                                                          gcol[:, t:t + 1], h[:, t, :], ALU.mult, ALU.add)
                        last.then_inc(S["tok_done_v"], 1)
                    v.drain()

                with n.loop(v, "l4", E // 2 - 1, S["loop_entered"]) as pair:
                    for k in range(2):
                        fourth_back(pair * 2 + k)
                fourth_back(E - 2)
                fourth_back(E - 1)
                v.drain().then_inc(S["h_final"], 1)


def _layout(a):
    import numpy as np

    f32 = np.float32

    def down(w, tiles):
        return w.T.reshape(tiles, P, -1).transpose(1, 0, 2).reshape(P, -1)

    def columns(b, tiles):
        return b.reshape(tiles, P).T

    x_off = np.arange(TP)[None, :] - (NT - 1) * P - np.arange(P)[:, None]
    win = np.arange(2 * P)[None, :] - np.arange(P)[:, None]
    inv = (f32(1.0) / f32(10000.0) ** (np.arange(0, D, 2, dtype=f32) / f32(D))).astype(f32)
    freqs = np.arange(T, dtype=f32)[:, None] * inv[None, :]
    emb = np.concatenate([np.sin(freqs), np.cos(freqs)], -1).astype(f32)
    sin, cos = emb[:, ::2].T, emb[:, 1::2].T
    even_odd = np.r_[0:D:2, 1:D:2]
    odd_even = np.r_[1:D:2, 0:D:2]
    valid = np.zeros((P, TPAD), f32)
    valid[:, PAD:PAD + T] = 1.0
    exp = a["L0_attn_expand"]
    lin0, pre0 = 2 * QK0, 2 * QK0 + 2 * D
    const = {
        "ident": np.eye(P, dtype=f32), "ones": np.ones((P, P), f32),
        "onehot8": (np.arange(P)[:, None] // 16 == np.arange(8)[None, :]).astype(f32),
        "rank8": np.broadcast_to(np.arange(8, 0, -1).astype(f32), (P, 8)),
        "tok_w": a["L0_tok_weight"].T.reshape(CONTEXT, P, P).transpose(1, 0, 2).reshape(P, -1),
        "expand_q": exp[:, 0:QK0], "expand_k": exp[:, QK0:2 * QK0],
        "expand_lin": exp[:, lin0:lin0 + D], "expand_pre": exp[:, pre0:pre0 + D],
        "expand_v": np.concatenate([exp[:, lin0 + D:pre0], exp[:, pre0 + D:]], 1),
        "project": a["L0_attn_project"].reshape(2, P, D).transpose(1, 0, 2).reshape(P, -1),
        "rel": x_off.astype(f32), "causal": np.where(x_off <= 0, 0.0, FAR).astype(f32), "valid": valid,
        "gfc1": a["L0_ffn_gfc1_w"].T, "gfc1_b": a["L0_ffn_gfc1_b"][:, None], "gfc2": a["L0_ffn_gfc2_w"].T,
        "w1w2": np.concatenate([a["L0_ffn_W1"].T, down(a["L0_ffn_W2"], FT)], 1),
        "b1": columns(a["L0_ffn_b1"], FT),
        "tv_b1": np.concatenate([columns(b, FT) for b in a["L0_ffn_tv_b1"]], 1),
        "rope_qa": a["L1_attn_Wq"][even_odd].T, "rope_qb": a["L1_attn_Wq"][odd_even].T,
        "rope_ka": a["L1_attn_Wk"][even_odd].T, "rope_kb": a["L1_attn_Wk"][odd_even].T,
        "rope_bias": np.stack([a["L1_attn_bq"][even_odd], a["L1_attn_bq"][odd_even],
                               a["L1_attn_bk"][even_odd], a["L1_attn_bk"][odd_even]], 1),
        "rope_cos": np.concatenate([cos, cos]), "rope_sin": np.concatenate([-sin, sin]),
        "v1": a["L1_attn_Wv"].T, "o1": a["L1_attn_Wo"].T,
        "band": np.where((win >= 0) & (win < WINDOW), 0.0, FAR).astype(f32),
        "gate_k": a["L1_ffn_gate_Wk"].T, "gate_kb": a["L1_ffn_gate_bk"][:, None],
        "queries": a["L1_ffn_expert_queries"].T,
        "q2": a["L2_attn_Wq"].T, "k2": a["L2_attn_Wk"].T, "v2": a["L2_attn_Wv"].T,
        "hq2": np.tile(a["L2_attn_W1"][:, :D].T, (1, 8)), "hk2": np.tile(a["L2_attn_W1"][:, D:].T, (1, 8)),
        "b1_2": np.tile(a["L2_attn_b1"], 8)[:, None], "w2_2": np.tile(a["L2_attn_W2"][0], 8)[:, None],
        "pool_w": a["L2_ffn_attn_w"], "gate_w2": a["L2_ffn_gate_w"], "gate_w3": a["L3_ffn_gate_w"],
    }
    rows = {
        "tok_b": a["L0_tok_bias"], "mult": a["L0_attn_position_bias_mult"].reshape(1), "gfc2_b": a["L0_ffn_gfc2_b"],
        "b2": a["L0_ffn_b2"], "tv_b2": a["L0_ffn_tv_b2"].reshape(-1), "ln_g": a["L0_ffn_ln_g"],
        "ln_b": a["L0_ffn_ln_b"], "bv1": a["L1_attn_bv"], "bo1": a["L1_attn_bo"],
        "b2_2": a["L2_attn_b2"], "pool_b": a["L2_ffn_attn_b"], "gate_b2": a["L2_ffn_gate_b"],
        "gate_b3": a["L3_ffn_gate_b"],
    }
    def places_first(w):
        return w.reshape((E, HD) + w.shape[1:]).swapaxes(0, 1).reshape(w.shape)

    l1, l1r = [], []
    for e in range(E):
        wq, wk, wv = a["L1_ffn_Wqkv"][e].reshape(3, D, D)
        bq, bk, bv = a["L1_ffn_bqkv"][e].reshape(3, D)
        l1.append(np.concatenate([places_first(wq).T, places_first(wk).T, wv.T,
                                  a["L1_ffn_Wo"][e].T, a["L1_ffn_W1"][e].T, down(a["L1_ffn_W2"][e], FT),
                                  places_first(bq)[:, None], places_first(bk)[:, None], columns(a["L1_ffn_bf1"][e], FT), a["L1_ffn_bf2"][e][:, None],
                                  a["L1_ffn_g1"][e][:, None], a["L1_ffn_be1"][e][:, None]], 1))
        l1r.append(np.concatenate([bv, a["L1_ffn_bo"][e], a["L1_ffn_g1"][e], a["L1_ffn_be1"][e],
                                   a["L1_ffn_g2"][e], a["L1_ffn_be2"][e]]))
    out = {
        "const": np.concatenate([const[name].reshape(P, width) for name, width in CONST], 1),
        "rows": np.concatenate([rows[name].reshape(width) for name, width in ROWS])[None],
        "tv": np.stack([np.concatenate([a["L0_ffn_tv_W1"][e].T, down(a["L0_ffn_tv_W2"][e], FT)], 1)
                        for e in range(E)], 1),
        "merge_rows": np.concatenate([a["L0_ffn_tv_ln_g"].reshape(-1), a["L0_ffn_tv_ln_b"].reshape(-1)])[None],
        "xT": a["x"].transpose(0, 2, 1),
        "l1": np.stack(l1), "l1_rows": np.stack(l1r),
        "l2": np.stack([np.concatenate([a["L2_ffn_w1"][e], down(a["L2_ffn_w2"][e].T, FT),
                                        columns(a["L2_ffn_b1"][e], FT), a["L2_ffn_b2"][e][:, None]], 1) for e in range(E)]),
        "l3": np.stack([np.concatenate([a[f"L3_attn_W{c}"][e * D:(e + 1) * D].T for c in "qkv"] +
                                       [a["L3_attn_Wo"][:, e * D:(e + 1) * D].T], 1) for e in range(E)]),
        "l4": np.stack([np.concatenate([a["L3_ffn_w1"][e], down(a["L3_ffn_w2"][e].T, F3 // P),
                                        columns(a["L3_ffn_b1"][e], F3 // P), a["L3_ffn_b2"][e][:, None]], 1) for e in range(E)]),
    }
    return {name: np.ascontiguousarray(value, dtype=f32) for name, value in out.items()}


def kernel(**inputs):
    import numpy as np
    import concourse.bacc as bacc
    from concourse.bass_utils import run_bass_kernel_spmd as run

    arrays = _layout({name: np.asarray(value) for name, value in inputs.items()})
    per_turn = {}
    for _ in range(2):
        nc = bacc.Bacc("TRN2", target_bir_lowering=False, num_devices=1)
        tensors = {name: nc.dram_tensor("in_" + name, value.shape, F32, kind="ExternalInput").ap()
                   for name, value in arrays.items()}
        tensors["out"] = nc.dram_tensor("out", (B, T, D), F32, kind="ExternalOutput").ap()
        audio_tower(nc, tensors, per_turn)
    r = run(nc, [{"in_" + name: value for name, value in arrays.items()}], core_ids=[0])
    return r.results[0]["out"]
```
